# Optimizing a Trainium2 kernel written in Bass

```python
import numpy as np
import jax
import jax.numpy as jnp

def _softmax(x, axis=-1):
    return jax.nn.softmax(x, axis=axis)

def _gelu(x):
    return jax.nn.gelu(x, approximate=True)

def _silu(x):
    return jax.nn.silu(x)

def _sigmoid(x):
    return jax.nn.sigmoid(x)

def _layernorm(x, axis=-1, eps=1e-05):
    m = jnp.mean(x, axis=axis, keepdims=True)
    v = jnp.var(x, axis=axis, keepdims=True)
    return (x - m) / jnp.sqrt(v + eps)

def _scatter_add(tgt, idx, src, axis=0):
    return tgt.at[idx].add(src)

def _segment_sum(src, seg, n):
    return jax.ops.segment_sum(src, seg, n)
kernel_name = 'mk_macaron_d2_jaxref_r8_7e9cab'

def setup_inputs(seed: int=0):
    np.random.seed(seed)
    _w = jnp.asarray

    def _L0_attn_setup():
        import jax, jax.numpy as jnp
        import numpy as np
        HEADS = 16
        KV_HEADS = 8
        DIMS = 64
        IN_DIMS = 128
        B, S = (2, 256)

        def rope(x):
            seq_len, dim = (x.shape[-2], x.shape[-1])
            thetas = 1.0 / 1250 ** (jnp.arange(0, dim, 2) / dim)
            ang = jnp.arange(1, seq_len + 1)[:, None] * thetas[None, :]
            cos, sin = (jnp.cos(ang), jnp.sin(ang))
            xe, xo = (x[..., ::2], x[..., 1::2])
            real = xe * cos - xo * sin
            imag = xe * sin + xo * cos
            return jnp.stack([real, imag], axis=-1).reshape(x.shape)
        key = jax.random.key(seed)
        k1, k2, k3, k4, k5 = jax.random.split(key, 5)
        q = jax.random.normal(k1, (B, S, IN_DIMS), dtype=jnp.float32)
        sd = 1.0 / np.sqrt(IN_DIMS)
        Wq = jax.random.normal(k2, (IN_DIMS, HEADS * DIMS), dtype=jnp.float32) * sd
        Wk = jax.random.normal(k3, (IN_DIMS, KV_HEADS * DIMS), dtype=jnp.float32) * sd
        Wv = jax.random.normal(k4, (IN_DIMS, KV_HEADS * DIMS), dtype=jnp.float32) * sd
        Wo = jax.random.normal(k5, (HEADS * DIMS, IN_DIMS), dtype=jnp.float32) / np.sqrt(HEADS * DIMS)
        return {'q': q, 'Wq': Wq, 'Wk': Wk, 'Wv': Wv, 'Wo': Wo}
    _L0_attn_in = _L0_attn_setup()

    def _L0_ffn_setup():
        import jax, jax.numpy as jnp
        import numpy as np
        INPUT_SIZE = 128
        OUTPUT_SIZE = 128
        key = jax.random.key(seed)
        kx, kt, kp, ktn, kpn = jax.random.split(key, 5)
        x = jax.random.normal(kx, (8, 256, INPUT_SIZE), dtype=jnp.float32)
        theta = jax.random.normal(kt, (INPUT_SIZE, OUTPUT_SIZE), dtype=jnp.float32) * 0.02
        phi = jax.random.normal(kp, (INPUT_SIZE, OUTPUT_SIZE), dtype=jnp.float32) * 0.02
        theta_noise = jax.random.normal(ktn, (INPUT_SIZE, OUTPUT_SIZE), dtype=jnp.float32) * 0.01
        phi_noise = jax.random.normal(kpn, (INPUT_SIZE, OUTPUT_SIZE), dtype=jnp.float32) * 0.01
        return {'x': x, 'theta': theta, 'phi': phi, 'theta_noise': theta_noise, 'phi_noise': phi_noise}
    _L0_ffn_in = _L0_ffn_setup()

    def _L1_attn_setup():
        import jax, jax.numpy as jnp
        import numpy as np
        D_MODEL = 128
        D_STATE = 64
        EXPAND = 2
        N_HEADS = 32
        NGROUPS = 1
        CHUNK = 128
        R = 2
        D_INNER = EXPAND * D_MODEL
        HEAD_DIM = D_INNER // N_HEADS
        BC = NGROUPS * D_STATE
        D_PROJ = D_INNER + D_INNER * R + BC * R + BC + 2 * N_HEADS + D_STATE // 2
        SCALE = (D_STATE * R) ** (-0.5)
        EPS = 1e-06
        NEG = -1e+30

        def _rms(x):
            return x * jax.lax.rsqrt(jnp.mean(x * x, axis=-1, keepdims=True) + EPS)

        def _rope(x, cos, sin):
            h = x.shape[-1] // 2
            x1, x2 = (x[..., :h], x[..., h:])
            return jnp.concatenate([x1 * cos - x2 * sin, x1 * sin + x2 * cos], axis=-1)
        key = jax.random.key(seed)
        ks = jax.random.split(key, 7)
        B, T = (2, 256)
        return {'x': jax.random.normal(ks[0], (B, T, D_MODEL), jnp.float32), 'W_in': jax.random.normal(ks[1], (D_MODEL, D_PROJ), jnp.float32) * 0.02, 'A_log': jax.random.normal(ks[2], (N_HEADS,), jnp.float32) * 0.5, 'dt_bias': jax.random.normal(ks[3], (N_HEADS,), jnp.float32) * 0.5, 'B_norm_bias': 1.0 + 0.1 * jax.random.normal(ks[4], (NGROUPS, D_STATE), jnp.float32), 'C_norm_bias': 1.0 + 0.1 * jax.random.normal(ks[5], (NGROUPS, D_STATE), jnp.float32), 'W_out': jax.random.normal(ks[6], (D_INNER, D_MODEL), jnp.float32) * 0.02}
    _L1_attn_in = _L1_attn_setup()

    def _L1_ffn_setup():
        import jax, jax.numpy as jnp
        import numpy as np
        TOP_K = 2
        key = jax.random.key(seed)
        k1, k2, k3 = jax.random.split(key, 3)
        B, S, D, E = (8, 256, 128, 8)
        x = jax.random.normal(k1, (B, S, D), dtype=jnp.float32)
        gate_w = jax.random.normal(k2, (E, D), dtype=jnp.float32) * (1.0 / np.sqrt(D))
        gate_b = jnp.zeros((E,), dtype=jnp.float32)
        expert_w = jax.random.normal(k3, (E, D, D), dtype=jnp.float32) * (1.0 / np.sqrt(D))
        expert_b = jnp.zeros((E, D), dtype=jnp.float32)
        return {'x': x, 'gate_w': gate_w, 'gate_b': gate_b, 'expert_w': expert_w, 'expert_b': expert_b}
    _L1_ffn_in = _L1_ffn_setup()
    _d = {'L0_attn_q': _L0_attn_in['q'], 'L0_attn_Wq': _L0_attn_in['Wq'], 'L0_attn_Wk': _L0_attn_in['Wk'], 'L0_attn_Wv': _L0_attn_in['Wv'], 'L0_attn_Wo': _L0_attn_in['Wo'], 'L0_ffn_theta': _L0_ffn_in['theta'], 'L0_ffn_phi': _L0_ffn_in['phi'], 'L0_ffn_theta_noise': _L0_ffn_in['theta_noise'], 'L0_ffn_phi_noise': _L0_ffn_in['phi_noise'], 'L1_attn_W_in': _L1_attn_in['W_in'], 'L1_attn_A_log': _L1_attn_in['A_log'], 'L1_attn_dt_bias': _L1_attn_in['dt_bias'], 'L1_attn_B_norm_bias': _L1_attn_in['B_norm_bias'], 'L1_attn_C_norm_bias': _L1_attn_in['C_norm_bias'], 'L1_attn_W_out': _L1_attn_in['W_out'], 'L1_ffn_gate_w': _L1_ffn_in['gate_w'], 'L1_ffn_gate_b': _L1_ffn_in['gate_b'], 'L1_ffn_expert_w': _L1_ffn_in['expert_w'], 'L1_ffn_expert_b': _L1_ffn_in['expert_b']}
    _x0 = _d['L0_attn_q']
    _d['L0_attn_q'] = jax.random.normal(jax.random.fold_in(jax.random.key(seed), 1), (16, 512, 128), dtype=_x0.dtype)
    del _x0
    return _d

def reference(L0_attn_q, L0_attn_Wq, L0_attn_Wk, L0_attn_Wv, L0_attn_Wo, L0_ffn_theta, L0_ffn_phi, L0_ffn_theta_noise, L0_ffn_phi_noise, L1_attn_W_in, L1_attn_A_log, L1_attn_dt_bias, L1_attn_B_norm_bias, L1_attn_C_norm_bias, L1_attn_W_out, L1_ffn_gate_w, L1_ffn_gate_b, L1_ffn_expert_w, L1_ffn_expert_b):

    def _L0_attn_ref(q, Wq, Wk, Wv, Wo):
        import jax, jax.numpy as jnp
        import numpy as np
        HEADS = 16
        KV_HEADS = 8
        DIMS = 64
        IN_DIMS = 128
        B, S = (2, 256)

        def rope(x):
            seq_len, dim = (x.shape[-2], x.shape[-1])
            thetas = 1.0 / 1250 ** (jnp.arange(0, dim, 2) / dim)
            ang = jnp.arange(1, seq_len + 1)[:, None] * thetas[None, :]
            cos, sin = (jnp.cos(ang), jnp.sin(ang))
            xe, xo = (x[..., ::2], x[..., 1::2])
            real = xe * cos - xo * sin
            imag = xe * sin + xo * cos
            return jnp.stack([real, imag], axis=-1).reshape(x.shape)
        batch, seq_len, in_dims = q.shape
        kv = q
        xq = rope(q @ Wq)
        xk = rope(kv @ Wk)
        xv = kv @ Wv
        xk = jnp.repeat(xk, 2, axis=-1)
        xv = jnp.repeat(xv, 2, axis=-1)
        xq = xq.reshape(batch, seq_len, HEADS, DIMS).transpose(0, 2, 1, 3)
        xk = xk.reshape(batch, seq_len, HEADS, DIMS).transpose(0, 2, 3, 1)
        xv = xv.reshape(batch, seq_len, HEADS, DIMS).transpose(0, 2, 1, 3)
        scale = (DIMS / HEADS) ** (-0.5)
        scores = jax.nn.softmax(xq @ xk * scale, axis=-1)
        out = (scores @ xv).transpose(0, 2, 1, 3).reshape(batch, seq_len, -1)
        return out @ Wo

    def _L0_ffn_ref(x, theta, phi, theta_noise, phi_noise):
        import jax, jax.numpy as jnp
        import numpy as np
        INPUT_SIZE = 128
        OUTPUT_SIZE = 128
        real = jnp.einsum('bti,io->bto', x, jnp.cos(theta + theta_noise))
        imag = jnp.einsum('bti,io->bto', x, jnp.sin(phi + phi_noise))
        return jnp.sqrt(real * real + imag * imag)

    def _L1_attn_ref(x, W_in, A_log, dt_bias, B_norm_bias, C_norm_bias, W_out):
        import jax, jax.numpy as jnp
        import numpy as np
        D_MODEL = 128
        D_STATE = 64
        EXPAND = 2
        N_HEADS = 32
        NGROUPS = 1
        CHUNK = 128
        R = 2
        D_INNER = EXPAND * D_MODEL
        HEAD_DIM = D_INNER // N_HEADS
        BC = NGROUPS * D_STATE
        D_PROJ = D_INNER + D_INNER * R + BC * R + BC + 2 * N_HEADS + D_STATE // 2
        SCALE = (D_STATE * R) ** (-0.5)
        EPS = 1e-06
        NEG = -1e+30

        def _rms(x):
            return x * jax.lax.rsqrt(jnp.mean(x * x, axis=-1, keepdims=True) + EPS)

        def _rope(x, cos, sin):
            h = x.shape[-1] // 2
            x1, x2 = (x[..., :h], x[..., h:])
            return jnp.concatenate([x1 * cos - x2 * sin, x1 * sin + x2 * cos], axis=-1)
        B, T, _ = x.shape
        L = CHUNK
        NC = T // L
        G, H, N, P = (NGROUPS, N_HEADS, D_STATE, HEAD_DIM)
        E = H // G
        proj = x @ W_in
        o = 0
        z = proj[..., :D_INNER]
        o = D_INNER
        x_raw = proj[..., o:o + D_INNER * R]
        o += D_INNER * R
        Bm = proj[..., o:o + BC * R]
        o += BC * R
        Cm = proj[..., o:o + BC]
        o += BC
        dt_raw = proj[..., o:o + H]
        o += H
        lam_raw = proj[..., o:o + H]
        o += H
        theta = proj[..., o:]
        x_raw = jax.nn.silu(x_raw)
        Bm = _rms(Bm.reshape(B, T, G, R, N)) * B_norm_bias[:, None, :]
        Cm = _rms(Cm.reshape(B, T, G, N)) * C_norm_bias
        A = -jnp.exp(A_log)
        dt = jnp.clip(jax.nn.softplus(dt_raw + dt_bias), 0.0001, 0.5)
        ang = -jnp.cumsum(jnp.mean(dt, axis=-1, keepdims=True) * theta, axis=1)
        cos, sin = (jnp.cos(ang), jnp.sin(ang))
        Cr = _rope(Cm, cos[:, :, None, :], sin[:, :, None, :])
        Br = _rope(Bm, cos[:, :, None, None, :], sin[:, :, None, None, :])
        xh = x_raw.reshape(B, T, H, R, P)
        log_dA = dt * A
        alpha = jnp.exp(log_dA)
        lam = jax.nn.sigmoid(lam_raw)
        xg = (lam * dt)[..., None, None] * xh
        x_prev = jnp.pad(xh, ((0, 0), (1, 0), (0, 0), (0, 0), (0, 0)))[:, :T]
        xb = ((1.0 - lam) * dt * alpha)[..., None, None] * x_prev
        Bb = jnp.pad(Br, ((0, 0), (1, 0), (0, 0), (0, 0), (0, 0)))[:, :T]

        def ch(a):
            return a.reshape(B, NC, L, *a.shape[2:])
        cum = jnp.cumsum(ch(log_dA), axis=2)
        mask = jnp.tril(jnp.ones((L, L), bool))
        diff = cum[:, :, :, None, :] - cum[:, :, None, :, :]
        dmat = jnp.exp(jnp.where(mask[None, None, :, :, None], diff, NEG))
        Cc = ch(Cr)
        Bgc, Bbc = (ch(Br), ch(Bb))
        xgc = ch(xg).reshape(B, NC, L, G, E, R, P)
        xbc = ch(xb).reshape(B, NC, L, G, E, R, P)
        sg = jnp.einsum('bclgn,bcmgrn->bclmgr', Cc, Bgc) * SCALE
        sb = jnp.einsum('bclgn,bcmgrn->bclmgr', Cc, Bbc) * SCALE
        dg = dmat.reshape(B, NC, L, L, G, E)
        y_intra = jnp.einsum('bclmgr,bclmge,bcmgerp->bclgep', sg, dg, xgc) + jnp.einsum('bclmgr,bclmge,bcmgerp->bclgep', sb, dg, xbc)
        dec_end = jnp.exp(cum[:, :, -1:, :] - cum).reshape(B, NC, L, G, E)
        st = (jnp.einsum('bclge,bclgrn,bclgerp->bcgenp', dec_end, Bgc, xgc) + jnp.einsum('bclge,bclgrn,bclgerp->bcgenp', dec_end, Bbc, xbc)).reshape(B, NC, H, N, P)
        cdec = jnp.exp(cum[:, :, -1, :])

        def step(S, inp):
            cd, s = inp
            return (cd[..., None, None] * S + s, S)
        _, Sprev = jax.lax.scan(step, jnp.zeros((B, H, N, P), x.dtype), (jnp.moveaxis(cdec, 1, 0), jnp.moveaxis(st, 1, 0)))
        Sprev = jnp.moveaxis(Sprev, 0, 1).reshape(B, NC, G, E, N, P)
        dec_in = jnp.exp(cum).reshape(B, NC, L, G, E)
        y_inter = SCALE * jnp.einsum('bclgn,bclge,bcgenp->bclgep', Cc, dec_in, Sprev)
        y = (y_intra + y_inter).reshape(B, T, D_INNER)
        y = _rms(y * jax.nn.silu(z))
        return y @ W_out

    def _L1_ffn_ref(x, gate_w, gate_b, expert_w, expert_b):
        import jax, jax.numpy as jnp
        import numpy as np
        TOP_K = 2
        gate = jnp.einsum('bsd,ed->bse', x, gate_w) + gate_b
        _, idx = jax.lax.top_k(gate, TOP_K)
        E = gate_w.shape[0]
        flat_idx = idx.reshape(-1)
        counts = jnp.zeros((E,), dtype=x.dtype).at[flat_idx].add(1.0)
        expert_out = jax.nn.relu(jnp.einsum('bsd,ehd->bseh', x, expert_w) + expert_b)
        total = flat_idx.size
        out = jnp.einsum('bseh,e->bsh', expert_out, counts) / total
        return out
    x = L0_attn_q
    x = x + 0.5 * _L0_ffn_ref(_layernorm(x, axis=-1), L0_ffn_theta, L0_ffn_phi, L0_ffn_theta_noise, L0_ffn_phi_noise)
    x = x + _L0_attn_ref(_layernorm(x, axis=-1), L0_attn_Wq, L0_attn_Wk, L0_attn_Wv, L0_attn_Wo)
    x = x + 0.5 * _L0_ffn_ref(_layernorm(x, axis=-1), L0_ffn_theta, L0_ffn_phi, L0_ffn_theta_noise, L0_ffn_phi_noise)
    x = x + 0.5 * _L1_ffn_ref(_layernorm(x, axis=-1), L1_ffn_gate_w, L1_ffn_gate_b, L1_ffn_expert_w, L1_ffn_expert_b)
    x = x + _L1_attn_ref(_layernorm(x, axis=-1), L1_attn_W_in, L1_attn_A_log, L1_attn_dt_bias, L1_attn_B_norm_bias, L1_attn_C_norm_bias, L1_attn_W_out)
    x = x + 0.5 * _L1_ffn_ref(_layernorm(x, axis=-1), L1_ffn_gate_w, L1_ffn_gate_b, L1_ffn_expert_w, L1_ffn_expert_b)
    return x

_drawn_inputs = setup_inputs


def setup_inputs(seed=0):
    import zlib

    import numpy as np

    out = dict(_drawn_inputs(seed))
    spreads = {'L1_ffn_gate_b': (0.0, 0.659), 'L1_ffn_expert_b': (0.0, 0.428)}
    factors = {'L0_ffn_theta': 8.0, 'L0_ffn_theta_noise': 8.0, 'L1_ffn_gate_w': 4.741}
    for name, (base, spread) in spreads.items():
        noise = np.random.default_rng([zlib.crc32(name.encode()), seed]).standard_normal(out[name].shape)
        drawn = base * np.exp(spread * noise) if base else spread * noise
        out[name] = jnp.asarray(drawn.astype(out[name].dtype))
    for name, factor in factors.items():
        out[name] = (out[name] * factor).astype(out[name].dtype)
    return out
```

```python
from contextlib import ExitStack

import numpy as np
import concourse.bass as bass
from concourse import mybir

F32 = mybir.dt.float32
F16 = mybir.dt.float16
U32 = mybir.dt.uint32
ALU = mybir.AluOpType
ACT = mybir.ActivationFunctionType
AX = mybir.AxisListType.X

P = 128
BATCH, SEQ, D = 16, 512, 128
NT = SEQ // P
HEADS, KVD, DH = 16, 512, 32
NG = 4
EXPERTS, TOPK = 8, 2
LN_EPS = 1e-5
STK = 3 * DH + 1
ATT_SCALE = float((64 / 16) ** -0.5)


def rope_tables():
    pos = np.arange(1, SEQ + 1, dtype=np.float32)
    def angles(dim):
        th = (np.float32(1.0) / np.power(np.float32(1250), np.arange(0, dim, 2, dtype=np.float32) / np.float32(dim))).astype(np.float32)
        return (pos[:, None] * th[None, :]).astype(np.float32).T.astype(np.float64)
    aq = angles(2 * KVD)
    ak = np.repeat(angles(KVD), 2, axis=0)
    sign = np.where(np.arange(KVD) % 2 == 0, -1.0, 1.0)[:, None]
    t = np.stack([np.cos(aq) + np.sin(aq), np.cos(aq) - np.sin(aq), np.cos(ak), sign * np.sin(ak)])
    return t.reshape(4, NG, P, SEQ).transpose(2, 0, 1, 3).astype(np.float32).copy()


def count_choices(v, dve, sem, mark, gl, g8, gix, gif, onehot, w, cnt_acc):
    for t in range(NT):
        n = mark(v.max(g8[:, t, :], gl[:, t, :]))
    dve.wait_ge(sem, n)
    for t in range(NT):
        n = mark(v.max_index(gix[:, t, :], g8[:, t, :], gl[:, t, :]))
    dve.wait_ge(sem, n)
    n = mark(v.tensor_copy(gif[:, :, :], gix[:, :, 0:TOPK]))
    dve.wait_ge(sem, n)
    for k in range(TOPK):
        n = mark(v.tensor_tensor(onehot[:, :, k, :], w["iota"][:, :, :],
                                 gif[:, :, k:k + 1].to_broadcast([P, NT, EXPERTS]), ALU.is_equal))
    dve.wait_ge(sem, n)
    v.tensor_tensor(cnt_acc[:, :], cnt_acc[:, :], onehot[:, :, :, :].rearrange("p t k e -> p (t k e)"), ALU.add)


def attention_phase(nc, q_in, x3_out, w, cnt_acc, only=None):
    with ExitStack() as ctx:
        def sb(name, shape, dt=F32):
            return ctx.enter_context(nc.sbuf_tensor(name, shape, dt))

        x8 = sb("x8", [P, 8, D])
        y8 = sb("y8", [P, 8, D])
        xkeep = sb("xkeep", [P, NT, D])
        stats = sb("stats", [P, 8, 6])
        mv = sb("mv", [P, 8, 2])
        sd = sb("sd", [P, 8, 2])
        xn = sb("xn", [P, 8, D])
        xnT = sb("xnT", [P, 2, SEQ])
        sq = sb("sq", [P, 8, 2, D])
        hh = sb("hh", [P, 8, D])
        t1 = sb("t1", [P, 2, SEQ])
        t2 = sb("t2", [P, 2, SEQ])
        rot = sb("rot", [P, 2, SEQ])
        hi = sb("hi", [P, 2, NG, SEQ], F16)
        lo = sb("lo", [P, 2, NG, SEQ], F16)
        qst = sb("qst", [STK, HEADS, SEQ], F16)
        kst = sb("kst", [STK, HEADS, SEQ], F16)
        vt = sb("vt", [P, NT, KVD])
        pr = sb("pr", [P, 2, NT, SEQ])
        mS = sb("mS", [P, NT, HEADS])
        nm = sb("nm", [NG, NG, SEQ], F16)
        rec = sb("rec", [P, SEQ])
        oT = sb("oT", [P, NG, SEQ])
        gl = sb("gl", [P, NT, EXPERTS])
        g8 = sb("g8", [P, NT, 8])
        gix = sb("gix", [P, NT, 8], U32)
        gif = sb("gif", [P, NT, TOPK])
        onehot = sb("onehot", [P, NT, TOPK, EXPERTS])
        ps = ctx.enter_context(nc.psum_tensor("ps", [P, 8, 512], F32))

        names = ("x_in", "stats", "var", "sd", "xn", "xT", "xnT_v", "xnT_a", "ff", "sq", "ss", "h", "y",
                 "pair", "pair_free", "rot", "hi", "lo", "gate", "st", "st_read", "exp", "s", "s_read",
                 "stacked", "mrow", "mrow_sent", "pv_head", "norm", "wo", "x2", "v", "v_read", "dve", "x_out", "gate_read")
        sems = {n: ctx.enter_context(nc.semaphore("a_" + n)) for n in names}
        nums = sorted(s.num for s in sems.values())
        assert nums[-1] - nums[0] + 1 == len(nums)

        def iteration(i, new, att, old, prefetch):
            S = sems
            tiles = (list(range(NT)) if new else []) + (list(range(NT, 2 * NT)) if old else [])
            halves = ([0] if new else []) + ([1] if old else [])
            nt, nh = len(tiles), len(halves)
            with nc.Block(no_gpsimd_drain=True) as block:
                @block.sync
                def _(sp):
                    if new:
                        for j in range(NG):
                            sp.wait_ge(S["hi"], 2 * NG)
                            sp.wait_ge(S["lo"], 2 * NG)
                            if att:
                                sp.wait_ge(S["st"], 8 * (j + 1))
                            r = slice(DH * j, DH * j + DH)
                            for dst, src, row in ((qst, hi[r, 0], 0), (qst, lo[r, 0], 1), (qst, hi[r, 0], 2),
                                                  (kst, hi[r, 1], 0), (kst, hi[r, 1], 1), (kst, lo[r, 1], 2)):
                                sp.dma_start(dst[DH * row:DH * row + DH, NG * j:NG * j + NG, :],
                                             src).then_inc(S["stacked"], 16)
                            sp.wait_ge(S["mrow"], j + 1)
                            sp.dma_start(qst[3 * DH:STK, NG * j:NG * j + NG, :],
                                         nm[:, j, :]).then_inc(S["mrow_sent"], 16)
                    if prefetch:
                        sp.wait_ge(S["y"], nh)
                        sp.dma_start(x8[:, 0:NT, :], q_in[bass.ds(i + 1, 1)].rearrange(
                            "b (t p) d -> p (b t) d", p=P)).then_inc(S["x_in"], 16)
                    if old:
                        sp.wait_ge(S["y"], nh)
                        sp.dma_start(x3_out[bass.ds(i - 2, 1)].rearrange("b (t p) d -> p (b t) d", p=P),
                                     y8[:, NT:2 * NT, :]).then_inc(S["x_out"], 16)
                        sp.wait_ge(S["x_out"], 16)
                    if prefetch:
                        sp.wait_ge(S["x_in"], 16)
                    if new:
                        sp.wait_ge(S["stacked"], 16 * 6 * NG)
                        sp.wait_ge(S["mrow_sent"], 16 * NG)

                @block.vector
                def _(dve):
                    v = nc.vector
                    done = [0]

                    def link(ins):
                        done[0] += 1
                        ins.then_inc(S["dve"], 1)
                        return done[0]

                    def layernorm(src, lap):
                        for t in tiles:
                            n = link(v.bn_stats(stats[:, t, :], src[:, t, :]))
                        dve.wait_ge(S["dve"], n)
                        for t in tiles:
                            n = link(v.bn_aggr(mv[:, t, :], stats[:, t, :]))
                        dve.wait_ge(S["dve"], n)
                        a, b = tiles[0], tiles[-1] + 1
                        v.tensor_scalar(sd[:, a:b, 0], mv[:, a:b, 1], LN_EPS, None, ALU.add).then_inc(S["var"], 1)
                        dve.wait_ge(S["sd"], lap)
                        dve.wait_ge(S["dve"], link(v.reciprocal(sd[:, a:b, 0], sd[:, a:b, 1])))
                        if lap == 2:
                            dve.wait_ge(S["xT"], nh)
                        for t in tiles:
                            v.tensor_scalar(xn[:, t, :], src[:, t, :], mv[:, t, 0:1], sd[:, t, 0:1],
                                            ALU.subtract, ALU.mult).then_inc(S["xn"], 1)
                        if new:
                            dve.wait_ge(S["xT"], nh * (lap - 1) + 1)
                            if lap == 2:
                                dve.wait_ge(S["ff"], nt // 2)
                            v.tensor_copy(xnT[:, 0, :], ps[:, 4, :]).then_inc(S["xnT_v"], 1)

                    if new or old:
                        layernorm(x8, 1)
                        for k in range(nt // 2):
                            dve.wait_ge(S["sq"], k + 1)
                            t = tiles[2 * k]
                            v.tensor_tensor(hh[:, t:t + 2, :], sq[:, t:t + 2, 0, :], sq[:, t:t + 2, 1, :],
                                            ALU.add).then_inc(S["ss"], 1)
                        for k, hf in enumerate(halves):
                            dve.wait_ge(S["h"], k + 1)
                            v.tensor_tensor(y8[:, NT * hf:NT * hf + NT, :], x8[:, NT * hf:NT * hf + NT, :],
                                            hh[:, NT * hf:NT * hf + NT, :], ALU.add).then_inc(S["y"], 1)
                        dve.wait_ge(S["y"], nh)
                        layernorm(y8, 2)
                    if old:
                        dve.wait_ge(S["gate"], 1)
                        v.tensor_tensor(gl[:, :, :], ps[:, 7, 0:NT * EXPERTS].rearrange(
                            "p (t e) -> p t e", t=NT), w["gate_b"][:, :, :], ALU.add).then_inc(S["gate_read"], 1)
                        dve.wait_ge(S["gate_read"], 1)
                        count_choices(v, dve, S["dve"], link, gl, g8, gix, gif, onehot, w, cnt_acc)
                    if new:
                        for p in range(2 * NG):
                            kq, g = p // NG, p % NG
                            bank = 2 * (p % 3)
                            dve.wait_ge(S["pair"], p + 1)
                            n = link(v.tensor_tensor(t1[:, p % 2, :], ps[:, bank, :],
                                                     w["rope"][:, 2 * kq, g, :], ALU.mult))
                            v.tensor_tensor(t2[:, p % 2, :], ps[:, bank + 1, :], w["rope"][:, 2 * kq + 1, g, :],
                                            ALU.mult).then_inc(S["pair_free"], 1)
                            dve.wait_ge(S["pair_free"], p + 1)
                            dve.wait_ge(S["dve"], n)
                            if p >= 2:
                                dve.wait_ge(S["hi"], p - 1)
                                dve.wait_ge(S["lo"], p - 1)
                            v.tensor_tensor(rot[:, p % 2, :], t1[:, p % 2, :], t2[:, p % 2, :],
                                            ALU.add).then_inc(S["rot"], 1)

                    def guard_row(j):
                        n = 4 * HEADS // NG * (j + 1) + j
                        dve.wait_ge(S["s"], n + 1)
                        v.tensor_scalar(nm[:, j, :], ps[0:NG, 4 + n % 2, :], -1.0, None,
                                        ALU.mult).then_inc(S["mrow"], 1)

                    def normalise(j):
                        dve.wait_ge(S["pv_head"], NG * (j + 1))
                        dve.wait_ge(S["dve"], link(v.reciprocal(rec[:, :], ps[:, 7, :])))
                        v.tensor_tensor(oT[:, j, :], ps[:, 6, :], rec[:, :], ALU.mult).then_inc(S["norm"], 1)
                        dve.wait_ge(S["norm"], j + 1)

                    for s in range(HEADS):
                        j = s // NG
                        if new:
                            for t in range(NT):
                                n = 4 * s + j + t
                                dve.wait_ge(S["s"], n + 1)
                                v.tensor_reduce(mS[:, t, s:s + 1], ps[:, 4 + n % 2, :], AX,
                                                ALU.max).then_inc(S["s_read"], 1)
                            if s % NG == NG - 1:
                                guard_row(j)
                        if att and s % NG == 1 and s > NG:
                            normalise(j - 1)
                    if att:
                        normalise(NG - 1)
                        dve.wait_ge(S["wo"], 1)
                        v.tensor_tensor(x8[:, NT:2 * NT, :], xkeep[:, :, :], ps[:, 4, :].rearrange(
                            "p (t d) -> p t d", t=NT), ALU.add).then_inc(S["x2"], 1)
                        dve.wait_ge(S["x2"], 1)
                    if new:
                        v.tensor_copy(xkeep[:, :, :], y8[:, 0:NT, :])

                @block.scalar
                def _(act):
                    a = nc.scalar
                    if new or old:
                        lo_t, hi_t = tiles[0], tiles[-1] + 1
                        for lap in (1, 2):
                            act.wait_ge(S["var"], lap)
                            a.activation(sd[:, lo_t:hi_t, 1], sd[:, lo_t:hi_t, 0], ACT.Sqrt).then_inc(S["sd"], 1)
                            if old:
                                act.wait_ge(S["xT"], nh * lap)
                                if lap == 2:
                                    act.wait_ge(S["ff"], nt // 2)
                                a.copy(xnT[:, 1, :], ps[:, 5, :]).then_inc(S["xnT_a"], 1)
                            if lap == 1:
                                for k in range(nt // 2):
                                    t = tiles[2 * k]
                                    act.wait_ge(S["ff"], k + 1)
                                    a.activation(sq[:, t:t + 2, :, :], ps[:, k, :].rearrange(
                                        "p (t c d) -> p t c d", t=2, c=2), ACT.Square).then_inc(S["sq"], 1)
                                for k, hf in enumerate(halves):
                                    act.wait_ge(S["ss"], 2 * k + 2)
                                    hv = hh[:, NT * hf:NT * hf + NT, :]
                                    a.activation(hv, hv, ACT.Sqrt, scale=0.25).then_inc(S["h"], 1)
                    if new:
                        for p in range(2 * NG):
                            act.wait_ge(S["rot"], p + 1)
                            a.copy(hi[:, p // NG, p % NG, :], rot[:, p % 2, :]).then_inc(S["hi"], 1)
                    if att:
                        for s in range(HEADS):
                            if s >= 2:
                                act.wait_ge(S["pv_head"], s - 1)
                            for u in range(2):
                                act.wait_ge(S["st"], 2 * s + u + 1)
                                a.activation(pr[:, s % 2, 2 * u:2 * u + 2, :], ps[:, 2 * u:2 * u + 2, :],
                                             ACT.Exp, scale=ATT_SCALE).then_inc(S["exp"], 1)
                    if new:
                        for t in range(NT):
                            act.wait_ge(S["v"], t + 1)
                            a.copy(vt[:, t, :], ps[:, t, :]).then_inc(S["v_read"], 1)

                @block.gpsimd
                def _(pool):
                    if new:
                        for p in range(2 * NG):
                            pool.wait_ge(S["hi"], p + 1)
                            nc.gpsimd.tensor_tensor(lo[:, p // NG, p % NG, :], rot[:, p % 2, :],
                                                    hi[:, p // NG, p % NG, :], ALU.subtract).then_inc(S["lo"], 1)

                @block.tensor
                def _(pe):
                    mm = nc.tensor.matmul

                    def transposes(lap):
                        for k, hf in enumerate(halves):
                            pe.wait_ge(S["xn"], nt * (lap - 1) + NT * (k + 1))
                            for t in range(NT):
                                ins = nc.tensor.transpose(ps[:, 4 + hf, P * t:P * t + P], xn[:, NT * hf + t, :],
                                                          w["ident"][:, :])
                            ins.then_inc(S["xT"], 1)

                    def xnT_ready(lap):
                        if new:
                            pe.wait_ge(S["xnT_v"], lap)
                        if old:
                            pe.wait_ge(S["xnT_a"], lap)

                    if new or old:
                        transposes(1)
                        xnT_ready(1)
                        for k in range(nt // 2):
                            for u in range(2):
                                t = tiles[2 * k + u]
                                ins = mm(ps[:, k, 256 * u:256 * u + 256], xnT[:, t // NT, P * (t % NT):P * (t % NT) + P],
                                         w["csT"][:, :], start=True, stop=True)
                            ins.then_inc(S["ff"], 1)
                        transposes(2)
                        xnT_ready(2)
                        pe.wait_ge(S["sq"], nt // 2)
                    if old:
                        for t in range(NT):
                            ins = mm(ps[:, 7, EXPERTS * t:EXPERTS * t + EXPERTS], xnT[:, 1, P * t:P * t + P],
                                     w["gwT"][:, :], start=True, stop=True)
                        ins.then_inc(S["gate"], 1)
                    if new:
                        for p in range(2 * NG):
                            kq, g = p // NG, p % NG
                            if p >= 3:
                                pe.wait_ge(S["pair_free"], p - 2)
                            for c in range(2):
                                if kq == 0:
                                    wt = w["wq"][:, g, c, :]
                                else:
                                    wt = w["wk"][:, c, P * g:P * g + P]
                                ins = mm(ps[:, 2 * (p % 3) + c, :], wt, xnT[:, 0, :], start=True, stop=True)
                            ins.then_inc(S["pair"], 1)

                    def shifted_scores(s):
                        for u in range(2):
                            if s >= 1:
                                pe.wait_ge(S["exp"], 2 * (s - 1) + u + 1)
                            elif new:
                                pe.wait_ge(S["pair_free"], 2 * NG)
                            for kt in (2 * u, 2 * u + 1):
                                ins = mm(ps[:, kt, :], kst[:, s, P * kt:P * kt + P], qst[:, s, :],
                                         start=True, stop=True)
                            ins.then_inc(S["st"], 1)

                    def scores(s):
                        j, g = s // NG, s % NG
                        r = slice(DH * j, DH * j + DH)
                        if s == 0:
                            pe.wait_ge(S["hi"], 2 * NG)
                            pe.wait_ge(S["pair_free"], 2 * NG)
                        for t in range(NT):
                            n = 4 * s + j + t
                            job_free(n)
                            mm(ps[:, 4 + n % 2, :], hi[r, 0, g, P * t:P * t + P], hi[r, 1, g, :],
                               start=True, stop=True).then_inc(S["s"], 1)

                    def job_free(n):
                        m = n - 2
                        if m < 0:
                            return
                        guards = (m + 1) // 17
                        if m % 17 == 16:
                            pe.wait_ge(S["mrow"], guards)
                        else:
                            pe.wait_ge(S["s_read"], m + 1 - guards)

                    def guard_row(j):
                        n = 16 * (j + 1) + j
                        pe.wait_ge(S["s_read"], 16 * (j + 1))
                        job_free(n)
                        for t in range(NT):
                            ins = nc.tensor.transpose(ps[0:NG, 4 + n % 2, P * t:P * t + P],
                                                      mS[:, t, NG * j:NG * j + NG], w["ident"][:, :])
                        ins.then_inc(S["s"], 1)

                    def values(s):
                        j, g = s // NG, s % NG
                        h = NG * g + j
                        pe.wait_ge(S["exp"], 2 * s + 2)
                        if g == 0:
                            if j:
                                pe.wait_ge(S["norm"], j)
                            elif old:
                                pe.wait_ge(S["gate_read"], 1)
                        rows = slice(DH * g, DH * g + DH)
                        for kt in range(NT):
                            mm(ps[rows, 6, :], vt[:, kt, DH * h:DH * h + DH], pr[:, s % 2, kt, :],
                               start=kt == 0, stop=kt == NT - 1, skip_group_check=True)
                            ins = mm(ps[rows, 7, :], w["ones"][:, 0:DH], pr[:, s % 2, kt, :],
                                     start=kt == 0, stop=kt == NT - 1, skip_group_check=True)
                        ins.then_inc(S["pv_head"], 1)

                    for s in range(HEADS):
                        if att:
                            shifted_scores(s)
                        if new:
                            scores(s)
                            if s % NG == NG - 1:
                                guard_row(s // NG)
                        if att and s >= 1:
                            values(s - 1)
                    if att:
                        values(HEADS - 1)
                        pe.wait_ge(S["norm"], NG)
                        if new:
                            pe.wait_ge(S["mrow"], NG)
                            pe.wait_ge(S["s_read"], 4 * HEADS)
                        for t in range(NT):
                            for j in range(NG):
                                ins = mm(ps[:, 4, P * t:P * t + P], oT[:, j, P * t:P * t + P], w["wo"][:, j, :],
                                         start=j == 0, stop=j == NG - 1)
                        ins.then_inc(S["wo"], 1)
                    if new:
                        if att:
                            pe.wait_ge(S["exp"], 2 * HEADS)
                        for t in range(NT):
                            mm(ps[:, t, :], xnT[:, 0, P * t:P * t + P], w["wv"][:, :],
                               start=True, stop=True).then_inc(S["v"], 1)
            nc.gpsimd.sem_clear(range(nums[0], nums[-1] + 1))
            nc.all_engine_barrier(sem_only=True)

        with nc.Block(no_gpsimd_drain=True) as block:
            @block.vector
            def _(dve):
                nc.vector.memset(kst[3 * DH:STK, :, :], 1.0)

            @block.sync
            def _(sp):
                sp.dma_start(x8[:, 0:NT, :], q_in[0].rearrange("(t p) d -> p t d", p=P)).then_inc(sems["x_in"], 16)
                sp.wait_ge(sems["x_in"], 16)
        nc.gpsimd.sem_clear(range(nums[0], nums[-1] + 1))
        nc.all_engine_barrier(sem_only=True)

        iteration(0, True, False, False, True)
        iteration(1, True, True, False, True)
        with nc.Fori(2, BATCH - 1, 1) as i:
            iteration(i, True, True, True, True)
        iteration(BATCH - 1, True, True, True, False)
        iteration(BATCH, False, True, True, False)
        iteration(BATCH + 1, False, False, True, False)



TWO_PI_HI = 6.28125
TWO_PI_LO = float(2 * np.pi - 6.28125)
ROUND = 1.5 * 2.0 ** 23
PI_F32 = 3.1415925


def reduce_angle(v, wait, r, k, x, quarter):
    wait(v.tensor_scalar(r, x, quarter * float(np.pi) / 2, None, ALU.add))
    wait(v.tensor_scalar(k, r, float(1 / (2 * np.pi)), ROUND, ALU.mult, ALU.add))
    wait(v.tensor_scalar(k, k, ROUND, None, ALU.subtract))
    wait(v.scalar_tensor_tensor(r, k, -TWO_PI_HI, r, ALU.mult, ALU.add))
    wait(v.scalar_tensor_tensor(r, k, -TWO_PI_LO, r, ALU.mult, ALU.add))
    return v.tensor_scalar(r, r, PI_F32, -PI_F32, ALU.min, ALU.max)


def consts_p1():
    return {
        "rope": rope_tables(),
        "ident": np.eye(P, dtype=np.float32),
        "iota": np.tile(np.arange(EXPERTS, dtype=np.float32), (P, NT, 1)),
    }


def layout_p1(x):
    wk = np.asarray(x["L0_attn_Wk"])
    wo = np.asarray(x["L0_attn_Wo"]).reshape(NG, NG, DH, 2, D)
    return {
        "q": np.asarray(x["L0_attn_q"]),
        "wq": np.asarray(x["L0_attn_Wq"]).reshape(D, NG, P, 2).transpose(0, 1, 3, 2),
        "wk": np.stack([wk, wk.reshape(D, KVD // 2, 2)[:, :, ::-1].reshape(D, KVD)], 1),
        "wv": np.asarray(x["L0_attn_Wv"]),
        "wo": wo.transpose(0, 2, 1, 3, 4).reshape(P, NG, 2, D),
        "angles": np.stack([np.asarray(x["L0_ffn_" + n]) for n in
                            ("theta", "theta_noise", "phi", "phi_noise")], 1),
        "gwT": np.asarray(x["L1_ffn_gate_w"]).T,
        "gate_b": np.broadcast_to(np.asarray(x["L1_ffn_gate_b"]), (P, NT, EXPERTS)),
    }


def load_layer0(nc, ctx, ins, cnt_acc):
    sb = lambda name, shape, dt=F32: ctx.enter_context(nc.sbuf_tensor(name, shape, dt))
    w = {"rope": sb("rope", [P, 4, NG, SEQ]), "wq": sb("wq", [P, NG, 2, P]), "wk": sb("wk", [P, 2, KVD]),
         "wv": sb("wv", [P, KVD]), "wo": sb("wo", [P, NG, D]), "csT": sb("csT", [P, 2 * D]),
         "ones": sb("ones", [P, P]), "ident": sb("ident", [P, P]), "gwT": sb("gwT", [P, EXPERTS]),
         "gate_b": sb("gate_b", [P, NT, EXPERTS]), "iota": sb("iota", [P, NT, EXPERTS])}
    with ExitStack() as tmp:
        sbt = lambda name, shape: tmp.enter_context(nc.sbuf_tensor(name, shape, F32))
        wo2, ang, red, k = sbt("wo2", [P, NG, 2, D]), sbt("ang", [P, 4, D]), sbt("red", [P, 2, D]), sbt("kk", [P, 2, D])
        loaded, vd, sn = (tmp.enter_context(nc.semaphore("l_" + n)) for n in ("loaded", "dve", "sin"))
        names = ("rope", "wq", "wk", "wv", "ident", "gwT", "gate_b", "iota")
        with nc.Block(no_gpsimd_drain=True) as block:
            @block.sync
            def _(sp):
                for n in names:
                    sp.dma_start(w[n][:], ins[n]).then_inc(loaded, 16)
                sp.wait_ge(loaded, 16 * len(names))
                sp.dma_start(wo2[:], ins["wo"]).then_inc(loaded, 16)
                sp.dma_start(ang[:], ins["angles"]).then_inc(loaded, 16)

            @block.vector
            def _(dve):
                v, n = nc.vector, [0]

                def wait(i):
                    n[0] += 1
                    i.then_inc(vd, 1)
                    dve.wait_ge(vd, n[0])
                v.memset(w["ones"][:, :], 1.0)
                v.memset(cnt_acc[:, :], 0.0)
                dve.wait_ge(loaded, 16 * (len(names) + 2))
                v.tensor_tensor(w["wo"][:, :, :], wo2[:, :, 0, :], wo2[:, :, 1, :], ALU.add)
                for c in range(2):
                    wait(v.tensor_tensor(ang[:, 2 * c, :], ang[:, 2 * c, :], ang[:, 2 * c + 1, :], ALU.add))
                    wait(reduce_angle(v, wait, red[:, c, :], k[:, c, :], ang[:, 2 * c, :], 1 - c))

            @block.scalar
            def _(act):
                act.wait_ge(vd, 14)
                nc.scalar.activation(w["csT"][:, :], red[:, :, :].rearrange("p c d -> p (c d)"), ACT.Sin).then_inc(sn, 1)
        nc.gpsimd.sem_clear(range(min(loaded.num, vd.num, sn.num), max(loaded.num, vd.num, sn.num) + 1))
        nc.all_engine_barrier(sem_only=True)
    return w




N_STATE, R, HP, M_HEADS = 64, 2, 8, 32
D_INNER = M_HEADS * HP
BLK = 32
RMS_EPS = 1e-6
STATE_SCALE = float((N_STATE * R) ** -0.5)
CLAMP = 85.0
DT_MIN, DT_MAX = 1e-4, 0.5
MID, REF1, REF_END, IN_BLOCK, FROM_START, WHOLE = 0, 1, 4, 5, 6, 7


def decay_sums():
    j, m = np.arange(P)[:, None], np.arange(P)[None, :]
    mid = BLK * (m // BLK) + BLK // 2 - 1
    sums = [((j > m) & (j <= mid)) * 1.0 - ((j > mid) & (j <= m)) * 1.0]
    sums += [(j > m) & (j < BLK * i) for i in (1, 2, 3)]
    sums += [j > m, (j <= m) & (j >= BLK * (m // BLK)), j <= m, j >= 0 * m]
    return np.stack([np.broadcast_to(s, (P, P)).astype(np.float32) for s in sums], 1)


def consts_p2():
    j, m = np.arange(P)[:, None], np.arange(P)[None, :]
    same = j // BLK == m // BLK
    tri = (j <= m).astype(np.float32)
    one = np.ones((P, P), np.float32)
    return {
        "sums": decay_sums(),
        "moves": np.stack([tri, one, (j == m + 1).astype(np.float32),
                           ((j == 0) & (m == P - 1)).astype(np.float32)], 1),
        "masks": np.stack([(same & (m > j)), (m // BLK > j // BLK)], 1).astype(np.float32),
    }


def layout_p2(x):
    w = np.asarray(x["L1_attn_W_in"])
    z, xr, rest, th = w[:, :256], w[:, 256:768], w[:, 768:1024], w[:, 1024:]
    rep = lambda a: np.broadcast_to(np.asarray(a), (P, NT, M_HEADS))
    b, c = np.asarray(x["L1_attn_B_norm_bias"])[0], np.asarray(x["L1_attn_C_norm_bias"])[0]
    return {
        "w_in": np.concatenate([xr, z, rest, th], 1),
        "w_out": np.asarray(x["L1_attn_W_out"]).reshape(2, P, D).transpose(1, 0, 2),
        "a_log": rep(x["L1_attn_A_log"]), "dt_bias": rep(x["L1_attn_dt_bias"]),
        "bc_bias": np.broadcast_to(np.stack([b, b, c]), (P, 3, N_STATE)),
        "ew": np.asarray(x["L1_ffn_expert_w"]).transpose(2, 0, 1),
        "eb": np.asarray(x["L1_ffn_expert_b"]).T,
    }


def load_layer1(nc, ctx, ins):
    sb = lambda name, shape: ctx.enter_context(nc.sbuf_tensor(name, shape, F32))
    w = {"w_in": sb("w_in", [P, 1056]), "w_out": sb("w_out", [P, 2, D]), "a_log": sb("a_log", [P, NT, M_HEADS]),
         "dt_bias": sb("dt_bias", [P, NT, M_HEADS]), "bc_bias": sb("bc_bias", [P, 3, N_STATE]),
         "ew": sb("ew", [P, EXPERTS, D]), "eb": sb("eb", [P, EXPERTS]), "sums": sb("sums", [P, 8, P]),
         "moves": sb("moves", [P, 4, P]), "masks": sb("masks", [P, 2, P]),
         "ident": sb("ident1", [P, P]), "gwT": sb("gwT1", [P, EXPERTS]),
         "gate_b": sb("gate_b1", [P, NT, EXPERTS]), "iota": sb("iota1", [P, NT, EXPERTS])}
    names = list(w)
    w["a"] = sb("a", [P, NT, M_HEADS])
    with ExitStack() as tmp:
        loaded, vd, ex = (tmp.enter_context(nc.semaphore("k_" + n)) for n in ("loaded", "dve", "exp"))
        with nc.Block(no_gpsimd_drain=True) as block:
            @block.sync
            def _(sp):
                for n in names:
                    sp.dma_start(w[n][:], ins[n]).then_inc(loaded, 16)

            @block.scalar
            def _(act):
                act.wait_ge(loaded, 16 * len(names))
                nc.scalar.activation(w["a"][:], w["a_log"][:], ACT.Exp).then_inc(ex, 1)

            @block.vector
            def _(dve):
                dve.wait_ge(ex, 1)
                nc.vector.tensor_scalar(w["a"][:], w["a"][:], -1.0, None, ALU.mult)
                nc.vector.tensor_scalar(w["bc_bias"][:, 2, :], w["bc_bias"][:, 2, :], STATE_SCALE, None, ALU.mult)
        nums = (loaded.num, vd.num, ex.num)
        nc.gpsimd.sem_clear(range(min(nums), max(nums) + 1))
        nc.all_engine_barrier(sem_only=True)
    return w


def expert_weights(nc, tag, w, cnt_acc, ew_s, negb, sumb):
    with ExitStack() as tmp:
        share = tmp.enter_context(nc.sbuf_tensor(tag + "share", [P, EXPERTS], F32))
        pc = tmp.enter_context(nc.psum_tensor(tag + "pc", [P, NT * TOPK * EXPERTS], F32))
        counted, vd = (tmp.enter_context(nc.semaphore(tag + n)) for n in ("counted", "dve"))
        with nc.Block(no_gpsimd_drain=True) as block:
            @block.tensor
            def _(pe):
                nc.tensor.matmul(pc[:, :], w["moves"][:, 1, :], cnt_acc[:, :], start=True, stop=True).then_inc(counted, 1)

            @block.vector
            def _(dve):
                v, n = nc.vector, [0]

                def wait(i):
                    n[0] += 1
                    i.then_inc(vd, 1)
                    dve.wait_ge(vd, n[0])
                dve.wait_ge(counted, 1)
                wait(v.tensor_reduce(share[:, :], pc[:, :].rearrange("p (a e) -> p e a", e=EXPERTS), AX, ALU.add))
                wait(v.tensor_scalar(share[:, :], share[:, :], 0.5 / (BATCH * SEQ * TOPK), None, ALU.mult))
                v.tensor_tensor(ew_s[:, :, :], w["ew"][:, :, :],
                                share[:, :].rearrange("p (e o) -> p e o", o=1).to_broadcast([P, EXPERTS, D]), ALU.mult)
                wait(v.tensor_tensor(negb[:, :], w["eb"][:, :], share[:, :], ALU.mult))
                wait(v.tensor_reduce(sumb[:, :], negb[:, :], AX, ALU.add))
                wait(v.tensor_scalar(negb[:, :], negb[:, :], -1.0, None, ALU.mult))
                v.memset(cnt_acc[:, :], 0.0)
        nc.gpsimd.sem_clear(range(min(counted.num, vd.num), max(counted.num, vd.num) + 1))
        nc.all_engine_barrier(sem_only=True)


def state_phase(nc, x_in, x_out, w, ew_s, negb, sumb, cnt_acc, last):
    with ExitStack() as ctx:
        pre = "f_" if last else "m_"

        def sb(name, shape, dt=F32):
            return ctx.enter_context(nc.sbuf_tensor(pre + name, shape, dt))

        x = sb("x", [P, NT, D])
        y = sb("y", [P, NT, D])
        stats, mv, sd = sb("stats", [P, NT, 6]), sb("mv", [P, NT, 2]), sb("sd", [P, NT, 2])
        xn, xnT = sb("xn", [P, NT, D]), sb("xnT", [P, SEQ])
        acc = sb("acc", [P, 2, SEQ])
        ps = ctx.enter_context(nc.psum_tensor(pre + "ps", [P, 8, 512], F32))
        if not last:
            xr, zs = sb("xr", [P, NT, M_HEADS, R, HP]), sb("zs", [P, NT, D_INNER])
            bc, dl, th = sb("bc", [P, NT, 3, N_STATE]), sb("dl", [P, NT, 2, M_HEADS]), sb("th", [P, NT, M_HEADS])
            t_dt, dt = sb("t_dt", [P, NT, M_HEADS]), sb("dt", [P, NT, M_HEADS])
            lam, gam, bet = sb("lam", [P, NT, M_HEADS]), sb("gam", [P, NT, M_HEADS]), sb("bet", [P, NT, M_HEADS])
            wgt, lda, md = sb("wgt", [P, NT, M_HEADS]), sb("lda", [P, NT, M_HEADS]), sb("md", [P, NT])
            dec = sb("dec", [P, 9, NT, M_HEADS])
            mid = sb("mid", [P, NT, M_HEADS])
            coef = sb("coef", [P, 6, NT, M_HEADS])
            ang, angk = sb("ang", [P, 2, NT, M_HEADS]), sb("angk", [P, 2, NT, M_HEADS])
            sc = sb("sc", [P, 2, NT, M_HEADS])
            sqb, rs12 = sb("sqb", [P, NT, 3, N_STATE]), sb("rs12", [P, 2, NT * 3])
            br = sb("br", [P, NT, 4, N_STATE])
            rp = sb("rp", [P, 4, NT, 3, N_STATE // 2])
            bt = sb("bt", [P, NT, 2, P])
            gm = sb("gm", [P, 2, NT, R, P])
            gd = sb("gd", [P, NT, R])
            xv = sb("xv", [P, 2, 6, M_HEADS, R, HP])
            state = sb("state", [N_STATE, M_HEADS, HP])
            part = sb("part", [P, 2, 4, M_HEADS, HP])
            yz = sb("yz", [P, NT, D_INNER])
            yy = sb("yy", [P, NT, D_INNER])
            rms = sb("rms", [P, 2, NT])
            yzT = sb("yzT", [P, NT, 2, P])
            gl, g8 = sb("gl", [P, NT, EXPERTS]), sb("g8", [P, NT, 8])
            gix, gif = sb("gix", [P, NT, 8], U32), sb("gif", [P, NT, TOPK])
            onehot = sb("onehot", [P, NT, TOPK, EXPERTS])
        names = ("x_in", "x_out", "dve", "var", "sd", "xn", "xT", "xnT", "ex", "ex_read", "accT", "acc", "y",
                 "proj", "proj_v", "proj_a", "silu", "e1", "e2", "e3", "e4", "u", "ang_ps", "ang_r", "sin",
                 "sum_ps", "sum_v", "dec", "rms12", "br", "bt_ps", "bt", "g_ps", "g", "xv", "ymm", "y_read",
                 "st_mm", "state", "ms", "rms", "yz", "yzT_ps", "yzT", "wo", "gate", "gate_read", "beta", "beta_ps")
        S = {n: ctx.enter_context(nc.semaphore(pre + n)) for n in names}
        nums = sorted(s.num for s in S.values())
        assert nums[-1] - nums[0] + 1 == len(nums)

        with nc.Fori(0, BATCH, 1) as b:
            with nc.Block(no_gpsimd_drain=True) as block:
                @block.sync
                def _(sp):
                    sp.dma_start(x[:, :, :], x_in[bass.ds(b, 1)].rearrange(
                        "b (t p) d -> p (b t) d", p=P)).then_inc(S["x_in"], 16)
                    sp.wait_ge(S["y"], 1 if last else 1 + NT)
                    sp.dma_start(x_out[bass.ds(b, 1)].rearrange("b (t p) d -> p (b t) d", p=P),
                                 y[:, :, :]).then_inc(S["x_out"], 16)
                    sp.wait_ge(S["x_out"], 16)

                @block.vector
                def _(dve):
                    v, done = nc.vector, [0]

                    def mark(ins):
                        done[0] += 1
                        ins.then_inc(S["dve"], 1)
                        return done[0]

                    def wait(ins):
                        dve.wait_ge(S["dve"], mark(ins))

                    def layernorm(src, lap):
                        for t in range(NT):
                            n = mark(v.bn_stats(stats[:, t, :], src[:, t, :]))
                        dve.wait_ge(S["dve"], n)
                        for t in range(NT):
                            n = mark(v.bn_aggr(mv[:, t, :], stats[:, t, :]))
                        dve.wait_ge(S["dve"], n)
                        v.tensor_scalar(sd[:, :, 0], mv[:, :, 1], LN_EPS, None, ALU.add).then_inc(S["var"], 1)
                        dve.wait_ge(S["sd"], lap)
                        wait(v.reciprocal(sd[:, :, 0], sd[:, :, 1]))
                        for t in range(NT):
                            v.tensor_scalar(xn[:, t, :], src[:, t, :], mv[:, t, 0:1], sd[:, t, 0:1],
                                            ALU.subtract, ALU.mult).then_inc(S["xn"], 1)
                        dve.wait_ge(S["xT"], lap)
                        v.tensor_copy(xnT[:, :], ps[:, 4, :]).then_inc(S["xnT"], 1)

                    dve.wait_ge(S["x_in"], 16)
                    layernorm(x, 1)
                    for e in range(EXPERTS):
                        dve.wait_ge(S["ex"], e + 1)
                        if e == 0:
                            ins = v.tensor_scalar(acc[:, 0, :], ps[:, 0, :], negb[:, 0:1], sumb[:, 0:1],
                                                  ALU.max, ALU.add)
                        else:
                            dve.wait_ge(S["ex_read"], e)
                            ins = v.scalar_tensor_tensor(acc[:, e % 2, :], ps[:, e % 4, :], negb[:, e:e + 1],
                                                         acc[:, (e - 1) % 2, :], ALU.max, ALU.add)
                        ins.then_inc(S["ex_read"], 1)
                    dve.wait_ge(S["accT"], 1)
                    v.tensor_tensor(y[:, :, :], x[:, :, :], ps[:, 5, :].rearrange("p (t d) -> p t d", t=NT),
                                    ALU.add).then_inc(S["y"], 1)
                    if last:
                        return
                    dve.wait_ge(S["y"], 1)
                    layernorm(y, 2)
                    for t in range(NT):
                        dve.wait_ge(S["proj"], t + 1)
                        dve.wait_ge(S["silu"], 2 * t + 2)
                        s0 = 3 * (t % 2)
                        v.tensor_copy(bc[:, t, :, :], ps[:, s0 + 1, 256:448].rearrange("p (c n) -> p c n", c=3))
                        v.tensor_copy(dl[:, t, :, :], ps[:, s0 + 1, 448:512].rearrange("p (c n) -> p c n", c=2))
                        v.tensor_copy(th[:, t, :], ps[:, s0 + 2, 0:M_HEADS]).then_inc(S["proj_v"], 1)
                    dve.wait_ge(S["proj_v"], NT)
                    wait(v.tensor_tensor(t_dt[:, :, :], dl[:, :, 0, :], w["dt_bias"][:, :, :], ALU.add))
                    v.tensor_scalar(t_dt[:, :, :], t_dt[:, :, :], 0.0, None, ALU.min).then_inc(S["u"], 1)
                    dve.wait_ge(S["e2"], 1)
                    wait(v.tensor_scalar(dt[:, :, :], dt[:, :, :], DT_MIN, DT_MAX, ALU.max, ALU.min))
                    mark(v.tensor_tensor(lda[:, :, :], dt[:, :, :], w["a"][:, :, :], ALU.mult))
                    wait(v.tensor_reduce(md[:, :], dt[:, :, :], AX, ALU.add))
                    wait(v.tensor_scalar(md[:, :], md[:, :], -1.0 / M_HEADS, None, ALU.mult))
                    v.tensor_tensor(th[:, :, :], th[:, :, :], md[:, :].rearrange(
                        "p (t o) -> p t o", o=1).to_broadcast([P, NT, M_HEADS]), ALU.mult).then_inc(S["e3"], 1)
                    wait(v.tensor_scalar(lam[:, :, :], lam[:, :, :], 1.0, None, ALU.add))
                    wait(v.reciprocal(lam[:, :, :], lam[:, :, :]))
                    wait(v.tensor_tensor(gam[:, :, :], lam[:, :, :], dt[:, :, :], ALU.mult))
                    v.tensor_tensor(bet[:, :, :], dt[:, :, :], gam[:, :, :], ALU.subtract).then_inc(S["beta"], 1)
                    wait(v.tensor_tensor(sqb[:, :, :, :], bc[:, :, :, :], bc[:, :, :, :], ALU.mult))
                    wait(v.tensor_reduce(rs12[:, 0, :], sqb[:, :, :, :].rearrange("p t c n -> p (t c) n"), AX, ALU.add))
                    v.tensor_scalar(rs12[:, 0, :], rs12[:, 0, :], 1.0 / N_STATE, RMS_EPS, ALU.mult,
                                    ALU.add).then_inc(S["rms12"], 1)
                    dve.wait_ge(S["ang_ps"], 1)
                    for q in range(2):
                        ins = reduce_angle(v, wait, ang[:, q], angk[:, q],
                                           ps[:, 7, 0:128].rearrange("p (t h) -> p t h", t=NT), q)
                    ins.then_inc(S["ang_r"], 1)
                    dve.wait_ge(S["sum_ps"], 1)
                    v.tensor_scalar(mid[:, :, :], ps[:, 0, 0:128].rearrange("p (t h) -> p t h", t=NT),
                                    CLAMP, -CLAMP, ALU.min, ALU.max).then_inc(S["sum_v"], 1)
                    dve.wait_ge(S["beta_ps"], 1)
                    wait(v.tensor_tensor(wgt[:, :, :], gam[:, :, :], ps[:, 7, 128:256].rearrange(
                        "p (t h) -> p t h", t=NT), ALU.add))
                    dve.wait_ge(S["dec"], 1)
                    mark(v.tensor_copy(coef[:, 5], gam[:, :, :]))
                    wait(v.tensor_tensor(
                        coef[:, 0:5].rearrange("p c t h -> p c (t h)"), dec[:, 0:5].rearrange("p c t h -> p c (t h)"),
                        wgt[:, :, :].rearrange("p (o t) h -> p o (t h)", o=1).to_broadcast([P, 5, NT * M_HEADS]),
                        ALU.mult))
                    dve.wait_ge(S["e4"], 1)
                    wait(v.reciprocal(rs12[:, 0, :], rs12[:, 1, :]))
                    wait(v.tensor_tensor(sqb[:, :, :, :].rearrange("p t c n -> p (t c) n"),
                                         bc[:, :, :, :].rearrange("p t c n -> p (t c) n"),
                                         rs12[:, 0, :].rearrange("p (c o) -> p c o", o=1).to_broadcast(
                                             [P, NT * 3, N_STATE]), ALU.mult))
                    wait(v.tensor_tensor(sqb[:, :, :, :].rearrange("p t c n -> p t (c n)"),
                                         sqb[:, :, :, :].rearrange("p t c n -> p t (c n)"),
                                         w["bc_bias"][:, :, :].rearrange("p (o c) n -> p o (c n)", o=1).to_broadcast(
                                             [P, NT, 3 * N_STATE]), ALU.mult))
                    dve.wait_ge(S["sin"], 1)
                    half = N_STATE // 2
                    for c, (s0, k) in enumerate(((0, 1), (half, 0), (0, 0), (half, 1))):
                        n = mark(v.tensor_tensor(rp[:, c], sqb[:, :, :, s0:s0 + half],
                                                 sc[:, k].rearrange("p t (o n) -> p t o n", o=1).to_broadcast(
                                                     [P, NT, 3, half]), ALU.mult))
                    dve.wait_ge(S["dve"], n)
                    v.tensor_tensor(br[:, :, 0:3, 0:half], rp[:, 0], rp[:, 1], ALU.subtract)
                    wait(v.tensor_tensor(br[:, :, 0:3, half:], rp[:, 2], rp[:, 3], ALU.add))
                    v.tensor_copy(br[:, :, 3, :], br[:, :, 2, :]).then_inc(S["br"], 1)
                    wait(v.tensor_tensor(sqb[:, :, 0:2, :], br[:, :, 0:2, :], br[:, :, 2:3, :].to_broadcast(
                        [P, NT, 2, N_STATE]), ALU.mult))
                    mark(v.tensor_reduce(gd[:, :, :], sqb[:, :, 0:2, :], AX, ALU.add))
                    dve.wait_ge(S["bt_ps"], 1)
                    v.tensor_copy(bt[:, 0:2], ps[:, 4, :].rearrange("p (t c m) -> p t c m", t=2, c=2))
                    v.tensor_copy(bt[:, 2:4], ps[:, 5, :].rearrange("p (t c m) -> p t c m", t=2, c=2)).then_inc(S["bt"], 1)
                    dve.wait_ge(S["g_ps"], 1)
                    for k in range(2):
                        for u in range(2):
                            ins = v.tensor_tensor(
                                gm[:, k, :, u, :],
                                ps[:, 6 + u, :].rearrange("p (a m) -> p a m", a=4),
                                w["masks"][:, k:k + 1, :].to_broadcast([P, 4, P]), ALU.mult)
                            ins.then_inc(S["g"], 1)
                    gam_done = done[0]
                    dve.wait_ge(S["dve"], gam_done)
                    dve.wait_ge(S["silu"], 2 * NT)

                    def variants(t):
                        if t >= 2:
                            dve.wait_ge(S["ymm"], t - 1)
                            dve.wait_ge(S["st_mm"], t - 1)
                        for c in (0, 1, 2, 3, 4, 5):
                            if c == REF_END and t == NT - 1:
                                continue
                            ins = v.tensor_tensor(
                                xv[:, t % 2, c].rearrange("p h r q -> p h (r q)"),
                                xr[:, t].rearrange("p h r q -> p h (r q)"),
                                coef[:, c, t, :].rearrange("p (h o) -> p h o", o=1).to_broadcast(
                                    [P, M_HEADS, R * HP]), ALU.mult)
                        ins.then_inc(S["xv"], 1)

                    def outputs(t):
                        bank = 2 * (t % 2)
                        pt = part[:, t % 2]

                        def row(c):
                            return dec[:, c, t, :].rearrange("p (h o) -> p h o", o=1).to_broadcast([P, M_HEADS, HP])

                        def mmo(k, o):
                            return ps[:, k, o:o + 256].rearrange("p (h q) -> p h q", q=HP)
                        dve.wait_ge(S["ymm"], t + 1)
                        v.tensor_tensor(pt[:, 0], mmo(bank, 0), row(8), ALU.mult)
                        ins = v.tensor_tensor(pt[:, 1], mmo(bank, 256), row(IN_BLOCK), ALU.mult)
                        if t < NT - 1:
                            dve.wait_ge(S["st_mm"], t + 1)
                        if t:
                            ins = v.tensor_tensor(pt[:, 2], mmo(bank + 1, 0), row(FROM_START), ALU.mult)
                        ins.then_inc(S["y_read"], 1)
                        if t < NT - 1:
                            new = ps[0:N_STATE, bank + 1, 256:512].rearrange("p (h q) -> p h q", q=HP)
                            if t == 0:
                                v.tensor_copy(state[:, :, :], new).then_inc(S["state"], 1)
                            else:
                                dve.wait_ge(S["state"], t)
                                wait(v.tensor_tensor(part[0:N_STATE, t % 2, 3], state[:, :, :],
                                                     dec[0:N_STATE, WHOLE, t, :].rearrange(
                                                         "p (h o) -> p h o", o=1).to_broadcast([N_STATE, M_HEADS, HP]),
                                                     ALU.mult))
                                v.tensor_tensor(state[:, :, :], part[0:N_STATE, t % 2, 3], new,
                                                ALU.add).then_inc(S["state"], 1)
                        dve.wait_ge(S["y_read"], t + 1)
                        wait(v.tensor_tensor(pt[:, 1], pt[:, 0], pt[:, 1], ALU.add))
                        if t:
                            wait(v.tensor_tensor(pt[:, 1], pt[:, 1], pt[:, 2], ALU.add))
                        for r in range(R):
                            wait(v.scalar_tensor_tensor(pt[:, r],
                                                        xv[:, t % 2, 5, :, r, :], gd[:, t, r:r + 1],
                                                        pt[:, 1 - r], ALU.mult, ALU.add))
                        v.tensor_tensor(yz[:, t, :], pt[:, 1].rearrange("p h q -> p (h q)"), zs[:, t, :],
                                        ALU.mult).then_inc(S["yz"], 1)
                        dve.wait_ge(S["yz"], t + 1)
                        mark(v.tensor_tensor_reduce(yy[:, t, :], yz[:, t, :], yz[:, t, :], 1.0, 0.0, ALU.mult, ALU.add,
                                                    rms[:, 0, t:t + 1]))

                    variants(0)
                    for t in range(NT):
                        if t + 1 < NT:
                            variants(t + 1)
                        outputs(t)
                    dve.wait_ge(S["dve"], done[0])
                    v.tensor_scalar(rms[:, 0, :], rms[:, 0, :], 1.0 / D_INNER, RMS_EPS, ALU.mult, ALU.add).then_inc(S["ms"], 1)
                    dve.wait_ge(S["yzT_ps"], 1)
                    v.tensor_copy(yzT[:, 0:2], ps[:, 4, :].rearrange("p (t c m) -> p t c m", t=2, c=2))
                    v.tensor_copy(yzT[:, 2:4], ps[:, 5, :].rearrange("p (t c m) -> p t c m", t=2, c=2)).then_inc(S["yzT"], 1)
                    dve.wait_ge(S["rms"], 1)
                    wait(v.reciprocal(rms[:, 0, :], rms[:, 1, :]))
                    dve.wait_ge(S["wo"], 1)
                    for t in range(NT):
                        v.scalar_tensor_tensor(y[:, t, :], ps[:, 6, P * t:P * t + P], rms[:, 0, t:t + 1], y[:, t, :],
                                               ALU.mult, ALU.add).then_inc(S["y"], 1)
                    dve.wait_ge(S["y"], 1 + NT)
                    layernorm(y, 3)
                    dve.wait_ge(S["gate"], 1)
                    v.tensor_tensor(gl[:, :, :], ps[:, 7, 0:NT * EXPERTS].rearrange(
                        "p (t e) -> p t e", t=NT), w["gate_b"][:, :, :], ALU.add).then_inc(S["gate_read"], 1)
                    dve.wait_ge(S["gate_read"], 1)
                    count_choices(v, dve, S["dve"], mark, gl, g8, gix, gif, onehot, w, cnt_acc)

                @block.scalar
                def _(act):
                    a = nc.scalar

                    def sqrt_of_var(lap):
                        act.wait_ge(S["var"], lap)
                        a.activation(sd[:, :, 1], sd[:, :, 0], ACT.Sqrt).then_inc(S["sd"], 1)
                    sqrt_of_var(1)
                    if last:
                        return
                    sqrt_of_var(2)
                    for t in range(NT):
                        s0 = 3 * (t % 2)
                        act.wait_ge(S["proj"], t + 1)
                        a.activation(xr[:, t].rearrange("p h r q -> p (h r q)"), ps[:, s0, :], ACT.Silu).then_inc(S["silu"], 1)
                        a.activation(zs[:, t, :], ps[:, s0 + 1, 0:256], ACT.Silu).then_inc(S["silu"], 1)
                    act.wait_ge(S["proj_v"], NT)
                    a.activation(lam[:, :, :], dl[:, :, 1, :], ACT.Exp, scale=-1.0)
                    act.wait_ge(S["u"], 1)
                    a.activation(dt[:, :, :], t_dt[:, :, :], ACT.Exp).then_inc(S["e1"], 1)
                    act.wait_ge(S["e1"], 1)
                    a.activation(dt[:, :, :], dt[:, :, :], ACT.Ln, bias=1.0).then_inc(S["e2"], 1)
                    act.wait_ge(S["sum_ps"], 1)
                    act.wait_ge(S["sum_v"], 1)
                    a.activation(dec[:, 0], mid[:, :, :], ACT.Exp)
                    a.activation(dec[:, 8], mid[:, :, :], ACT.Exp, scale=-1.0)
                    a.activation(dec[:, 1:4].rearrange("p c t h -> p (c t h)"), ps[:, 0, 128:512], ACT.Exp)
                    a.activation(dec[:, 4:8].rearrange("p c t h -> p (c t h)"), ps[:, 1, :], ACT.Exp).then_inc(S["dec"], 1)
                    act.wait_ge(S["rms12"], 1)
                    a.activation(rs12[:, 1, :], rs12[:, 0, :], ACT.Sqrt).then_inc(S["e4"], 1)
                    act.wait_ge(S["ang_r"], 1)
                    a.activation(sc[:, :].rearrange("p c t h -> p (c t h)"),
                                 ang[:, :].rearrange("p c t h -> p (c t h)"), ACT.Sin).then_inc(S["sin"], 1)
                    act.wait_ge(S["ms"], 1)
                    a.activation(rms[:, 1, :], rms[:, 0, :], ACT.Sqrt).then_inc(S["rms"], 1)
                    sqrt_of_var(3)

                @block.tensor
                def _(pe):
                    mm = nc.tensor.matmul

                    def transposes(lap):
                        pe.wait_ge(S["xn"], NT * lap)
                        for t in range(NT):
                            ins = nc.tensor.transpose(ps[:, 4, P * t:P * t + P], xn[:, t, :], w["ident"][:, :])
                        ins.then_inc(S["xT"], 1)
                        pe.wait_ge(S["xnT"], lap)

                    transposes(1)
                    for e in range(EXPERTS):
                        if e >= 4:
                            pe.wait_ge(S["ex_read"], e - 3)
                        mm(ps[:, e % 4, :], ew_s[:, e, :], xnT[:, :], start=True, stop=True).then_inc(S["ex"], 1)
                    pe.wait_ge(S["ex_read"], EXPERTS)
                    for t in range(NT):
                        ins = nc.tensor.transpose(ps[:, 5, P * t:P * t + P], acc[:, 1, P * t:P * t + P], w["ident"][:, :])
                    ins.then_inc(S["accT"], 1)
                    if last:
                        return
                    transposes(2)
                    for t in range(NT):
                        s0 = 3 * (t % 2)
                        if t >= 2:
                            pe.wait_ge(S["silu"], 2 * (t - 1))
                            pe.wait_ge(S["proj_v"], t - 1)
                        if t == 1:
                            pe.wait_ge(S["y"], 1)
                        xs = xnT[:, P * t:P * t + P]
                        mm(ps[:, s0, :], xs, w["w_in"][:, 0:512], start=True, stop=True)
                        mm(ps[:, s0 + 1, :], xs, w["w_in"][:, 512:1024], start=True, stop=True)
                        mm(ps[:, s0 + 2, 0:32], xs, w["w_in"][:, 1024:1056], start=True, stop=True).then_inc(S["proj"], 1)
                    pe.wait_ge(S["e3"], 1)
                    mm(ps[:, 7, 0:128], w["moves"][:, 0, :], th[:, :, :], start=True, stop=False, skip_group_check=True)
                    for s in range(1, NT):
                        ins = mm(ps[:, 7, 32 * s:128], w["moves"][:, 1, :], th[:, 0:NT - s, :], start=False,
                                 stop=s == NT - 1, skip_group_check=True)
                    ins.then_inc(S["ang_ps"], 1)
                    pe.wait_ge(S["silu"], 2 * NT)
                    pe.wait_ge(S["proj_v"], NT)
                    for c in range(8):
                        ins = mm(ps[:, c // 4, P * (c % 4):P * (c % 4) + P], w["sums"][:, c, :], lda[:, :, :],
                                 start=True, stop=True)
                    ins.then_inc(S["sum_ps"], 1)
                    pe.wait_ge(S["beta"], 1)
                    pe.wait_ge(S["ang_r"], 1)
                    mm(ps[:, 7, 128:256], w["moves"][:, 2, :], bet[:, :, :], start=True, stop=False, skip_group_check=True)
                    mm(ps[:, 7, 128:224], w["moves"][:, 3, :], bet[:, 1:NT, :], start=False, stop=True,
                       skip_group_check=True).then_inc(S["beta_ps"], 1)
                    pe.wait_ge(S["br"], 1)
                    for t in range(NT):
                        for c in range(2):
                            ins = nc.tensor.transpose(ps[:, 4 + t // 2, 256 * (t % 2) + P * c:256 * (t % 2) + P * c + P],
                                                      br[:, t, 2 * c:2 * c + 2, :].rearrange("p c n -> p (c n)"),
                                                      w["ident"][:, :])
                    ins.then_inc(S["bt_ps"], 1)
                    pe.wait_ge(S["bt"], 1)
                    pe.wait_ge(S["dec"], 1)
                    for t in range(NT):
                        for r in range(R):
                            n = slice(N_STATE * r, N_STATE * r + N_STATE)
                            ins = mm(ps[:, 6 + r, P * t:P * t + P], bt[n, t, 0, :], bt[n, t, 1, :], start=True, stop=True)
                    ins.then_inc(S["g_ps"], 1)
                    pe.wait_ge(S["g"], 4)
                    for t in range(NT):
                        bank = 2 * (t % 2)
                        pe.wait_ge(S["xv"], t + 1)
                        if t >= 2:
                            pe.wait_ge(S["state"], t - 1)
                            pe.wait_ge(S["y_read"], t - 1)
                        for r in range(R):
                            mm(ps[:, bank, 0:256], gm[:, 0, t, r, :], xv[:, t % 2, 0, :, r, :],
                               start=r == 0, stop=r == R - 1, skip_group_check=True)
                        for blk in range(4):
                            for r in range(R):
                                rows = slice(BLK * blk, BLK * blk + BLK)
                                ins = mm(ps[rows, bank, 256:512], gm[:, 1, t, r, rows], xv[:, t % 2, max(blk, 1), :, r, :],
                                         start=r == 0, stop=r == R - 1, skip_group_check=True)
                        if t:
                            pe.wait_ge(S["state"], t)
                            ins = mm(ps[:, bank + 1, 0:256], bt[0:N_STATE, t, 1, :], state[:, :, :],
                                     start=True, stop=True, skip_group_check=True)
                        ins.then_inc(S["ymm"], 1)
                        if t < NT - 1:
                            for r in range(R):
                                ins = mm(ps[0:N_STATE, bank + 1, 256:512], br[:, t, r, :], xv[:, t % 2, REF_END, :, r, :],
                                         start=r == 0, stop=r == R - 1, skip_group_check=True)
                            ins.then_inc(S["st_mm"], 1)
                    pe.wait_ge(S["yz"], NT)
                    for t in range(NT):
                        for c in range(2):
                            o = 256 * (t % 2) + P * c
                            ins = nc.tensor.transpose(ps[:, 4 + t // 2, o:o + P], yz[:, t, P * c:P * c + P], w["ident"][:, :])
                    ins.then_inc(S["yzT_ps"], 1)
                    pe.wait_ge(S["yzT"], 1)
                    for t in range(NT):
                        for c in range(2):
                            ins = mm(ps[:, 6, P * t:P * t + P], yzT[:, t, c, :], w["w_out"][:, c, :],
                                     start=c == 0, stop=c == 1)
                    ins.then_inc(S["wo"], 1)
                    transposes(3)
                    for t in range(NT):
                        ins = mm(ps[:, 7, EXPERTS * t:EXPERTS * t + EXPERTS], xnT[:, P * t:P * t + P],
                                 w["gwT"][:, :], start=True, stop=True)
                    ins.then_inc(S["gate"], 1)
            nc.gpsimd.sem_clear(range(nums[0], nums[-1] + 1))
            nc.all_engine_barrier(sem_only=True)


INS = ["q", "wq", "wk", "wv", "wo", "angles", "gwT", "gate_b", "rope", "ident", "iota",
       "w_in", "w_out", "a_log", "dt_bias", "bc_bias", "ew", "eb", "sums", "moves", "masks"]


def build(nc, ins, out):
    x3 = nc.dram_tensor("x3", (BATCH, SEQ, D), F32, kind="Internal").ap()
    x5 = nc.dram_tensor("x5", (BATCH, SEQ, D), F32, kind="Internal").ap()
    with ExitStack() as ctx:
        sb = lambda name, shape: ctx.enter_context(nc.sbuf_tensor(name, shape, F32))
        cnt_acc = sb("cnt_acc", [P, NT * TOPK * EXPERTS])
        with ExitStack() as layer0:
            w = load_layer0(nc, layer0, ins, cnt_acc)
            attention_phase(nc, ins["q"], x3, w, cnt_acc)
        w = load_layer1(nc, ctx, ins)
        ew_s, negb, sumb = sb("ew_s", [P, EXPERTS, D]), sb("negb", [P, EXPERTS]), sb("sumb", [P, 1])
        expert_weights(nc, "e1_", w, cnt_acc, ew_s, negb, sumb)
        state_phase(nc, x3, x5, w, ew_s, negb, sumb, cnt_acc, False)
        expert_weights(nc, "e2_", w, cnt_acc, ew_s, negb, sumb)
        state_phase(nc, x5, out, w, ew_s, negb, sumb, cnt_acc, True)


def kernel(**inputs):
    import numpy as _np
    import concourse.bacc as _bacc
    from concourse import mybir as _mybir
    from concourse.bass_utils import run_bass_kernel_spmd as _run

    nc = _bacc.Bacc("TRN2", target_bir_lowering=False, num_devices=1)
    given = {**layout_p1(inputs), **layout_p2(inputs), **consts_p1(), **consts_p2()}
    arrays, aps = {}, {}
    for name in INS:
        a = _np.ascontiguousarray(given[name])
        arrays[f"in_{name}"] = a
        aps[name] = nc.dram_tensor(f"in_{name}", a.shape, _mybir.dt.from_np(a.dtype), kind="ExternalInput").ap()
    out = nc.dram_tensor("out_0", (BATCH, SEQ, D), F32, kind="ExternalOutput").ap()
    build(nc, aps, out)
    r = _run(nc, [arrays], core_ids=[0])
    return r.results[0]["out_0"]
```

```python
from contextlib import ExitStack

import numpy as np
import concourse.bass as bass
from concourse import mybir

F32 = mybir.dt.float32
F16 = mybir.dt.float16
U32 = mybir.dt.uint32
ALU = mybir.AluOpType
ACT = mybir.ActivationFunctionType
AX = mybir.AxisListType.X

P = 128
BATCH, SEQ, D = 16, 512, 128
NT = SEQ // P
HEADS, KVD, DH = 16, 512, 32
NG = 4
EXPERTS, TOPK = 8, 2
LN_EPS = 1e-5
STK = 3 * DH + 1
ATT_SCALE = float((64 / 16) ** -0.5)


def rope_tables():
    pos = np.arange(1, SEQ + 1, dtype=np.float32)
    def angles(dim):
        th = (np.float32(1.0) / np.power(np.float32(1250), np.arange(0, dim, 2, dtype=np.float32) / np.float32(dim))).astype(np.float32)
        return (pos[:, None] * th[None, :]).astype(np.float32).T.astype(np.float64)
    aq = angles(2 * KVD)
    ak = np.repeat(angles(KVD), 2, axis=0)
    sign = np.where(np.arange(KVD) % 2 == 0, -1.0, 1.0)[:, None]
    t = np.stack([np.cos(aq) + np.sin(aq), np.cos(aq) - np.sin(aq), np.cos(ak), sign * np.sin(ak)])
    return t.reshape(4, NG, P, SEQ).transpose(2, 0, 1, 3).astype(np.float32).copy()


def top_two(v, dve, sem, mark, gl, g8, gix, gif):
    for t in range(NT):
        n = mark(v.max(g8[:, t, :], gl[:, t, :]))
    dve.wait_ge(sem, n)
    for t in range(NT):
        n = mark(v.max_index(gix[:, t, :], g8[:, t, :], gl[:, t, :]))
    dve.wait_ge(sem, n)
    dve.wait_ge(sem, mark(v.tensor_copy(gif[:, :, :], gix[:, :, 0:TOPK])))


def count_choices(v, dve, sem, mark, gif, onehot, w, cnt_acc):
    for k in range(TOPK):
        n = mark(v.tensor_tensor(onehot[:, :, k, :], w["iota"][:, :, :],
                                 gif[:, :, k:k + 1].to_broadcast([P, NT, EXPERTS]), ALU.is_equal))
    dve.wait_ge(sem, n)
    v.tensor_tensor(cnt_acc[:, :], cnt_acc[:, :], onehot[:, :, :, :].rearrange("p t k e -> p (t k e)"), ALU.add)


def attention_phase(nc, q_in, x3_out, w, cnt_acc):
    with ExitStack() as ctx:
        def sb(name, shape, dt=F32):
            return ctx.enter_context(nc.sbuf_tensor(name, shape, dt))

        x8 = sb("x8", [P, 8, D])
        ynew = sb("ynew", [P, 2, NT, D])
        yold = sb("yold", [P, NT, D])
        xkeep = sb("xkeep", [P, 2, NT, D])
        stats = sb("stats", [P, 8, 6])
        mv = sb("mv", [P, 8, 2])
        veps = sb("veps", [P, 8])
        rstd = sb("rstd", [P, 8])
        xn = sb("xn", [P, 8, D])
        xnTn = sb("xnTn", [P, 2, SEQ])
        xnTo = sb("xnTo", [P, SEQ])
        sq = sb("sq", [P, 2, 2, 2, D])
        hh = sb("hh", [P, 8, D])
        t1 = sb("t1", [P, SEQ])
        t2 = sb("t2", [P, SEQ])
        rot = sb("rot", [P, 2, SEQ])
        hi = sb("hi", [P, 2, 2, NG, SEQ], F16)
        lo = sb("lo", [P, 2, 2, NG, SEQ], F16)
        qst = sb("qst", [STK, HEADS, SEQ], F16)
        kst = sb("kst", [STK, HEADS, SEQ], F16)
        vt = sb("vt", [P, NT, KVD])
        pr = sb("pr", [P, 2, NT, SEQ])
        mS = sb("mS", [P, NT, HEADS])
        nm = sb("nm", [NG, NG, SEQ], F16)
        den = sb("den", [P, SEQ])
        denT = sb("denT", [P, SEQ])
        inv = sb("inv", [P, SEQ // 32])
        rec = sb("rec", [P, SEQ])
        oT = sb("oT", [P, NG, SEQ])
        gl = sb("gl", [P, NT, EXPERTS])
        g8 = sb("g8", [P, NT, 8])
        gix = sb("gix", [P, NT, 8], U32)
        gif = sb("gif", [P, NT, TOPK])
        onehot = sb("onehot", [P, NT, TOPK, EXPERTS])
        ps = ctx.enter_context(nc.psum_tensor("ps", [P, 8, 512], F32))

        names = ("x_in", "var", "rstd", "xn", "xT", "xnT", "ff", "sq", "ss", "h", "y", "pair", "pair_free",
                 "rot", "hi", "lo", "gate", "gate_read", "st", "exp", "s", "s_read", "stacked", "mrow",
                 "mrow_sent", "pv", "den", "norm", "wo", "x2", "v", "v_read_a", "v_read_v", "dve", "x_out")
        S = {n: ctx.enter_context(nc.semaphore("a_" + n)) for n in names}
        nums = sorted(s.num for s in S.values())
        assert nums[-1] - nums[0] + 1 == len(nums)

        jobs = []
        for s in range(HEADS + 1):
            for t in range(NT):
                if s < HEADS:
                    jobs.append(("tile", 4 * s + t))
                if t == 0 and s and s % NG == 0:
                    jobs.append(("guard", s // NG - 1))
        job_of = {j: n for n, j in enumerate(jobs)}
        AT = {"stats1": 0, "aggr1": 2, "xn1": 5, "turn1": 8, "evac1": 9, "ffn": 11, "squares": 13,
              "ffn_b": 15, "squares_b": 17, "sqrt": 20, "resid": 22, "stats2": 24, "aggr2": 26,
              "xn2": 29, "turn2": 32, "evac2": 33, "gate": 34, "gate_in": 35, "gate_top": 36, "gate_count": 37}
        PROJ0 = 37
        project_at = {PROJ0 + (26 * m) // (4 * NG): m for m in range(4 * NG)}
        product_at = {q + 1: m for q, m in project_at.items()}
        high_at = {q + 2: m // 2 for q, m in project_at.items() if m % 2}

        def iteration(i, par, new, mid, att, old, prefetch):
            halves = ([0] if new else []) + ([1] if old else [])
            tiles = [NT * h + t for h in halves for t in range(NT)]
            nt, nh = len(tiles), len(halves)
            a0, b0 = (tiles[0], tiles[-1] + 1) if tiles else (0, 0)

            def after_ffn(t):
                return ynew[:, par, t, :] if t < NT else yold[:, t - NT, :]

            def xnT_tile(t):
                src = xnTn[:, par] if t < NT else xnTo
                return src[:, P * (t % NT):P * (t % NT) + P]

            with nc.Block(no_gpsimd_drain=True) as block:
                @block.sync
                def _(sp):
                    if mid:
                        for j in range(NG):
                            if att:
                                sp.wait_ge(S["st"], 16 * (j + 1))
                            r = slice(DH * j, DH * j + DH)
                            q_hi, q_lo = hi[r, 1 - par, 0], lo[r, 1 - par, 0]
                            k_hi, k_lo = hi[r, 1 - par, 1], lo[r, 1 - par, 1]
                            for dst, src, row in ((qst, q_hi, 0), (qst, q_lo, 1), (qst, q_hi, 2),
                                                  (kst, k_hi, 0), (kst, k_hi, 1), (kst, k_lo, 2)):
                                sp.dma_start(dst[DH * row:DH * row + DH, NG * j:NG * j + NG, :],
                                             src).then_inc(S["stacked"], 16)
                            sp.wait_ge(S["mrow"], j + 1)
                            sp.dma_start(qst[3 * DH:STK, NG * j:NG * j + NG, :],
                                         nm[:, j, :]).then_inc(S["mrow_sent"], 16)
                    if new or old:
                        sp.wait_ge(S["y"], nh)
                    if prefetch:
                        sp.dma_start(x8[:, 0:NT, :], q_in[bass.ds(i + 1, 1)].rearrange(
                            "b (t p) d -> p (b t) d", p=P)).then_inc(S["x_in"], 16)
                    if old:
                        sp.dma_start(x3_out[bass.ds(i - 3, 1)].rearrange("b (t p) d -> p (b t) d", p=P),
                                     yold[:, :, :]).then_inc(S["x_out"], 16)
                        sp.wait_ge(S["x_out"], 16)
                    if prefetch:
                        sp.wait_ge(S["x_in"], 16)
                    if mid:
                        sp.wait_ge(S["stacked"], 16 * 6 * NG)
                        sp.wait_ge(S["mrow_sent"], 16 * NG)

                @block.vector
                def _(dve):
                    v = nc.vector
                    done = [0]

                    def mark(ins):
                        done[0] += 1
                        ins.then_inc(S["dve"], 1)
                        return done[0]

                    def stats_of(src, part):
                        for t in tiles[nt // 2 * part:nt // 2 * (part + 1)]:
                            stats_done[0] = mark(v.bn_stats(stats[:, t, :], src(t)))

                    def aggregate():
                        dve.wait_ge(S["dve"], stats_done[0])
                        for t in tiles:
                            n = mark(v.bn_aggr(mv[:, t, :], stats[:, t, :]))
                        dve.wait_ge(S["dve"], n)
                        v.tensor_scalar(veps[:, a0:b0], mv[:, a0:b0, 1], LN_EPS, None, ALU.add).then_inc(S["var"], 1)

                    def normalise(src, lap, part):
                        if part == 0:
                            dve.wait_ge(S["rstd"], lap)
                            if lap == 2:
                                dve.wait_ge(S["xT"], 1)
                        for t in tiles[3 * part:3 * part + 3]:
                            ins = v.tensor_scalar(xn[:, t, :], src(t), mv[:, t, 0:1], rstd[:, t:t + 1],
                                                  ALU.subtract, ALU.mult)
                            if t == tiles[-1]:
                                ins.then_inc(S["xn"], 1)

                    def residual(hf):
                        dve.wait_ge(S["h"], 1)
                        dst = ynew[:, par] if hf == 0 else yold[:, :, :]
                        v.tensor_tensor(dst, x8[:, NT * hf:NT * hf + NT, :], hh[:, NT * hf:NT * hf + NT, :],
                                        ALU.add).then_inc(S["y"], 1)

                    def gate_in():
                        dve.wait_ge(S["gate"], 1)
                        v.tensor_tensor(gl[:, :, :], ps[:, 4, 0:NT * EXPERTS].rearrange(
                            "p (t e) -> p t e", t=NT), w["gate_b"][:, :, :], ALU.add).then_inc(S["gate_read"], 1)

                    def product(m):
                        p, c = m // 2, m % 2
                        kq, g = p // NG, p % NG
                        dve.wait_ge(S["pair"], m + 1)
                        if c == 0:
                            if p:
                                dve.wait_ge(S["rot"], p)
                            t1_done[0] = mark(v.tensor_tensor(t1[:, :], ps[:, 4, :], w["rope"][:, 2 * kq, g, :],
                                                              ALU.mult))
                            return
                        v.tensor_tensor(t2[:, :], ps[:, 5, :], w["rope"][:, 2 * kq + 1, g, :],
                                        ALU.mult).then_inc(S["pair_free"], 1)
                        dve.wait_ge(S["pair_free"], p + 1)
                        dve.wait_ge(S["dve"], t1_done[0])
                        if p >= 2:
                            dve.wait_ge(S["lo"], p - 1)
                        v.tensor_tensor(rot[:, p % 2, :], t1[:, :], t2[:, :], ALU.add).then_inc(S["rot"], 1)

                    def maximum(s, t):
                        n = job_of["tile", 4 * s + t]
                        dve.wait_ge(S["s"], n + 1)
                        v.tensor_reduce(mS[:, t, s:s + 1], ps[:, 2 + n % 2, :], AX, ALU.max).then_inc(S["s_read"], 1)

                    def guard_row(j):
                        n = job_of["guard", j]
                        dve.wait_ge(S["s"], n + 1)
                        v.tensor_scalar(nm[:, j, :], ps[0:NG, 2 + n % 2, :], -1.0, None, ALU.mult).then_inc(S["mrow"], 1)

                    def divide(j, part):
                        if part == 0:
                            dve.wait_ge(S["den"], j + 1)
                            dve.wait_ge(S["dve"], mark(v.transpose(denT[:, :], den[:, :])))
                            div_done[0] = mark(v.reciprocal(inv[:, :], denT[:, 0:SEQ:32]))
                        if part == 1:
                            dve.wait_ge(S["dve"], div_done[0])
                            dve.wait_ge(S["dve"], mark(v.tensor_copy(
                                denT[:, :].rearrange("p (b i) -> p b i", i=32),
                                inv[:, :].rearrange("p (b o) -> p b o", o=1).to_broadcast([P, SEQ // 32, 32]))))
                            div_done[0] = mark(v.transpose(rec[:, :], denT[:, :]))
                        if part == 2:
                            dve.wait_ge(S["dve"], div_done[0])
                            v.tensor_tensor(oT[:, j, :], oT[:, j, :], rec[:, :], ALU.mult).then_inc(S["norm"], 1)

                    stats_done, t1_done, div_done = [0], [0], [0]
                    for q in range(NT * HEADS + 2):
                        s, t = q // NT, q % NT
                        if mid and s < HEADS:
                            maximum(s, t)
                        if mid and t == 0 and s and s % NG == 0:
                            guard_row(s // NG - 1)
                        if att and s % NG == 1 and s > NG and t < 3:
                            divide(s // NG - 1, t)
                        if new and q in product_at:
                            product(product_at[q])
                        if new or old:
                            for part in range(3):
                                if part < 2 and q == AT["stats1"] + part:
                                    stats_of(lambda t: x8[:, t, :], part)
                                if q == AT["xn1"] + part:
                                    normalise(lambda t: x8[:, t, :], 1, part)
                                if part < 2 and q == AT["stats2"] + part:
                                    dve.wait_ge(S["y"], nh)
                                    stats_of(after_ffn, part)
                                if q == AT["xn2"] + part:
                                    normalise(after_ffn, 2, part)
                            if q in (AT["aggr1"], AT["aggr2"]):
                                aggregate()
                            for k, hf in enumerate(halves):
                                if q == AT["resid"] + k:
                                    residual(hf)
                        if old:
                            if q == AT["gate_in"]:
                                gate_in()
                            if q == AT["gate_top"]:
                                dve.wait_ge(S["gate_read"], 1)
                                top_two(v, dve, S["dve"], mark, gl, g8, gix, gif)
                            if q == AT["gate_count"]:
                                count_choices(v, dve, S["dve"], mark, gif, onehot, w, cnt_acc)
                    if att:
                        for part in range(3):
                            divide(NG - 1, part)
                    if mid:
                        for t in (1, 3):
                            dve.wait_ge(S["v"], t + 1)
                            v.tensor_copy(vt[:, t, :], ps[:, t, :]).then_inc(S["v_read_v"], 1)
                    if att:
                        dve.wait_ge(S["wo"], 1)
                        v.tensor_tensor(x8[:, NT:2 * NT, :], xkeep[:, par], ps[:, 4, :].rearrange(
                            "p (t d) -> p t d", t=NT), ALU.add).then_inc(S["x2"], 1)

                @block.scalar
                def _(act):
                    a = nc.scalar

                    def transposed(lap):
                        act.wait_ge(S["xT"], lap)
                        for hf in halves:
                            dst = xnTn[:, par] if hf == 0 else xnTo[:, :]
                            ins = a.copy(dst, ps[:, 4 + hf, :])
                        ins.then_inc(S["xnT"], 1)

                    def squares(k):
                        act.wait_ge(S["ff"], k + 1)
                        if k >= 2:
                            act.wait_ge(S["ss"], k - 1)
                        a.activation(sq[:, k % 2].rearrange("p t c d -> p (t c d)"), ps[:, 4 + k % 2, :],
                                     ACT.Square).then_inc(S["sq"], 1)

                    def high(p):
                        act.wait_ge(S["rot"], p + 1)
                        a.copy(hi[:, par, p // NG, p % NG, :], rot[:, p % 2, :]).then_inc(S["hi"], 1)

                    def denominators(j):
                        act.wait_ge(S["pv"], NG * (j + 1))
                        if j:
                            act.wait_ge(S["norm"], j)
                        a.copy(oT[:, j, :], ps[:, 6, :])
                        a.copy(den[:, :], ps[:, 7, :]).then_inc(S["den"], 1)

                    for q in range(NT * HEADS + 3):
                        s, g = q // NG, q % NG
                        if att and s < HEADS:
                            if s >= 2 and g == 0:
                                act.wait_ge(S["pv"], s - 1)
                            act.wait_ge(S["st"], q + 1)
                            a.activation(pr[:, s % 2, g, :], ps[:, g % 2, :], ACT.Exp,
                                         scale=ATT_SCALE).then_inc(S["exp"], 1)
                        if att and s and s < HEADS and s % NG == 0 and g == 3:
                            denominators(s // NG - 1)
                        if new or old:
                            if q == AT["evac1"]:
                                transposed(1)
                            if q == AT["squares"]:
                                for k in range(min(2, nt // 2)):
                                    squares(k)
                            if q == AT["squares_b"]:
                                for k in range(2, nt // 2):
                                    squares(k)
                            if q == AT["sqrt"]:
                                act.wait_ge(S["ss"], nt // 2)
                                a.activation(hh[:, a0:b0, :], hh[:, a0:b0, :], ACT.Sqrt, scale=0.25).then_inc(S["h"], 1)
                            if q == AT["evac2"]:
                                transposed(2)
                        if new and q in high_at:
                            high(high_at[q])
                    if att:
                        denominators(NG - 1)
                    if mid:
                        for t in (0, 2):
                            act.wait_ge(S["v"], t + 1)
                            a.copy(vt[:, t, :], ps[:, t, :]).then_inc(S["v_read_a"], 1)

                @block.gpsimd
                def _(pool):
                    g = nc.gpsimd

                    def reciprocal_deviations(lap):
                        pool.wait_ge(S["var"], lap)
                        g.tensor_tensor(rstd[:, a0:b0], veps[:, a0:b0], w["minus_half"][:, a0:b0],
                                        ALU.pow).then_inc(S["rstd"], 1)

                    if new or old:
                        reciprocal_deviations(1)
                        for k in range(nt // 2):
                            pool.wait_ge(S["sq"], k + 1)
                            t = tiles[2 * k]
                            g.tensor_tensor(hh[:, t:t + 2, :], sq[:, k % 2, :, 0, :], sq[:, k % 2, :, 1, :],
                                            ALU.add).then_inc(S["ss"], 1)
                        reciprocal_deviations(2)
                    if mid:
                        g.tensor_copy(xkeep[:, 1 - par], ynew[:, 1 - par])
                    if new:
                        for p in range(2 * NG):
                            pool.wait_ge(S["hi"], p + 1)
                            g.tensor_tensor(lo[:, par, p // NG, p % NG, :], rot[:, p % 2, :],
                                            hi[:, par, p // NG, p % NG, :], ALU.subtract).then_inc(S["lo"], 1)
                        pool.wait_ge(S["lo"], 2 * NG)

                @block.tensor
                def _(pe):
                    mm = nc.tensor.matmul

                    def transposes(lap):
                        pe.wait_ge(S["xn"], lap)
                        if lap == 2:
                            pe.wait_ge(S["sq"], nt // 2)
                        for hf in halves:
                            for t in range(NT):
                                ins = nc.tensor.transpose(ps[:, 4 + hf, P * t:P * t + P], xn[:, NT * hf + t, :],
                                                          w["ident"][:, :])
                        ins.then_inc(S["xT"], 1)

                    def ffn(k):
                        if k < 2:
                            pe.wait_ge(S["xnT"], 1)
                        else:
                            pe.wait_ge(S["sq"], k - 1)
                        for u in range(2):
                            ins = mm(ps[:, 4 + k % 2, 256 * u:256 * u + 256], xnT_tile(tiles[2 * k + u]),
                                     w["csT"][:, :], start=True, stop=True)
                        ins.then_inc(S["ff"], 1)

                    def gate():
                        pe.wait_ge(S["xnT"], 2)
                        for t in range(NT):
                            ins = mm(ps[:, 4, EXPERTS * t:EXPERTS * t + EXPERTS], xnT_tile(NT + t),
                                     w["gwT"][:, :], start=True, stop=True)
                        ins.then_inc(S["gate"], 1)

                    def project(p, c):
                        kq, g = p // NG, p % NG
                        if c == 0:
                            if p == 0:
                                pe.wait_ge(S["xnT"], 2)
                                if old:
                                    pe.wait_ge(S["gate_read"], 1)
                            else:
                                pe.wait_ge(S["pair_free"], p)
                        wt = w["wq"][:, g, c, :] if kq == 0 else w["wk"][:, c, P * g:P * g + P]
                        mm(ps[:, 4 + c, :], wt, xnTn[:, par], start=True, stop=True).then_inc(S["pair"], 1)

                    def shifted_scores(s, g):
                        j, kt = s // NT, s % NT
                        n = NG * s + g
                        if n >= 2:
                            pe.wait_ge(S["exp"], n - 1)
                        mm(ps[:, g % 2, :], kst[:, NG * j + g, P * kt:P * kt + P], qst[:, NG * j + g, :],
                           start=True, stop=True).then_inc(S["st"], 1)

                    def bank_read(n):
                        if n >= 2:
                            kind, m = jobs[n - 2]
                            pe.wait_ge(S["mrow" if kind == "guard" else "s_read"], m + 1)

                    def scores(s, t):
                        j, g = s // NG, s % NG
                        r = slice(DH * j, DH * j + DH)
                        n = job_of["tile", 4 * s + t]
                        bank_read(n)
                        mm(ps[:, 2 + n % 2, :], hi[r, 1 - par, 0, g, P * t:P * t + P], hi[r, 1 - par, 1, g, :],
                           start=True, stop=True).then_inc(S["s"], 1)

                    def guard_row(j):
                        n = job_of["guard", j]
                        pe.wait_ge(S["s_read"], 4 * NG * (j + 1))
                        bank_read(n)
                        for t in range(NT):
                            ins = nc.tensor.transpose(ps[0:NG, 2 + n % 2, P * t:P * t + P],
                                                      mS[:, t, NG * j:NG * j + NG], w["ident"][:, :])
                        ins.then_inc(S["s"], 1)

                    def values(s):
                        j, kt = s // NT, s % NT
                        pe.wait_ge(S["exp"], NG * (s + 1))
                        if kt == 0 and j:
                            pe.wait_ge(S["den"], j)
                        for g in range(NG):
                            h = NG * g + j
                            mm(ps[DH * g:DH * g + DH, 6, :], vt[:, kt, DH * h:DH * h + DH], pr[:, s % 2, g, :],
                               start=kt == 0, stop=kt == NT - 1, skip_group_check=True)

                    def denominators(s):
                        kt = s % NT
                        for g in range(NG):
                            ins = mm(ps[DH * g:DH * g + DH, 7, :], w["ones"][:, 0:DH], pr[:, s % 2, g, :],
                                     start=kt == 0, stop=kt == NT - 1, skip_group_check=True)
                        ins.then_inc(S["pv"], 1)

                    for q in range(NT * HEADS):
                        s, t = q // NT, q % NT
                        if att:
                            shifted_scores(s, t)
                        if mid:
                            scores(s, t)
                            if t == 0 and s and s % NG == 0:
                                guard_row(s // NG - 1)
                        if att and s and t == 1:
                            values(s - 1)
                        if att and s and t == 2:
                            denominators(s - 1)
                        if new or old:
                            if q == AT["turn1"]:
                                transposes(1)
                            if q == AT["ffn"]:
                                for k in range(min(2, nt // 2)):
                                    ffn(k)
                            if q == AT["ffn_b"]:
                                for k in range(2, nt // 2):
                                    ffn(k)
                            if q == AT["turn2"]:
                                transposes(2)
                        if old and q == AT["gate"]:
                            gate()
                        if new and q in project_at:
                            project(project_at[q] // 2, project_at[q] % 2)
                    if mid:
                        guard_row(NG - 1)
                    if att:
                        values(NG * NT - 1)
                        denominators(NG * NT - 1)
                    if mid:
                        pe.wait_ge(S["mrow"], NG)
                        pe.wait_ge(S["s_read"], 4 * HEADS)
                        if att:
                            pe.wait_ge(S["exp"], 4 * HEADS)
                        for t in range(NT):
                            mm(ps[:, t, :], xnTn[:, 1 - par, P * t:P * t + P], w["wv"][:, :],
                               start=True, stop=True).then_inc(S["v"], 1)
                    if att:
                        pe.wait_ge(S["norm"], NG)
                        if new:
                            pe.wait_ge(S["pair_free"], 2 * NG)
                        elif old:
                            pe.wait_ge(S["gate_read"], 1)
                        for t in range(NT):
                            for j in range(NG):
                                ins = mm(ps[:, 4, P * t:P * t + P], oT[:, j, P * t:P * t + P], w["wo"][:, j, :],
                                         start=j == 0, stop=j == NG - 1)
                        ins.then_inc(S["wo"], 1)
            nc.gpsimd.sem_clear(range(nums[0], nums[-1] + 1))
            nc.all_engine_barrier(sem_only=True)

        with nc.Block(no_gpsimd_drain=True) as block:
            @block.vector
            def _(dve):
                nc.vector.memset(kst[3 * DH:STK, :, :], 1.0)

            @block.sync
            def _(sp):
                sp.dma_start(x8[:, 0:NT, :], q_in[0].rearrange("(t p) d -> p t d", p=P)).then_inc(S["x_in"], 16)
                sp.wait_ge(S["x_in"], 16)
        nc.gpsimd.sem_clear(range(nums[0], nums[-1] + 1))
        nc.all_engine_barrier(sem_only=True)

        def roles(i):
            return dict(new=i < BATCH, mid=1 <= i <= BATCH, att=2 <= i <= BATCH + 1, old=3 <= i, prefetch=i < BATCH - 1)

        for i in range(3):
            iteration(i, i % 2, **roles(i))
        with nc.Fori(0, (BATCH - 4) // 2, 1) as k:
            iteration(k * 2 + 3, 1, **roles(3))
            iteration(k * 2 + 4, 0, **roles(4))
        for i in range(BATCH - 1, BATCH + 3):
            iteration(i, i % 2, **roles(i))


TWO_PI_HI = 6.28125
TWO_PI_LO = float(2 * np.pi - 6.28125)
ROUND = 1.5 * 2.0 ** 23
PI_F32 = 3.1415925


def reduce_angle(v, wait, r, k, x, quarter):
    wait(v.tensor_scalar(r, x, quarter * float(np.pi) / 2, None, ALU.add))
    wait(v.tensor_scalar(k, r, float(1 / (2 * np.pi)), ROUND, ALU.mult, ALU.add))
    wait(v.tensor_scalar(k, k, ROUND, None, ALU.subtract))
    wait(v.scalar_tensor_tensor(r, k, -TWO_PI_HI, r, ALU.mult, ALU.add))
    wait(v.scalar_tensor_tensor(r, k, -TWO_PI_LO, r, ALU.mult, ALU.add))
    return v.tensor_scalar(r, r, PI_F32, -PI_F32, ALU.min, ALU.max)


def consts_p1():
    return {
        "rope": rope_tables(),
        "ident": np.eye(P, dtype=np.float32),
        "iota": np.tile(np.arange(EXPERTS, dtype=np.float32), (P, NT, 1)),
    }


def layout_p1(x):
    wk = np.asarray(x["L0_attn_Wk"])
    wo = np.asarray(x["L0_attn_Wo"]).reshape(NG, NG, DH, 2, D)
    return {
        "q": np.asarray(x["L0_attn_q"]),
        "wq": np.asarray(x["L0_attn_Wq"]).reshape(D, NG, P, 2).transpose(0, 1, 3, 2),
        "wk": np.stack([wk, wk.reshape(D, KVD // 2, 2)[:, :, ::-1].reshape(D, KVD)], 1),
        "wv": np.asarray(x["L0_attn_Wv"]),
        "wo": wo.transpose(0, 2, 1, 3, 4).reshape(P, NG, 2, D),
        "angles": np.stack([np.asarray(x["L0_ffn_" + n]) for n in
                            ("theta", "theta_noise", "phi", "phi_noise")], 1),
        "gwT": np.asarray(x["L1_ffn_gate_w"]).T,
        "gate_b": np.broadcast_to(np.asarray(x["L1_ffn_gate_b"]), (P, NT, EXPERTS)),
    }


def load_layer0(nc, ctx, ins, cnt_acc):
    sb = lambda name, shape, dt=F32: ctx.enter_context(nc.sbuf_tensor(name, shape, dt))
    w = {"rope": sb("rope", [P, 4, NG, SEQ]), "wq": sb("wq", [P, NG, 2, P]), "wk": sb("wk", [P, 2, KVD]),
         "wv": sb("wv", [P, KVD]), "wo": sb("wo", [P, NG, D]), "csT": sb("csT", [P, 2 * D]),
         "ones": sb("ones", [P, P]), "minus_half": sb("minus_half", [P, 8]), "ident": sb("ident", [P, P]), "gwT": sb("gwT", [P, EXPERTS]),
         "gate_b": sb("gate_b", [P, NT, EXPERTS]), "iota": sb("iota", [P, NT, EXPERTS])}
    with ExitStack() as tmp:
        sbt = lambda name, shape: tmp.enter_context(nc.sbuf_tensor(name, shape, F32))
        wo2, ang, red, k = sbt("wo2", [P, NG, 2, D]), sbt("ang", [P, 4, D]), sbt("red", [P, 2, D]), sbt("kk", [P, 2, D])
        loaded, vd, sn = (tmp.enter_context(nc.semaphore("l_" + n)) for n in ("loaded", "dve", "sin"))
        names = ("rope", "wq", "wk", "wv", "ident", "gwT", "gate_b", "iota")
        with nc.Block(no_gpsimd_drain=True) as block:
            @block.sync
            def _(sp):
                for n in names:
                    sp.dma_start(w[n][:], ins[n]).then_inc(loaded, 16)
                sp.wait_ge(loaded, 16 * len(names))
                sp.dma_start(wo2[:], ins["wo"]).then_inc(loaded, 16)
                sp.dma_start(ang[:], ins["angles"]).then_inc(loaded, 16)

            @block.vector
            def _(dve):
                v, n = nc.vector, [0]

                def wait(i):
                    n[0] += 1
                    i.then_inc(vd, 1)
                    dve.wait_ge(vd, n[0])
                v.memset(w["ones"][:, :], 1.0)
                v.memset(w["minus_half"][:, :], -0.5)
                v.memset(cnt_acc[:, :], 0.0)
                dve.wait_ge(loaded, 16 * (len(names) + 2))
                v.tensor_tensor(w["wo"][:, :, :], wo2[:, :, 0, :], wo2[:, :, 1, :], ALU.add)
                for c in range(2):
                    wait(v.tensor_tensor(ang[:, 2 * c, :], ang[:, 2 * c, :], ang[:, 2 * c + 1, :], ALU.add))
                    wait(reduce_angle(v, wait, red[:, c, :], k[:, c, :], ang[:, 2 * c, :], 1 - c))

            @block.scalar
            def _(act):
                act.wait_ge(vd, 14)
                nc.scalar.activation(w["csT"][:, :], red[:, :, :].rearrange("p c d -> p (c d)"), ACT.Sin).then_inc(sn, 1)
        nc.gpsimd.sem_clear(range(min(loaded.num, vd.num, sn.num), max(loaded.num, vd.num, sn.num) + 1))
        nc.all_engine_barrier(sem_only=True)
    return w




N_STATE, R, HP, M_HEADS = 64, 2, 8, 32
D_INNER = M_HEADS * HP
BLK = 32
RMS_EPS = 1e-6
STATE_SCALE = float((N_STATE * R) ** -0.5)
CLAMP = 85.0
DT_MIN, DT_MAX = 1e-4, 0.5
MID, REF1, REF_END, IN_BLOCK, FROM_START, WHOLE = 0, 1, 4, 5, 6, 7


def decay_sums():
    j, m = np.arange(P)[:, None], np.arange(P)[None, :]
    mid = BLK * (m // BLK) + BLK // 2 - 1
    sums = [((j > m) & (j <= mid)) * 1.0 - ((j > mid) & (j <= m)) * 1.0]
    sums += [(j > m) & (j < BLK * i) for i in (1, 2, 3)]
    sums += [j > m, (j <= m) & (j >= BLK * (m // BLK)), j <= m, j >= 0 * m]
    return np.stack([np.broadcast_to(s, (P, P)).astype(np.float32) for s in sums], 1)


def consts_p2():
    j, m = np.arange(P)[:, None], np.arange(P)[None, :]
    same = j // BLK == m // BLK
    tri = (j <= m).astype(np.float32)
    one = np.ones((P, P), np.float32)
    return {
        "sums": decay_sums(),
        "moves": np.stack([tri, one, (j == m + 1).astype(np.float32),
                           ((j == 0) & (m == P - 1)).astype(np.float32)], 1),
        "masks": np.stack([(same & (m > j)), (m // BLK > j // BLK)], 1).astype(np.float32),
    }


def layout_p2(x):
    w = np.asarray(x["L1_attn_W_in"])
    z, xr, rest, th = w[:, :256], w[:, 256:768], w[:, 768:1024], w[:, 1024:]
    rep = lambda a: np.broadcast_to(np.asarray(a), (P, NT, M_HEADS))
    b, c = np.asarray(x["L1_attn_B_norm_bias"])[0], np.asarray(x["L1_attn_C_norm_bias"])[0]
    return {
        "w_in": np.concatenate([xr, z, rest, th], 1),
        "w_out": np.asarray(x["L1_attn_W_out"]).reshape(2, P, D).transpose(1, 0, 2),
        "a_log": rep(x["L1_attn_A_log"]), "dt_bias": rep(x["L1_attn_dt_bias"]),
        "bc_bias": np.broadcast_to(np.stack([b, b, c]), (P, 3, N_STATE)),
        "ew": np.asarray(x["L1_ffn_expert_w"]).transpose(2, 0, 1),
        "eb": np.asarray(x["L1_ffn_expert_b"]).T,
    }


def load_layer1(nc, ctx, ins):
    sb = lambda name, shape: ctx.enter_context(nc.sbuf_tensor(name, shape, F32))
    w = {"w_in": sb("w_in", [P, 1056]), "w_out": sb("w_out", [P, 2, D]), "a_log": sb("a_log", [P, NT, M_HEADS]),
         "dt_bias": sb("dt_bias", [P, NT, M_HEADS]), "bc_bias": sb("bc_bias", [P, 3, N_STATE]),
         "ew": sb("ew", [P, EXPERTS, D]), "eb": sb("eb", [P, EXPERTS]), "sums": sb("sums", [P, 8, P]),
         "moves": sb("moves", [P, 4, P]), "masks": sb("masks", [P, 2, P]),
         "ident": sb("ident1", [P, P]), "gwT": sb("gwT1", [P, EXPERTS]),
         "gate_b": sb("gate_b1", [P, NT, EXPERTS]), "iota": sb("iota1", [P, NT, EXPERTS])}
    names = list(w)
    w["a"] = sb("a", [P, NT, M_HEADS])
    with ExitStack() as tmp:
        loaded, vd, ex = (tmp.enter_context(nc.semaphore("k_" + n)) for n in ("loaded", "dve", "exp"))
        with nc.Block(no_gpsimd_drain=True) as block:
            @block.sync
            def _(sp):
                for n in names:
                    sp.dma_start(w[n][:], ins[n]).then_inc(loaded, 16)

            @block.scalar
            def _(act):
                act.wait_ge(loaded, 16 * len(names))
                nc.scalar.activation(w["a"][:], w["a_log"][:], ACT.Exp).then_inc(ex, 1)

            @block.vector
            def _(dve):
                dve.wait_ge(ex, 1)
                nc.vector.tensor_scalar(w["a"][:], w["a"][:], -1.0, None, ALU.mult)
                nc.vector.tensor_scalar(w["bc_bias"][:, 2, :], w["bc_bias"][:, 2, :], STATE_SCALE, None, ALU.mult)
        nums = (loaded.num, vd.num, ex.num)
        nc.gpsimd.sem_clear(range(min(nums), max(nums) + 1))
        nc.all_engine_barrier(sem_only=True)
    return w


def expert_weights(nc, tag, w, cnt_acc, ew_s, negb, sumb):
    with ExitStack() as tmp:
        share = tmp.enter_context(nc.sbuf_tensor(tag + "share", [P, EXPERTS], F32))
        pc = tmp.enter_context(nc.psum_tensor(tag + "pc", [P, NT * TOPK * EXPERTS], F32))
        counted, vd = (tmp.enter_context(nc.semaphore(tag + n)) for n in ("counted", "dve"))
        with nc.Block(no_gpsimd_drain=True) as block:
            @block.tensor
            def _(pe):
                nc.tensor.matmul(pc[:, :], w["moves"][:, 1, :], cnt_acc[:, :], start=True, stop=True).then_inc(counted, 1)

            @block.vector
            def _(dve):
                v, n = nc.vector, [0]

                def wait(i):
                    n[0] += 1
                    i.then_inc(vd, 1)
                    dve.wait_ge(vd, n[0])
                dve.wait_ge(counted, 1)
                wait(v.tensor_reduce(share[:, :], pc[:, :].rearrange("p (a e) -> p e a", e=EXPERTS), AX, ALU.add))
                wait(v.tensor_scalar(share[:, :], share[:, :], 0.5 / (BATCH * SEQ * TOPK), None, ALU.mult))
                v.tensor_tensor(ew_s[:, :, :], w["ew"][:, :, :],
                                share[:, :].rearrange("p (e o) -> p e o", o=1).to_broadcast([P, EXPERTS, D]), ALU.mult)
                wait(v.tensor_tensor(negb[:, :], w["eb"][:, :], share[:, :], ALU.mult))
                wait(v.tensor_reduce(sumb[:, :], negb[:, :], AX, ALU.add))
                wait(v.tensor_scalar(negb[:, :], negb[:, :], -1.0, None, ALU.mult))
                v.memset(cnt_acc[:, :], 0.0)
        nc.gpsimd.sem_clear(range(min(counted.num, vd.num), max(counted.num, vd.num) + 1))
        nc.all_engine_barrier(sem_only=True)


def state_phase(nc, x_in, x_out, w, ew_s, negb, sumb, cnt_acc, last):
    with ExitStack() as ctx:
        pre = "f_" if last else "m_"

        def sb(name, shape, dt=F32):
            return ctx.enter_context(nc.sbuf_tensor(pre + name, shape, dt))

        x = sb("x", [P, NT, D])
        y = sb("y", [P, NT, D])
        stats, mv, sd = sb("stats", [P, NT, 6]), sb("mv", [P, NT, 2]), sb("sd", [P, NT, 2])
        xn, xnT = sb("xn", [P, NT, D]), sb("xnT", [P, SEQ])
        acc = sb("acc", [P, 2, SEQ])
        ps = ctx.enter_context(nc.psum_tensor(pre + "ps", [P, 8, 512], F32))
        if not last:
            xr, zs = sb("xr", [P, NT, M_HEADS, R, HP]), sb("zs", [P, NT, D_INNER])
            bc, dl, th = sb("bc", [P, NT, 3, N_STATE]), sb("dl", [P, NT, 2, M_HEADS]), sb("th", [P, NT, M_HEADS])
            t_dt, dt = sb("t_dt", [P, NT, M_HEADS]), sb("dt", [P, NT, M_HEADS])
            lam, gam, bet = sb("lam", [P, NT, M_HEADS]), sb("gam", [P, NT, M_HEADS]), sb("bet", [P, NT, M_HEADS])
            wgt, lda, md = sb("wgt", [P, NT, M_HEADS]), sb("lda", [P, NT, M_HEADS]), sb("md", [P, NT])
            dec = sb("dec", [P, 9, NT, M_HEADS])
            mid = sb("mid", [P, NT, M_HEADS])
            coef = sb("coef", [P, 6, NT, M_HEADS])
            ang, angk = sb("ang", [P, 2, NT, M_HEADS]), sb("angk", [P, 2, NT, M_HEADS])
            sc = sb("sc", [P, 2, NT, M_HEADS])
            sqb, rs12 = sb("sqb", [P, NT, 3, N_STATE]), sb("rs12", [P, 2, NT * 3])
            br = sb("br", [P, NT, 4, N_STATE])
            rp = sb("rp", [P, 4, NT, 3, N_STATE // 2])
            bt = sb("bt", [P, NT, 2, P])
            gm = sb("gm", [P, 2, NT, R, P])
            gd = sb("gd", [P, NT, R])
            xv = sb("xv", [P, 2, 6, M_HEADS, R, HP])
            state = sb("state", [N_STATE, M_HEADS, HP])
            part = sb("part", [P, 2, 4, M_HEADS, HP])
            yz = sb("yz", [P, NT, D_INNER])
            yy = sb("yy", [P, NT, D_INNER])
            rms = sb("rms", [P, 2, NT])
            yzT = sb("yzT", [P, NT, 2, P])
            gl, g8 = sb("gl", [P, NT, EXPERTS]), sb("g8", [P, NT, 8])
            gix, gif = sb("gix", [P, NT, 8], U32), sb("gif", [P, NT, TOPK])
            onehot = sb("onehot", [P, NT, TOPK, EXPERTS])
        names = ("x_in", "x_out", "dve", "var", "sd", "xn", "xT", "xnT", "ex", "ex_read", "accT", "acc", "y",
                 "proj", "proj_v", "proj_a", "silu", "e1", "e2", "e3", "e4", "u", "ang_ps", "ang_r", "sin",
                 "sum_ps", "sum_v", "dec", "rms12", "br", "bt_ps", "bt", "g_ps", "g", "xv", "ymm", "y_read",
                 "st_mm", "state", "ms", "rms", "yz", "yzT_ps", "yzT", "wo", "gate", "gate_read", "beta", "beta_ps")
        S = {n: ctx.enter_context(nc.semaphore(pre + n)) for n in names}
        nums = sorted(s.num for s in S.values())
        assert nums[-1] - nums[0] + 1 == len(nums)

        with nc.Fori(0, BATCH, 1) as b:
            with nc.Block(no_gpsimd_drain=True) as block:
                @block.sync
                def _(sp):
                    sp.dma_start(x[:, :, :], x_in[bass.ds(b, 1)].rearrange(
                        "b (t p) d -> p (b t) d", p=P)).then_inc(S["x_in"], 16)
                    sp.wait_ge(S["y"], 1 if last else 1 + NT)
                    sp.dma_start(x_out[bass.ds(b, 1)].rearrange("b (t p) d -> p (b t) d", p=P),
                                 y[:, :, :]).then_inc(S["x_out"], 16)
                    sp.wait_ge(S["x_out"], 16)

                @block.vector
                def _(dve):
                    v, done = nc.vector, [0]

                    def mark(ins):
                        done[0] += 1
                        ins.then_inc(S["dve"], 1)
                        return done[0]

                    def wait(ins):
                        dve.wait_ge(S["dve"], mark(ins))

                    def layernorm(src, lap):
                        for t in range(NT):
                            n = mark(v.bn_stats(stats[:, t, :], src[:, t, :]))
                        dve.wait_ge(S["dve"], n)
                        for t in range(NT):
                            n = mark(v.bn_aggr(mv[:, t, :], stats[:, t, :]))
                        dve.wait_ge(S["dve"], n)
                        v.tensor_scalar(sd[:, :, 0], mv[:, :, 1], LN_EPS, None, ALU.add).then_inc(S["var"], 1)
                        dve.wait_ge(S["sd"], lap)
                        wait(v.reciprocal(sd[:, :, 0], sd[:, :, 1]))
                        for t in range(NT):
                            v.tensor_scalar(xn[:, t, :], src[:, t, :], mv[:, t, 0:1], sd[:, t, 0:1],
                                            ALU.subtract, ALU.mult).then_inc(S["xn"], 1)
                        dve.wait_ge(S["xT"], lap)
                        v.tensor_copy(xnT[:, :], ps[:, 4, :]).then_inc(S["xnT"], 1)

                    dve.wait_ge(S["x_in"], 16)
                    layernorm(x, 1)
                    for e in range(EXPERTS):
                        dve.wait_ge(S["ex"], e + 1)
                        if e == 0:
                            ins = v.tensor_scalar(acc[:, 0, :], ps[:, 0, :], negb[:, 0:1], sumb[:, 0:1],
                                                  ALU.max, ALU.add)
                        else:
                            dve.wait_ge(S["ex_read"], e)
                            ins = v.scalar_tensor_tensor(acc[:, e % 2, :], ps[:, e % 4, :], negb[:, e:e + 1],
                                                         acc[:, (e - 1) % 2, :], ALU.max, ALU.add)
                        ins.then_inc(S["ex_read"], 1)
                    dve.wait_ge(S["accT"], 1)
                    v.tensor_tensor(y[:, :, :], x[:, :, :], ps[:, 5, :].rearrange("p (t d) -> p t d", t=NT),
                                    ALU.add).then_inc(S["y"], 1)
                    if last:
                        return
                    dve.wait_ge(S["y"], 1)
                    layernorm(y, 2)
                    for t in range(NT):
                        dve.wait_ge(S["proj"], t + 1)
                        dve.wait_ge(S["silu"], 2 * t + 2)
                        s0 = 3 * (t % 2)
                        v.tensor_copy(bc[:, t, :, :], ps[:, s0 + 1, 256:448].rearrange("p (c n) -> p c n", c=3))
                        v.tensor_copy(dl[:, t, :, :], ps[:, s0 + 1, 448:512].rearrange("p (c n) -> p c n", c=2))
                        v.tensor_copy(th[:, t, :], ps[:, s0 + 2, 0:M_HEADS]).then_inc(S["proj_v"], 1)
                    dve.wait_ge(S["proj_v"], NT)
                    wait(v.tensor_tensor(t_dt[:, :, :], dl[:, :, 0, :], w["dt_bias"][:, :, :], ALU.add))
                    v.tensor_scalar(t_dt[:, :, :], t_dt[:, :, :], 0.0, None, ALU.min).then_inc(S["u"], 1)
                    dve.wait_ge(S["e2"], 1)
                    wait(v.tensor_scalar(dt[:, :, :], dt[:, :, :], DT_MIN, DT_MAX, ALU.max, ALU.min))
                    mark(v.tensor_tensor(lda[:, :, :], dt[:, :, :], w["a"][:, :, :], ALU.mult))
                    wait(v.tensor_reduce(md[:, :], dt[:, :, :], AX, ALU.add))
                    wait(v.tensor_scalar(md[:, :], md[:, :], -1.0 / M_HEADS, None, ALU.mult))
                    v.tensor_tensor(th[:, :, :], th[:, :, :], md[:, :].rearrange(
                        "p (t o) -> p t o", o=1).to_broadcast([P, NT, M_HEADS]), ALU.mult).then_inc(S["e3"], 1)
                    wait(v.tensor_scalar(lam[:, :, :], lam[:, :, :], 1.0, None, ALU.add))
                    wait(v.reciprocal(lam[:, :, :], lam[:, :, :]))
                    wait(v.tensor_tensor(gam[:, :, :], lam[:, :, :], dt[:, :, :], ALU.mult))
                    v.tensor_tensor(bet[:, :, :], dt[:, :, :], gam[:, :, :], ALU.subtract).then_inc(S["beta"], 1)
                    wait(v.tensor_tensor(sqb[:, :, :, :], bc[:, :, :, :], bc[:, :, :, :], ALU.mult))
                    wait(v.tensor_reduce(rs12[:, 0, :], sqb[:, :, :, :].rearrange("p t c n -> p (t c) n"), AX, ALU.add))
                    v.tensor_scalar(rs12[:, 0, :], rs12[:, 0, :], 1.0 / N_STATE, RMS_EPS, ALU.mult,
                                    ALU.add).then_inc(S["rms12"], 1)
                    dve.wait_ge(S["ang_ps"], 1)
                    for q in range(2):
                        ins = reduce_angle(v, wait, ang[:, q], angk[:, q],
                                           ps[:, 7, 0:128].rearrange("p (t h) -> p t h", t=NT), q)
                    ins.then_inc(S["ang_r"], 1)
                    dve.wait_ge(S["sum_ps"], 1)
                    v.tensor_scalar(mid[:, :, :], ps[:, 0, 0:128].rearrange("p (t h) -> p t h", t=NT),
                                    CLAMP, -CLAMP, ALU.min, ALU.max).then_inc(S["sum_v"], 1)
                    dve.wait_ge(S["beta_ps"], 1)
                    wait(v.tensor_tensor(wgt[:, :, :], gam[:, :, :], ps[:, 7, 128:256].rearrange(
                        "p (t h) -> p t h", t=NT), ALU.add))
                    dve.wait_ge(S["dec"], 1)
                    mark(v.tensor_copy(coef[:, 5], gam[:, :, :]))
                    wait(v.tensor_tensor(
                        coef[:, 0:5].rearrange("p c t h -> p c (t h)"), dec[:, 0:5].rearrange("p c t h -> p c (t h)"),
                        wgt[:, :, :].rearrange("p (o t) h -> p o (t h)", o=1).to_broadcast([P, 5, NT * M_HEADS]),
                        ALU.mult))
                    dve.wait_ge(S["e4"], 1)
                    wait(v.reciprocal(rs12[:, 0, :], rs12[:, 1, :]))
                    wait(v.tensor_tensor(sqb[:, :, :, :].rearrange("p t c n -> p (t c) n"),
                                         bc[:, :, :, :].rearrange("p t c n -> p (t c) n"),
                                         rs12[:, 0, :].rearrange("p (c o) -> p c o", o=1).to_broadcast(
                                             [P, NT * 3, N_STATE]), ALU.mult))
                    wait(v.tensor_tensor(sqb[:, :, :, :].rearrange("p t c n -> p t (c n)"),
                                         sqb[:, :, :, :].rearrange("p t c n -> p t (c n)"),
                                         w["bc_bias"][:, :, :].rearrange("p (o c) n -> p o (c n)", o=1).to_broadcast(
                                             [P, NT, 3 * N_STATE]), ALU.mult))
                    dve.wait_ge(S["sin"], 1)
                    half = N_STATE // 2
                    for c, (s0, k) in enumerate(((0, 1), (half, 0), (0, 0), (half, 1))):
                        n = mark(v.tensor_tensor(rp[:, c], sqb[:, :, :, s0:s0 + half],
                                                 sc[:, k].rearrange("p t (o n) -> p t o n", o=1).to_broadcast(
                                                     [P, NT, 3, half]), ALU.mult))
                    dve.wait_ge(S["dve"], n)
                    v.tensor_tensor(br[:, :, 0:3, 0:half], rp[:, 0], rp[:, 1], ALU.subtract)
                    wait(v.tensor_tensor(br[:, :, 0:3, half:], rp[:, 2], rp[:, 3], ALU.add))
                    v.tensor_copy(br[:, :, 3, :], br[:, :, 2, :]).then_inc(S["br"], 1)
                    wait(v.tensor_tensor(sqb[:, :, 0:2, :], br[:, :, 0:2, :], br[:, :, 2:3, :].to_broadcast(
                        [P, NT, 2, N_STATE]), ALU.mult))
                    mark(v.tensor_reduce(gd[:, :, :], sqb[:, :, 0:2, :], AX, ALU.add))
                    dve.wait_ge(S["bt_ps"], 1)
                    v.tensor_copy(bt[:, 0:2], ps[:, 4, :].rearrange("p (t c m) -> p t c m", t=2, c=2))
                    v.tensor_copy(bt[:, 2:4], ps[:, 5, :].rearrange("p (t c m) -> p t c m", t=2, c=2)).then_inc(S["bt"], 1)
                    dve.wait_ge(S["g_ps"], 1)
                    for k in range(2):
                        for u in range(2):
                            ins = v.tensor_tensor(
                                gm[:, k, :, u, :],
                                ps[:, 6 + u, :].rearrange("p (a m) -> p a m", a=4),
                                w["masks"][:, k:k + 1, :].to_broadcast([P, 4, P]), ALU.mult)
                            ins.then_inc(S["g"], 1)
                    gam_done = done[0]
                    dve.wait_ge(S["dve"], gam_done)
                    dve.wait_ge(S["silu"], 2 * NT)

                    def variants(t):
                        if t >= 2:
                            dve.wait_ge(S["ymm"], t - 1)
                            dve.wait_ge(S["st_mm"], t - 1)
                        for c in (0, 1, 2, 3, 4, 5):
                            if c == REF_END and t == NT - 1:
                                continue
                            ins = v.tensor_tensor(
                                xv[:, t % 2, c].rearrange("p h r q -> p h (r q)"),
                                xr[:, t].rearrange("p h r q -> p h (r q)"),
                                coef[:, c, t, :].rearrange("p (h o) -> p h o", o=1).to_broadcast(
                                    [P, M_HEADS, R * HP]), ALU.mult)
                        ins.then_inc(S["xv"], 1)

                    def outputs(t):
                        bank = 2 * (t % 2)
                        pt = part[:, t % 2]

                        def row(c):
                            return dec[:, c, t, :].rearrange("p (h o) -> p h o", o=1).to_broadcast([P, M_HEADS, HP])

                        def mmo(k, o):
                            return ps[:, k, o:o + 256].rearrange("p (h q) -> p h q", q=HP)
                        dve.wait_ge(S["ymm"], t + 1)
                        v.tensor_tensor(pt[:, 0], mmo(bank, 0), row(8), ALU.mult)
                        ins = v.tensor_tensor(pt[:, 1], mmo(bank, 256), row(IN_BLOCK), ALU.mult)
                        if t < NT - 1:
                            dve.wait_ge(S["st_mm"], t + 1)
                        if t:
                            ins = v.tensor_tensor(pt[:, 2], mmo(bank + 1, 0), row(FROM_START), ALU.mult)
                        ins.then_inc(S["y_read"], 1)
                        if t < NT - 1:
                            new = ps[0:N_STATE, bank + 1, 256:512].rearrange("p (h q) -> p h q", q=HP)
                            if t == 0:
                                v.tensor_copy(state[:, :, :], new).then_inc(S["state"], 1)
                            else:
                                dve.wait_ge(S["state"], t)
                                wait(v.tensor_tensor(part[0:N_STATE, t % 2, 3], state[:, :, :],
                                                     dec[0:N_STATE, WHOLE, t, :].rearrange(
                                                         "p (h o) -> p h o", o=1).to_broadcast([N_STATE, M_HEADS, HP]),
                                                     ALU.mult))
                                v.tensor_tensor(state[:, :, :], part[0:N_STATE, t % 2, 3], new,
                                                ALU.add).then_inc(S["state"], 1)
                        dve.wait_ge(S["y_read"], t + 1)
                        wait(v.tensor_tensor(pt[:, 1], pt[:, 0], pt[:, 1], ALU.add))
                        if t:
                            wait(v.tensor_tensor(pt[:, 1], pt[:, 1], pt[:, 2], ALU.add))
                        for r in range(R):
                            wait(v.scalar_tensor_tensor(pt[:, r],
                                                        xv[:, t % 2, 5, :, r, :], gd[:, t, r:r + 1],
                                                        pt[:, 1 - r], ALU.mult, ALU.add))
                        v.tensor_tensor(yz[:, t, :], pt[:, 1].rearrange("p h q -> p (h q)"), zs[:, t, :],
                                        ALU.mult).then_inc(S["yz"], 1)
                        dve.wait_ge(S["yz"], t + 1)
                        mark(v.tensor_tensor_reduce(yy[:, t, :], yz[:, t, :], yz[:, t, :], 1.0, 0.0, ALU.mult, ALU.add,
                                                    rms[:, 0, t:t + 1]))

                    variants(0)
                    for t in range(NT):
                        if t + 1 < NT:
                            variants(t + 1)
                        outputs(t)
                    dve.wait_ge(S["dve"], done[0])
                    v.tensor_scalar(rms[:, 0, :], rms[:, 0, :], 1.0 / D_INNER, RMS_EPS, ALU.mult, ALU.add).then_inc(S["ms"], 1)
                    dve.wait_ge(S["yzT_ps"], 1)
                    v.tensor_copy(yzT[:, 0:2], ps[:, 4, :].rearrange("p (t c m) -> p t c m", t=2, c=2))
                    v.tensor_copy(yzT[:, 2:4], ps[:, 5, :].rearrange("p (t c m) -> p t c m", t=2, c=2)).then_inc(S["yzT"], 1)
                    dve.wait_ge(S["rms"], 1)
                    wait(v.reciprocal(rms[:, 0, :], rms[:, 1, :]))
                    dve.wait_ge(S["wo"], 1)
                    for t in range(NT):
                        v.scalar_tensor_tensor(y[:, t, :], ps[:, 6, P * t:P * t + P], rms[:, 0, t:t + 1], y[:, t, :],
                                               ALU.mult, ALU.add).then_inc(S["y"], 1)
                    dve.wait_ge(S["y"], 1 + NT)
                    layernorm(y, 3)
                    dve.wait_ge(S["gate"], 1)
                    v.tensor_tensor(gl[:, :, :], ps[:, 7, 0:NT * EXPERTS].rearrange(
                        "p (t e) -> p t e", t=NT), w["gate_b"][:, :, :], ALU.add).then_inc(S["gate_read"], 1)
                    dve.wait_ge(S["gate_read"], 1)
                    top_two(v, dve, S["dve"], mark, gl, g8, gix, gif)
                    count_choices(v, dve, S["dve"], mark, gif, onehot, w, cnt_acc)

                @block.scalar
                def _(act):
                    a = nc.scalar

                    def sqrt_of_var(lap):
                        act.wait_ge(S["var"], lap)
                        a.activation(sd[:, :, 1], sd[:, :, 0], ACT.Sqrt).then_inc(S["sd"], 1)
                    sqrt_of_var(1)
                    if last:
                        return
                    sqrt_of_var(2)
                    for t in range(NT):
                        s0 = 3 * (t % 2)
                        act.wait_ge(S["proj"], t + 1)
                        a.activation(xr[:, t].rearrange("p h r q -> p (h r q)"), ps[:, s0, :], ACT.Silu).then_inc(S["silu"], 1)
                        a.activation(zs[:, t, :], ps[:, s0 + 1, 0:256], ACT.Silu).then_inc(S["silu"], 1)
                    act.wait_ge(S["proj_v"], NT)
                    a.activation(lam[:, :, :], dl[:, :, 1, :], ACT.Exp, scale=-1.0)
                    act.wait_ge(S["u"], 1)
                    a.activation(dt[:, :, :], t_dt[:, :, :], ACT.Exp).then_inc(S["e1"], 1)
                    act.wait_ge(S["e1"], 1)
                    a.activation(dt[:, :, :], dt[:, :, :], ACT.Ln, bias=1.0).then_inc(S["e2"], 1)
                    act.wait_ge(S["sum_ps"], 1)
                    act.wait_ge(S["sum_v"], 1)
                    a.activation(dec[:, 0], mid[:, :, :], ACT.Exp)
                    a.activation(dec[:, 8], mid[:, :, :], ACT.Exp, scale=-1.0)
                    a.activation(dec[:, 1:4].rearrange("p c t h -> p (c t h)"), ps[:, 0, 128:512], ACT.Exp)
                    a.activation(dec[:, 4:8].rearrange("p c t h -> p (c t h)"), ps[:, 1, :], ACT.Exp).then_inc(S["dec"], 1)
                    act.wait_ge(S["rms12"], 1)
                    a.activation(rs12[:, 1, :], rs12[:, 0, :], ACT.Sqrt).then_inc(S["e4"], 1)
                    act.wait_ge(S["ang_r"], 1)
                    a.activation(sc[:, :].rearrange("p c t h -> p (c t h)"),
                                 ang[:, :].rearrange("p c t h -> p (c t h)"), ACT.Sin).then_inc(S["sin"], 1)
                    act.wait_ge(S["ms"], 1)
                    a.activation(rms[:, 1, :], rms[:, 0, :], ACT.Sqrt).then_inc(S["rms"], 1)
                    sqrt_of_var(3)

                @block.tensor
                def _(pe):
                    mm = nc.tensor.matmul

                    def transposes(lap):
                        pe.wait_ge(S["xn"], NT * lap)
                        for t in range(NT):
                            ins = nc.tensor.transpose(ps[:, 4, P * t:P * t + P], xn[:, t, :], w["ident"][:, :])
                        ins.then_inc(S["xT"], 1)
                        pe.wait_ge(S["xnT"], lap)

                    transposes(1)
                    for e in range(EXPERTS):
                        if e >= 4:
                            pe.wait_ge(S["ex_read"], e - 3)
                        mm(ps[:, e % 4, :], ew_s[:, e, :], xnT[:, :], start=True, stop=True).then_inc(S["ex"], 1)
                    pe.wait_ge(S["ex_read"], EXPERTS)
                    for t in range(NT):
                        ins = nc.tensor.transpose(ps[:, 5, P * t:P * t + P], acc[:, 1, P * t:P * t + P], w["ident"][:, :])
                    ins.then_inc(S["accT"], 1)
                    if last:
                        return
                    transposes(2)
                    for t in range(NT):
                        s0 = 3 * (t % 2)
                        if t >= 2:
                            pe.wait_ge(S["silu"], 2 * (t - 1))
                            pe.wait_ge(S["proj_v"], t - 1)
                        if t == 1:
                            pe.wait_ge(S["y"], 1)
                        xs = xnT[:, P * t:P * t + P]
                        mm(ps[:, s0, :], xs, w["w_in"][:, 0:512], start=True, stop=True)
                        mm(ps[:, s0 + 1, :], xs, w["w_in"][:, 512:1024], start=True, stop=True)
                        mm(ps[:, s0 + 2, 0:32], xs, w["w_in"][:, 1024:1056], start=True, stop=True).then_inc(S["proj"], 1)
                    pe.wait_ge(S["e3"], 1)
                    mm(ps[:, 7, 0:128], w["moves"][:, 0, :], th[:, :, :], start=True, stop=False, skip_group_check=True)
                    for s in range(1, NT):
                        ins = mm(ps[:, 7, 32 * s:128], w["moves"][:, 1, :], th[:, 0:NT - s, :], start=False,
                                 stop=s == NT - 1, skip_group_check=True)
                    ins.then_inc(S["ang_ps"], 1)
                    pe.wait_ge(S["silu"], 2 * NT)
                    pe.wait_ge(S["proj_v"], NT)
                    for c in range(8):
                        ins = mm(ps[:, c // 4, P * (c % 4):P * (c % 4) + P], w["sums"][:, c, :], lda[:, :, :],
                                 start=True, stop=True)
                    ins.then_inc(S["sum_ps"], 1)
                    pe.wait_ge(S["beta"], 1)
                    pe.wait_ge(S["ang_r"], 1)
                    mm(ps[:, 7, 128:256], w["moves"][:, 2, :], bet[:, :, :], start=True, stop=False, skip_group_check=True)
                    mm(ps[:, 7, 128:224], w["moves"][:, 3, :], bet[:, 1:NT, :], start=False, stop=True,
                       skip_group_check=True).then_inc(S["beta_ps"], 1)
                    pe.wait_ge(S["br"], 1)
                    for t in range(NT):
                        for c in range(2):
                            ins = nc.tensor.transpose(ps[:, 4 + t // 2, 256 * (t % 2) + P * c:256 * (t % 2) + P * c + P],
                                                      br[:, t, 2 * c:2 * c + 2, :].rearrange("p c n -> p (c n)"),
                                                      w["ident"][:, :])
                    ins.then_inc(S["bt_ps"], 1)
                    pe.wait_ge(S["bt"], 1)
                    pe.wait_ge(S["dec"], 1)
                    for t in range(NT):
                        for r in range(R):
                            n = slice(N_STATE * r, N_STATE * r + N_STATE)
                            ins = mm(ps[:, 6 + r, P * t:P * t + P], bt[n, t, 0, :], bt[n, t, 1, :], start=True, stop=True)
                    ins.then_inc(S["g_ps"], 1)
                    pe.wait_ge(S["g"], 4)
                    for t in range(NT):
                        bank = 2 * (t % 2)
                        pe.wait_ge(S["xv"], t + 1)
                        if t >= 2:
                            pe.wait_ge(S["state"], t - 1)
                            pe.wait_ge(S["y_read"], t - 1)
                        for r in range(R):
                            mm(ps[:, bank, 0:256], gm[:, 0, t, r, :], xv[:, t % 2, 0, :, r, :],
                               start=r == 0, stop=r == R - 1, skip_group_check=True)
                        for blk in range(4):
                            for r in range(R):
                                rows = slice(BLK * blk, BLK * blk + BLK)
                                ins = mm(ps[rows, bank, 256:512], gm[:, 1, t, r, rows], xv[:, t % 2, max(blk, 1), :, r, :],
                                         start=r == 0, stop=r == R - 1, skip_group_check=True)
                        if t:
                            pe.wait_ge(S["state"], t)
                            ins = mm(ps[:, bank + 1, 0:256], bt[0:N_STATE, t, 1, :], state[:, :, :],
                                     start=True, stop=True, skip_group_check=True)
                        ins.then_inc(S["ymm"], 1)
                        if t < NT - 1:
                            for r in range(R):
                                ins = mm(ps[0:N_STATE, bank + 1, 256:512], br[:, t, r, :], xv[:, t % 2, REF_END, :, r, :],
                                         start=r == 0, stop=r == R - 1, skip_group_check=True)
                            ins.then_inc(S["st_mm"], 1)
                    pe.wait_ge(S["yz"], NT)
                    for t in range(NT):
                        for c in range(2):
                            o = 256 * (t % 2) + P * c
                            ins = nc.tensor.transpose(ps[:, 4 + t // 2, o:o + P], yz[:, t, P * c:P * c + P], w["ident"][:, :])
                    ins.then_inc(S["yzT_ps"], 1)
                    pe.wait_ge(S["yzT"], 1)
                    for t in range(NT):
                        for c in range(2):
                            ins = mm(ps[:, 6, P * t:P * t + P], yzT[:, t, c, :], w["w_out"][:, c, :],
                                     start=c == 0, stop=c == 1)
                    ins.then_inc(S["wo"], 1)
                    transposes(3)
                    for t in range(NT):
                        ins = mm(ps[:, 7, EXPERTS * t:EXPERTS * t + EXPERTS], xnT[:, P * t:P * t + P],
                                 w["gwT"][:, :], start=True, stop=True)
                    ins.then_inc(S["gate"], 1)
            nc.gpsimd.sem_clear(range(nums[0], nums[-1] + 1))
            nc.all_engine_barrier(sem_only=True)


INS = ["q", "wq", "wk", "wv", "wo", "angles", "gwT", "gate_b", "rope", "ident", "iota",
       "w_in", "w_out", "a_log", "dt_bias", "bc_bias", "ew", "eb", "sums", "moves", "masks"]


def build(nc, ins, out):
    x3 = nc.dram_tensor("x3", (BATCH, SEQ, D), F32, kind="Internal").ap()
    x5 = nc.dram_tensor("x5", (BATCH, SEQ, D), F32, kind="Internal").ap()
    with ExitStack() as ctx:
        sb = lambda name, shape: ctx.enter_context(nc.sbuf_tensor(name, shape, F32))
        cnt_acc = sb("cnt_acc", [P, NT * TOPK * EXPERTS])
        with ExitStack() as layer0:
            w = load_layer0(nc, layer0, ins, cnt_acc)
            attention_phase(nc, ins["q"], x3, w, cnt_acc)
        w = load_layer1(nc, ctx, ins)
        ew_s, negb, sumb = sb("ew_s", [P, EXPERTS, D]), sb("negb", [P, EXPERTS]), sb("sumb", [P, 1])
        expert_weights(nc, "e1_", w, cnt_acc, ew_s, negb, sumb)
        state_phase(nc, x3, x5, w, ew_s, negb, sumb, cnt_acc, False)
        expert_weights(nc, "e2_", w, cnt_acc, ew_s, negb, sumb)
        state_phase(nc, x5, out, w, ew_s, negb, sumb, cnt_acc, True)


def kernel(**inputs):
    import numpy as _np
    import concourse.bacc as _bacc
    from concourse import mybir as _mybir
    from concourse.bass_utils import run_bass_kernel_spmd as _run

    nc = _bacc.Bacc("TRN2", target_bir_lowering=False, num_devices=1)
    given = {**layout_p1(inputs), **layout_p2(inputs), **consts_p1(), **consts_p2()}
    arrays, aps = {}, {}
    for name in INS:
        a = _np.ascontiguousarray(given[name])
        arrays[f"in_{name}"] = a
        aps[name] = nc.dram_tensor(f"in_{name}", a.shape, _mybir.dt.from_np(a.dtype), kind="ExternalInput").ap()
    out = nc.dram_tensor("out_0", (BATCH, SEQ, D), F32, kind="ExternalOutput").ap()
    build(nc, aps, out)
    r = _run(nc, [arrays], core_ids=[0])
    return r.results[0]["out_0"]
```

```python
from contextlib import ExitStack

import numpy as np
import concourse.bass as bass
from concourse import mybir

F32 = mybir.dt.float32
F16 = mybir.dt.float16
U32 = mybir.dt.uint32
ALU = mybir.AluOpType
ACT = mybir.ActivationFunctionType
AX = mybir.AxisListType.X

P = 128
BATCH, SEQ, D = 16, 512, 128
NT = SEQ // P
HEADS, KVD, DH = 16, 512, 32
NG = 4
EXPERTS, TOPK = 8, 2
LN_EPS = 1e-5
STK = 3 * DH + 1
W_SCALE = 64.0
ATT_SCALE = float((64 / 16) ** -0.5)


def rope_tables():
    pos = np.arange(1, SEQ + 1, dtype=np.float32)
    def angles(dim):
        exponent = np.arange(0, dim, 2, dtype=np.float32) / np.float32(dim)
        th = (np.float32(1.0) / np.power(np.float32(1250), exponent)).astype(np.float32)
        return (pos[:, None] * th[None, :]).astype(np.float32).T.astype(np.float64)
    aq = angles(2 * KVD)
    ak = np.repeat(angles(KVD), 2, axis=0)
    sign = np.where(np.arange(KVD) % 2 == 0, -1.0, 1.0)[:, None]
    t = np.stack([np.cos(aq) + np.sin(aq), np.cos(aq) - np.sin(aq), np.cos(ak), sign * np.sin(ak)])
    t = t / W_SCALE
    return t.reshape(4, NG, P, SEQ).transpose(2, 0, 1, 3).astype(np.float32).copy()


def top_two(v, dve, sem, mark, gl, g8, gix, gif):
    for t in range(NT):
        n = mark(v.max(g8[:, t, :], gl[:, t, :]))
    dve.wait_ge(sem, n)
    for t in range(NT):
        n = mark(v.max_index(gix[:, t, :], g8[:, t, :], gl[:, t, :]))
    dve.wait_ge(sem, n)
    dve.wait_ge(sem, mark(v.tensor_copy(gif[:, :, :], gix[:, :, 0:TOPK])))


def count_choices(v, dve, sem, mark, gif, onehot, w, cnt_acc):
    for k in range(TOPK):
        n = mark(v.tensor_tensor(onehot[:, :, k, :], w["iota"][:, :, :],
                                 gif[:, :, k:k + 1].to_broadcast([P, NT, EXPERTS]), ALU.is_equal))
    dve.wait_ge(sem, n)
    v.tensor_tensor(cnt_acc[:, :], cnt_acc[:, :], onehot[:, :, :, :].rearrange("p t k e -> p (t k e)"), ALU.add)


ATTENTION_AT = {
    "values": (1, 3, 8, 9), "output": 4, "x2": 4, "keep": 5,
    "stats1": 5, "aggr1": 9, "xn1": 11, "turn1": 16, "evac1": 16, "ffn": 17, "squares": 21, "ffn_b": 22,
    "squares_b": 22, "sqrt": 25, "resid": 25, "stats2": 27, "aggr2": 29, "xn2": 31, "turn2": 36, "evac2": 36,
    "gate": 37, "gate_in": 37, "gate_top": 38, "gate_count": 44,
    "project": (37, 38, 39, 40, 41, 43, 44, 46, 47, 48, 50, 51, 54, 57, 59, 60), "high_lag": 3, "low_lag": 2,
    "add_lag": 0, "denominators_lag": 3,
}


def attention_phase(nc, q_in, rope_in, x3_out, w, cnt_acc):
    with ExitStack() as ctx:
        def sb(name, shape, dt=F32):
            return ctx.enter_context(nc.sbuf_tensor(name, shape, dt))

        x8 = sb("x8", [P, 8, D])
        ynew = sb("ynew", [P, 2, NT, D])
        yold = sb("yold", [P, NT, D])
        xkeep = sb("xkeep", [P, 2, NT, D])
        stats = sb("stats", [P, 8, 6])
        mv = sb("mv", [P, 8, 2])
        veps = sb("veps", [P, 8])
        nmean = sb("nmean", [P, 8])
        shift = sb("shift", [P, 8])
        rstd = sb("rstd", [P, 8])
        xn = sb("xn", [P, 8, D])
        xnTn = sb("xnTn", [P, SEQ])
        xnh, xnl = (sb(n, [P, 2, SEQ], F16) for n in ("xnh", "xnl"))
        xnTo = sb("xnTo", [P, SEQ])
        sq = sb("sq", [P, 2, 2, 2, D])
        hh = xn
        terms = sb("terms", [P, 2, 2, SEQ])
        hi = sb("hi", [P, 2, 2, NG, SEQ], F16)
        lo = sb("lo", [P, 2, 2, NG, SEQ], F16)
        qst = sb("qst", [STK, HEADS, SEQ], F16)
        kst = sb("kst", [STK, HEADS, SEQ], F16)
        vt = sb("vt", [P, NT, KVD])
        pr = sb("pr", [P, 2, NT, SEQ])
        mS = sb("mS", [P, NT, HEADS])
        nm = sb("nm", [NG, 2, SEQ], F16)
        den = sb("den", [P, SEQ])
        denT = sb("denT", [P, SEQ])
        inv = sb("inv", [P, SEQ // 32])
        prs = sb("prs", [P, NG, SEQ])
        oT = sb("oT", [P, NG, SEQ])
        gl = sb("gl", [P, NT, EXPERTS])
        g8 = sb("g8", [P, NT, 8])
        gix = sb("gix", [P, NT, 8], U32)
        gif = sb("gif", [P, NT, TOPK])
        onehot = sb("onehot", [P, NT, TOPK, EXPERTS])
        ps = ctx.enter_context(nc.psum_tensor("ps", [P, 8, 512], F32))

        names = ("x_in", "var", "rstd", "xn", "xT", "xnT", "ff", "sq", "ss", "h", "y", "pair", "pair_free",
                 "rot", "hi", "lo", "gate", "gate_read", "st", "exp", "s", "s_read", "stacked", "mrow",
                 "pv", "den", "norm", "last_norm", "wo", "x2", "v", "dve", "x_out",
                 "xnh", "xnl", "v_ps", "prs", "dn", "dd", "o", "late", "shift", "x_first", "rope_in")
        S = {n: ctx.enter_context(nc.semaphore("a_" + n)) for n in names}
        for c in range(2):
            S["mrow_sent", c] = ctx.enter_context(nc.semaphore(f"a_mrow_sent{c}"))
        nums = sorted(s.num for s in S.values())
        assert nums[-1] - nums[0] + 1 == len(nums)

        jobs = []
        for s in range(HEADS + 1):
            for t in range(NT):
                if s < HEADS:
                    jobs.append(("tile", 4 * s + t))
                if t == 0 and s and s % NG == 0:
                    jobs.append(("guard", s // NG - 1))
        job_of = {j: n for n, j in enumerate(jobs)}
        AT = ATTENTION_AT
        product_at = {q + 1: m for m, q in enumerate(AT["project"])}
        rotated_at, high_at, low_at = ({q + lag: m // 2 for m, q in enumerate(AT["project"]) if m % 2}
                                       for lag in (1, AT["high_lag"], AT["low_lag"]))

        def iteration(i, par, new, mid, att, old, prefetch, first=False):
            halves = ([0] if new else []) + ([1] if old else [])
            tiles = [NT * h + t for h in halves for t in range(NT)]
            nt, nh = len(tiles), len(halves)
            a0, b0 = (tiles[0], tiles[-1] + 1) if tiles else (0, 0)

            def after_ffn(t):
                return ynew[:, par, t, :] if t < NT else yold[:, t - NT, :]

            def xnT_tile(t):
                src = xnTn if t < NT else xnTo
                return src[:, P * (t % NT):P * (t % NT) + P]

            with nc.Block(no_gpsimd_drain=True) as block:
                @block.sync
                def _(sp):
                    def stack(j, p, halves_sent, guard_sent):
                        r = slice(DH * j, DH * j + DH)
                        q_hi, q_lo, k_hi, k_lo = hi[r, p, 0], lo[r, p, 0], hi[r, p, 1], lo[r, p, 1]
                        for dst, src, row in ((qst, q_hi, 0), (qst, q_lo, 1), (qst, q_hi, 2),
                                              (kst, k_hi, 0), (kst, k_hi, 1), (kst, k_lo, 2)):
                            sp.dma_start(dst[DH * row:DH * row + DH, NG * j:NG * j + NG, :],
                                         src).then_inc(halves_sent, 16)
                        if guard_sent is not S["late"]:
                            sp.wait_ge(S["mrow"], j + 1)
                        sp.dma_start(qst[3 * DH:STK, NG * j:NG * j + NG, :], nm[:, j % 2, :]).then_inc(guard_sent, 16)

                    if first:
                        sp.dma_start(x8[:, 0:NT, :], q_in[0].rearrange("(t p) d -> p t d", p=P)).then_inc(S["x_first"], 16)
                        sp.dma_start(w["rope"][:], rope_in).then_inc(S["rope_in"], 16)
                        sp.wait_ge(S["rope_in"], 16)

                    if att:
                        stack(NG - 1, par, S["late"], S["late"])
                    if mid:
                        for j in range(NG - 1):
                            if att:
                                sp.wait_ge(S["st"], 16 * (j + 1))
                            stack(j, 1 - par, S["stacked"], S["mrow_sent", j % 2])
                    if new or old:
                        sp.wait_ge(S["y"], nh)
                    if prefetch:
                        sp.dma_start(x8[:, 0:NT, :], q_in[bass.ds(i + 1, 1)].rearrange(
                            "b (t p) d -> p (b t) d", p=P)).then_inc(S["x_in"], 16)
                    if old:
                        sp.dma_start(x3_out[bass.ds(i - 3, 1)].rearrange("b (t p) d -> p (b t) d", p=P),
                                     yold[:, :, :]).then_inc(S["x_out"], 16)
                        sp.wait_ge(S["x_out"], 16)
                    if prefetch:
                        sp.wait_ge(S["x_in"], 16)
                    if mid:
                        sp.wait_ge(S["stacked"], 16 * 6 * (NG - 1))
                        sp.wait_ge(S["mrow_sent", 0], 32)
                        sp.wait_ge(S["mrow_sent", 1], 16)
                    if att:
                        sp.wait_ge(S["late"], 16 * 7)

                @block.vector
                def _(dve):
                    v = nc.vector
                    done = [0]

                    def mark(ins):
                        done[0] += 1
                        ins.then_inc(S["dve"], 1)
                        return done[0]

                    def residual_of_attention():
                        dve.wait_ge(S["wo"], 1)
                        v.tensor_tensor(x8[:, NT:2 * NT, :], xkeep[:, 1 - par], ps[:, 4, :].rearrange(
                            "p (t d) -> p t d", t=NT), ALU.add).then_inc(S["x2"], 1)
                        dve.wait_ge(S["x2"], 1)

                    def stats_of(src, part):
                        for t in tiles[nt // 2 * part:nt // 2 * (part + 1)]:
                            stats_done[0] = mark(v.bn_stats(stats[:, t, :], src(t)))

                    def aggregate():
                        dve.wait_ge(S["dve"], stats_done[0])
                        for t in tiles:
                            n = mark(v.bn_aggr(mv[:, t, :], stats[:, t, :]))
                        dve.wait_ge(S["dve"], n)
                        v.tensor_scalar(nmean[:, a0:b0], mv[:, a0:b0, 0], -1.0, None, ALU.mult)
                        v.tensor_scalar(veps[:, a0:b0], mv[:, a0:b0, 1], LN_EPS, None, ALU.add).then_inc(S["var"], 1)

                    def residual(hf):
                        dve.wait_ge(S["h"], 1)
                        dst = ynew[:, par] if hf == 0 else yold[:, :, :]
                        v.tensor_tensor(dst, x8[:, NT * hf:NT * hf + NT, :], hh[:, NT * hf:NT * hf + NT, :],
                                        ALU.add).then_inc(S["y"], 1)

                    def gate_in():
                        dve.wait_ge(S["gate"], 1)
                        v.tensor_tensor(gl[:, :, :], ps[:, 4, 0:NT * EXPERTS].rearrange(
                            "p (t e) -> p t e", t=NT), w["gate_b"][:, :, :], ALU.add).then_inc(S["gate_read"], 1)

                    def product(m):
                        p, c = m // 2, m % 2
                        kq, g = p // NG, p % NG
                        dve.wait_ge(S["pair"], m + 1)
                        if c == 0 and p >= 2:
                            dve.wait_ge(S["lo"], p - 1)
                        v.tensor_tensor(terms[:, p % 2, c, :], ps[:, 4 + c, :], w["rope"][:, 2 * kq + c, g, :],
                                        ALU.mult).then_inc(S["pair_free"], 1)

                    def maximum(s, t):
                        n = job_of["tile", 4 * s + t]
                        dve.wait_ge(S["s"], n + 1)
                        v.tensor_reduce(mS[:, t, s:s + 1], ps[:, 2 + n % 2, :], AX, ALU.max).then_inc(S["s_read"], 1)

                    def guard_row(j):
                        n = job_of["guard", j]
                        dve.wait_ge(S["s"], n + 1)
                        if j == 1 and att:
                            dve.wait_ge(S["late"], 16 * 7)
                        if j >= 2:
                            dve.wait_ge(S["mrow_sent", j % 2], 16)
                        v.tensor_scalar(nm[:, j % 2, :], ps[0:NG, 2 + n % 2, :], -1.0, None, ALU.mult).then_inc(S["mrow"], 1)

                    def divide(j, part):
                        if part == 0:
                            if j < NG - 1:
                                dve.wait_ge(S["den"], j + 1)
                            dve.wait_ge(S["dve"], mark(v.transpose(denT[:, :], den[:, :])))
                            div_done[0] = mark(v.reciprocal(inv[:, :], denT[:, 0:SEQ:32]))
                        if part == 1:
                            dve.wait_ge(S["dve"], div_done[0])
                            dve.wait_ge(S["dve"], mark(v.tensor_copy(
                                denT[:, :].rearrange("p (b i) -> p b i", i=32),
                                inv[:, :].rearrange("p (b o) -> p b o", o=1).to_broadcast([P, SEQ // 32, 32]))))
                            div_done[0] = mark(v.transpose(den[:, :], denT[:, :]))
                        if part == 2:
                            dve.wait_ge(S["dve"], div_done[0])
                            v.tensor_tensor(oT[:, j, :], oT[:, j, :], den[:, :], ALU.mult).then_inc(
                                S["norm" if j < NG - 1 else "last_norm"], 1)

                    stats_done, div_done = [0], [0]
                    if first:
                        dve.wait_ge(S["x_first"], 16)
                    for q in range(NT * HEADS + 2):
                        s, t = q // NT, q % NT
                        if mid and s < HEADS:
                            maximum(s, t)
                        if mid and t == 0 and s and s % NG == 0:
                            guard_row(s // NG - 1)
                        if att and s % NG == 2 and s > NG and t < 3:
                            divide(s // NG - 1, t)
                        if old and q < 3:
                            divide(NG - 1, q)
                        if old and q == AT["x2"]:
                            residual_of_attention()
                        if new and q in product_at:
                            if first and product_at[q] == 0:
                                dve.wait_ge(S["rope_in"], 16)
                            product(product_at[q])
                        if first and q in (AT["turn1"], AT["ffn"] + 1, AT["squares_b"] + 1, AT["turn2"]):
                            j = (AT["turn1"], AT["ffn"] + 1, AT["squares_b"] + 1, AT["turn2"]).index(q)
                            v.memset(kst[3 * DH:STK, NG * j:NG * j + NG, :], 1.0)
                        if new or old:
                            for part in range(2):
                                if q == AT["stats1"] + part:
                                    stats_of(lambda t: x8[:, t, :], part)
                                if q == AT["stats2"] + part:
                                    dve.wait_ge(S["y"], nh)
                                    stats_of(after_ffn, part)
                            if q in (AT["aggr1"], AT["aggr2"]):
                                aggregate()
                            for k, hf in enumerate(halves):
                                if q == AT["resid"] + k:
                                    residual(hf)
                        if old:
                            if q == AT["gate_in"]:
                                gate_in()
                            if q == AT["gate_top"]:
                                dve.wait_ge(S["gate_read"], 1)
                                top_two(v, dve, S["dve"], mark, gl, g8, gix, gif)
                            if q == AT["gate_count"]:
                                count_choices(v, dve, S["dve"], mark, gif, onehot, w, cnt_acc)

                @block.scalar
                def _(act):
                    a = nc.scalar

                    def transposed(lap):
                        act.wait_ge(S["xT"], lap)
                        for hf in halves:
                            dst = xnTn[:, :] if hf == 0 else xnTo[:, :]
                            ins = a.copy(dst, ps[:, 4 + hf, :])
                        ins.then_inc(S["xnT"], 1)
                        if new and lap == 2:
                            if att:
                                act.wait_ge(S["v_ps"], NT)
                            a.copy(xnh[:, par], ps[:, 4, :]).then_inc(S["xnh"], 1)

                    def normalise(src, lap, part):
                        act.wait_ge(S["shift"], lap)
                        for t in tiles[nt // 4 * part:nt // 4 * (part + 1)]:
                            ins = a.activation(xn[:, t, :], src(t), ACT.Identity, scale=rstd[:, t:t + 1],
                                               bias=shift[:, t:t + 1])
                            if t == tiles[-1]:
                                ins.then_inc(S["xn"], 1)

                    def squares(k):
                        act.wait_ge(S["ff"], k + 1)
                        if k >= 2:
                            act.wait_ge(S["ss"], k - 1)
                        a.activation(sq[:, k % 2].rearrange("p t c d -> p (t c d)"), ps[:, 4 + k % 2, :],
                                     ACT.Square).then_inc(S["sq"], 1)

                    def high(p):
                        act.wait_ge(S["rot"], p + 1)
                        if p == 0 and att:
                            act.wait_ge(S["late"], 16 * 7)
                        a.copy(hi[:, par, p // NG, p % NG, :], terms[:, p % 2, 0, :]).then_inc(S["hi"], 1)

                    def numerators(j):
                        act.wait_ge(S["pv"], NG * (j + 1))
                        a.copy(oT[:, j, :], ps[:, 6, :]).then_inc(S["o"], 1)

                    def denominators(j):
                        if j < NG - 1:
                            act.wait_ge(S["dn"], 2 * (j + 1))
                        else:
                            act.wait_ge(S["dd"], NT)
                        if j:
                            act.wait_ge(S["norm"], j)
                        elif old:
                            act.wait_ge(S["last_norm"], 1)
                        a.copy(den[:, :], ps[:, 7, :]).then_inc(S["den"], 1)

                    for q in range(NT * HEADS + 8):
                        s, g = q // NG, q % NG
                        if att and s < HEADS:
                            if s >= 2:
                                if g == 0:
                                    act.wait_ge(S["pv"], s - 1)
                                if s % 2 == 0 and s < HEADS - 2:
                                    act.wait_ge(S["prs"], NG * (s // 2 - 1) + g + 1)
                                if s >= HEADS - 2 and g == 0:
                                    act.wait_ge(S["dd"], s + 3 - HEADS)
                            act.wait_ge(S["st"], q + 1)
                            a.activation(pr[:, s % 2, g, :], ps[:, g % 2, :], ACT.Exp,
                                         scale=ATT_SCALE).then_inc(S["exp"], 1)
                        if att and q in AT["values"]:
                            t = AT["values"].index(q)
                            act.wait_ge(S["v_ps"], t + 1)
                            a.copy(vt[:, t, :], ps[:, 5, :]).then_inc(S["v"], 1)
                        if att and s and s < HEADS and s % NG == 0 and g == 3:
                            numerators(s // NG - 1)
                        if att and s > NG and s < HEADS and s % NG == 1 and g == 2:
                            denominators(s // NG - 1)
                        if new or old:
                            for part in range(4):
                                if q == AT["xn1"] + part:
                                    normalise(lambda t: x8[:, t, :], 1, part)
                                if q == AT["xn2"] + part:
                                    if part == 0:
                                        act.wait_ge(S["y"], nh)
                                    normalise(after_ffn, 2, part)
                            if q == AT["evac1"]:
                                transposed(1)
                            if q == AT["squares"]:
                                for k in range(min(2, nt // 2)):
                                    squares(k)
                            if q == AT["squares_b"]:
                                for k in range(2, nt // 2):
                                    squares(k)
                            if q == AT["sqrt"]:
                                act.wait_ge(S["ss"], nt // 2)
                                a.activation(hh[:, a0:b0, :], hh[:, a0:b0, :], ACT.Sqrt, scale=0.25).then_inc(S["h"], 1)
                            if q == AT["evac2"]:
                                transposed(2)
                        if new and q in high_at:
                            high(high_at[q])
                    if att:
                        numerators(NG - 1)
                        denominators(NG - 1)

                @block.gpsimd
                def _(pool):
                    g = nc.gpsimd

                    def reciprocal_deviations(lap):
                        pool.wait_ge(S["var"], lap)
                        g.tensor_tensor(rstd[:, a0:b0], veps[:, a0:b0], w["minus_half"][:, a0:b0],
                                        ALU.pow).then_inc(S["rstd"], 1)
                        pool.wait_ge(S["rstd"], lap)
                        g.tensor_tensor(shift[:, a0:b0], nmean[:, a0:b0], rstd[:, a0:b0], ALU.mult).then_inc(S["shift"], 1)

                    def add_squares(k):
                        pool.wait_ge(S["sq"], k + 1)
                        t = tiles[2 * k]
                        g.tensor_tensor(hh[:, t:t + 2, :], sq[:, k % 2, :, 0, :], sq[:, k % 2, :, 1, :],
                                        ALU.add).then_inc(S["ss"], 1)

                    def add_pair(n, c):
                        pool.wait_ge(S["exp"], NG * (2 * n + 1) + c + 1)
                        if n:
                            pool.wait_ge(S["dn"], n)
                        g.tensor_tensor(prs[:, c, :], pr[:, 0, c, :], pr[:, 1, c, :], ALU.add).then_inc(S["prs"], 1)

                    def rotated(p):
                        pool.wait_ge(S["pair_free"], 2 * (p + 1))
                        g.tensor_tensor(terms[:, p % 2, 0, :], terms[:, p % 2, 0, :], terms[:, p % 2, 1, :],
                                        ALU.add).then_inc(S["rot"], 1)

                    def low(p):
                        pool.wait_ge(S["hi"], p + 1)
                        g.tensor_tensor(lo[:, par, p // NG, p % NG, :], terms[:, p % 2, 0, :],
                                        hi[:, par, p // NG, p % NG, :], ALU.subtract).then_inc(S["lo"], 1)

                    for q in range(NT * HEADS + 8):
                        if new or old:
                            if q == AT["aggr1"]:
                                reciprocal_deviations(1)
                            if q == AT["squares"]:
                                for k in range(min(2, nt // 2)):
                                    add_squares(k)
                            if q == AT["squares_b"]:
                                for k in range(2, nt // 2):
                                    add_squares(k)
                            if q == AT["aggr2"]:
                                reciprocal_deviations(2)
                        if mid and q == AT["keep"]:
                            if old:
                                pool.wait_ge(S["x2"], 1)
                            g.tensor_copy(xkeep[:, 1 - par], ynew[:, 1 - par])
                        if new:
                            if q == AT["evac2"]:
                                pool.wait_ge(S["xnh"], 1)
                                g.tensor_tensor(xnl[:, par], xnTn[:, :], xnh[:, par], ALU.subtract).then_inc(S["xnl"], 1)
                            if q in rotated_at:
                                rotated(rotated_at[q])
                            if q in low_at:
                                low(low_at[q])
                        s, c = (q - AT["add_lag"]) // NG, (q - AT["add_lag"]) % NG
                        if att and 0 < s < HEADS - NT and s % 2:
                            add_pair(s // 2, c)
                    if new:
                        pool.wait_ge(S["lo"], 2 * NG)

                @block.tensor
                def _(pe):
                    mm = nc.tensor.matmul

                    def transposes(lap):
                        pe.wait_ge(S["xn"], lap)
                        if lap == 1 and att:
                            pe.wait_ge(S["v"], NT)
                        if lap == 2:
                            pe.wait_ge(S["sq"], nt // 2)
                        for hf in halves:
                            for t in range(NT):
                                ins = nc.tensor.transpose(ps[:, 4 + hf, P * t:P * t + P], xn[:, NT * hf + t, :],
                                                          w["ident"][:, :])
                        ins.then_inc(S["xT"], 1)

                    def ffn(k):
                        if k < 2:
                            pe.wait_ge(S["xnT"], 1)
                        else:
                            pe.wait_ge(S["sq"], k - 1)
                        for u in range(2):
                            ins = mm(ps[:, 4 + k % 2, 256 * u:256 * u + 256], xnT_tile(tiles[2 * k + u]),
                                     w["csT"][:, :], start=True, stop=True)
                        ins.then_inc(S["ff"], 1)

                    def gate():
                        pe.wait_ge(S["xnT"], 2)
                        if new:
                            pe.wait_ge(S["xnh"], 1)
                        for t in range(NT):
                            ins = mm(ps[:, 4, EXPERTS * t:EXPERTS * t + EXPERTS], xnT_tile(NT + t),
                                     w["gwT"][:, :], start=True, stop=True)
                        ins.then_inc(S["gate"], 1)

                    def three_passes(out, lhs, rhs):
                        for k, (a, b) in enumerate(((0, 0), (0, 1), (1, 0))):
                            ins = mm(out, lhs[a], rhs[b], start=k == 0, stop=k == 2)
                        return ins

                    def project_values(t):
                        if t:
                            pe.wait_ge(S["v"], t)
                        xt = [x[:, par, P * t:P * t + P] for x in (xnh, xnl)]
                        three_passes(ps[:, 5, :], xt, [w["wv"][:, c, :] for c in range(2)]).then_inc(S["v_ps"], 1)

                    def output():
                        pe.wait_ge(S["last_norm"], 1)
                        for t in range(NT):
                            for j in range(NG):
                                ins = mm(ps[:, 4, P * t:P * t + P], oT[:, j, P * t:P * t + P], w["wo"][:, j, :],
                                         start=j == 0, stop=j == NG - 1)
                        ins.then_inc(S["wo"], 1)

                    def project(p, c):
                        kq, g = p // NG, p % NG
                        if c == 0:
                            if p == 0:
                                pe.wait_ge(S["xnl"], 1)
                                if old:
                                    pe.wait_ge(S["gate_read"], 1)
                        if p:
                            pe.wait_ge(S["pair_free"], 2 * p - 1 + c)
                        wt = [w["wq"][:, h, g, c, :] if kq == 0 else w["wk"][:, h, c, P * g:P * g + P] for h in range(2)]
                        three_passes(ps[:, 4 + c, :], wt, [xnh[:, par], xnl[:, par]]).then_inc(S["pair"], 1)

                    def shifted_scores(s, g):
                        j, kt = s // NT, s % NT
                        n = NG * s + g
                        if n >= 2:
                            pe.wait_ge(S["exp"], n - 1)
                        if n == NG * (HEADS - NT):
                            pe.wait_ge(S["late"], 16 * 7)
                        mm(ps[:, g % 2, :], kst[:, NG * j + g, P * kt:P * kt + P], qst[:, NG * j + g, :],
                           start=True, stop=True).then_inc(S["st"], 1)

                    def bank_read(n):
                        if n >= 2:
                            kind, m = jobs[n - 2]
                            pe.wait_ge(S["mrow" if kind == "guard" else "s_read"], m + 1)

                    def scores(s, t):
                        j, g = s // NG, s % NG
                        r = slice(DH * j, DH * j + DH)
                        n = job_of["tile", 4 * s + t]
                        bank_read(n)
                        mm(ps[:, 2 + n % 2, :], hi[r, 1 - par, 0, g, P * t:P * t + P], hi[r, 1 - par, 1, g, :],
                           start=True, stop=True).then_inc(S["s"], 1)

                    def guard_row(j):
                        n = job_of["guard", j]
                        pe.wait_ge(S["s_read"], 4 * NG * (j + 1))
                        bank_read(n)
                        for t in range(NT):
                            ins = nc.tensor.transpose(ps[0:NG, 2 + n % 2, P * t:P * t + P],
                                                      mS[:, t, NG * j:NG * j + NG], w["ident"][:, :])
                        ins.then_inc(S["s"], 1)

                    def values(s):
                        j, kt = s // NT, s % NT
                        pe.wait_ge(S["exp"], NG * (s + 1))
                        if s < NT:
                            pe.wait_ge(S["v"], kt + 1)
                        if kt == 0 and j:
                            pe.wait_ge(S["o"], j)
                        for g in range(NG):
                            h = NG * g + j
                            ins = mm(ps[DH * g:DH * g + DH, 6, :], vt[:, kt, DH * h:DH * h + DH], pr[:, s % 2, g, :],
                                     start=kt == 0, stop=kt == NT - 1, skip_group_check=True)
                        ins.then_inc(S["pv"], 1)

                    def denominators(n):
                        pe.wait_ge(S["prs"], NG * (n + 1))
                        if n % 2 == 0 and n:
                            pe.wait_ge(S["den"], n // 2)
                        for g in range(NG):
                            ins = mm(ps[DH * g:DH * g + DH, 7, :], w["ones"][:, 0:DH], prs[:, g, :],
                                     start=n % 2 == 0, stop=n % 2 == 1, skip_group_check=True)
                        ins.then_inc(S["dn"], 1)

                    def denominators_directly(s):
                        kt = s % NT
                        if kt == 0:
                            pe.wait_ge(S["den"], NG - 1)
                        for g in range(NG):
                            ins = mm(ps[DH * g:DH * g + DH, 7, :], w["ones"][:, 0:DH], pr[:, s % 2, g, :],
                                     start=kt == 0, stop=kt == NT - 1, skip_group_check=True)
                        ins.then_inc(S["dd"], 1)

                    for q in range(NT * HEADS):
                        s, t = q // NT, q % NT
                        if att:
                            shifted_scores(s, t)
                        if mid:
                            scores(s, t)
                            if t == 0 and s and s % NG == 0:
                                guard_row(s // NG - 1)
                        if att and s and t == 1:
                            values(s - 1)
                        n, lag = q // (2 * NT), q % (2 * NT)
                        if att and 0 < n < HEADS // 2 - 1 and lag == AT["denominators_lag"]:
                            denominators(n - 1)
                        if att and s > HEADS - NT and t == 3:
                            denominators_directly(s - 1)
                        if att and q in AT["values"]:
                            project_values(AT["values"].index(q))
                        if old and q == AT["output"]:
                            output()
                        if new or old:
                            if q == AT["turn1"]:
                                transposes(1)
                            if q == AT["ffn"]:
                                for k in range(min(2, nt // 2)):
                                    ffn(k)
                            if q == AT["ffn_b"]:
                                for k in range(2, nt // 2):
                                    ffn(k)
                            if q == AT["turn2"]:
                                transposes(2)
                        if old and q == AT["gate"]:
                            gate()
                        if new and q in AT["project"]:
                            project(AT["project"].index(q) // 2, AT["project"].index(q) % 2)
                    if mid:
                        guard_row(NG - 1)
                    if att:
                        values(NG * NT - 1)
                        denominators_directly(HEADS - 1)
            nc.gpsimd.sem_clear(range(nums[0], nums[-1] + 1))
            nc.all_engine_barrier(sem_only=True)

        def roles(i):
            return dict(new=i < BATCH, mid=1 <= i <= BATCH, att=2 <= i <= BATCH + 1, old=3 <= i, prefetch=i < BATCH - 1)

        for i in range(3):
            iteration(i, i % 2, **roles(i), first=i == 0)
        with nc.Fori(0, (BATCH - 4) // 2, 1) as k:
            iteration(k * 2 + 3, 1, **roles(3))
            iteration(k * 2 + 4, 0, **roles(4))
        for i in range(BATCH - 1, BATCH + 3):
            iteration(i, i % 2, **roles(i))


TWO_PI_HI = 6.28125
TWO_PI_LO = float(2 * np.pi - 6.28125)
ROUND = 1.5 * 2.0 ** 23
PI_F32 = 3.1415925


def reduce_angle(v, wait, r, k):
    wait(v.tensor_scalar(k, r, float(1 / (2 * np.pi)), ROUND, ALU.mult, ALU.add))
    wait(v.tensor_scalar(k, k, ROUND, None, ALU.subtract))
    wait(v.scalar_tensor_tensor(r, k, -TWO_PI_HI, r, ALU.mult, ALU.add))
    wait(v.scalar_tensor_tensor(r, k, -TWO_PI_LO, r, ALU.mult, ALU.add))
    return v.tensor_scalar(r, r, PI_F32, -PI_F32, ALU.min, ALU.max)


def consts_p1():
    return {
        "rope": rope_tables(),
        "ident": np.eye(P, dtype=np.float32),
        "iota": np.tile(np.arange(EXPERTS, dtype=np.float32), (P, NT, 1)),
    }


def layout_p1(x):
    wk = np.asarray(x["L0_attn_Wk"])
    wo = np.asarray(x["L0_attn_Wo"]).reshape(NG, NG, DH, 2, D)
    return {
        "q": np.asarray(x["L0_attn_q"]),
        "wq": np.asarray(x["L0_attn_Wq"]).reshape(D, NG, P, 2).transpose(0, 1, 3, 2),
        "wk": np.stack([wk, wk.reshape(D, KVD // 2, 2)[:, :, ::-1].reshape(D, KVD)], 1),
        "wv": np.asarray(x["L0_attn_Wv"]),
        "wo": wo.transpose(0, 2, 1, 3, 4).reshape(P, NG, 2, D),
        "angles": np.stack([np.asarray(x["L0_ffn_" + n]) for n in
                            ("theta", "theta_noise", "phi", "phi_noise")], 1),
        "gwT": np.asarray(x["L1_ffn_gate_w"]).T,
        "gate_b": np.broadcast_to(np.asarray(x["L1_ffn_gate_b"]), (P, NT, EXPERTS)),
    }


def load_layer0(nc, ctx, ins, cnt_acc):
    sb = lambda name, shape, dt=F32: ctx.enter_context(nc.sbuf_tensor(name, shape, dt))
    w = {"rope": sb("rope", [P, 4, NG, SEQ]), "wq": sb("wq", [P, 2, NG, 2, P], F16),
         "wk": sb("wk", [P, 2, 2, KVD], F16), "wv": sb("wv", [P, 2, KVD], F16), "wo": sb("wo", [P, NG, D]),
         "csT": sb("csT", [P, 2 * D]), "ones": sb("ones", [P, P]), "minus_half": sb("minus_half", [P, 8]),
         "ident": sb("ident", [P, P]), "gwT": sb("gwT", [P, EXPERTS]),
         "gate_b": sb("gate_b", [P, NT, EXPERTS]), "iota": sb("iota", [P, NT, EXPERTS])}
    with ExitStack() as tmp:
        sbt = lambda name, shape: tmp.enter_context(nc.sbuf_tensor(name, shape, F32))
        full = {"wq": sbt("wq32", [P, NG, 2, P]), "wk": sbt("wk32", [P, 2, KVD]), "wv": sbt("wv32", [P, KVD])}
        wo2, ang, red, k = sbt("wo2", [P, NG, 2, D]), sbt("ang", [P, 4, D]), sbt("red", [P, 2, D]), sbt("kk", [P, 2, D])
        angles_in, loaded, vd, sn = (tmp.enter_context(nc.semaphore("l_" + n)) for n in ("angles_in", "loaded", "dve", "sin"))
        names = ("wq", "wk", "wv", "ident", "gwT", "gate_b", "iota")
        with nc.Block(no_gpsimd_drain=True) as block:
            @block.sync
            def _(sp):
                sp.dma_start(ang[:], ins["angles"]).then_inc(angles_in, 16)
                sp.dma_start(wo2[:], ins["wo"]).then_inc(loaded, 16)
                for n in names:
                    sp.dma_start(full.get(n, w[n])[:], ins[n]).then_inc(loaded, 16)

            @block.vector
            def _(dve):
                v, n = nc.vector, [0]

                def wait(i):
                    n[0] += 1
                    i.then_inc(vd, 1)
                    dve.wait_ge(vd, n[0])
                v.memset(w["ones"][:, :], 1.0)
                v.memset(w["minus_half"][:, :], -0.5)
                v.memset(cnt_acc[:, :], 0.0)
                dve.wait_ge(angles_in, 16)
                wait(v.tensor_tensor(red[:, :, :], ang[:, 0:4:2, :], ang[:, 1:4:2, :], ALU.add))
                wait(v.tensor_scalar(red[:, 0, :], red[:, 0, :], float(np.pi) / 2, None, ALU.add))
                wait(reduce_angle(v, wait, red[:, :, :], k[:, :, :]))
                dve.wait_ge(loaded, 16 * (len(names) + 1))
                wait(v.tensor_tensor(w["wo"][:, :, :], wo2[:, :, 0, :], wo2[:, :, 1, :], ALU.add))
                v.tensor_scalar(w["wo"][:, :, :], w["wo"][:, :, :], 1.0 / W_SCALE, None, ALU.mult)
                for name in ("wq", "wk", "wv"):
                    flat = {"wq": "p g c n -> p (g c n)", "wk": "p c n -> p (c n)", "wv": "p n -> p n"}[name]
                    f = full[name][:].rearrange(flat)
                    h, l = (w[name][:, c].rearrange(flat) for c in range(2))
                    wait(v.tensor_scalar(f, f, W_SCALE, None, ALU.mult))
                    wait(v.tensor_copy(h, f))
                    v.tensor_tensor(l, f, h, ALU.subtract)

            @block.scalar
            def _(act):
                act.wait_ge(vd, 7)
                nc.scalar.activation(w["csT"][:, :], red[:, :, :].rearrange("p c d -> p (c d)"), ACT.Sin).then_inc(sn, 1)
        nums = [s.num for s in (angles_in, loaded, vd, sn)]
        nc.gpsimd.sem_clear(range(min(nums), max(nums) + 1))
        nc.all_engine_barrier(sem_only=True)
    return w


N_STATE, R, HP, M_HEADS = 64, 2, 8, 32
D_INNER = M_HEADS * HP
BLK = 32
RMS_EPS = 1e-6
STATE_SCALE = float((N_STATE * R) ** -0.5)
CLAMP = 85.0
DT_MIN, DT_MAX = 1e-4, 0.5
MID, REF1, REF_END, IN_BLOCK, FROM_START, WHOLE = 0, 1, 4, 5, 6, 7


def decay_sums():
    j, m = np.arange(P)[:, None], np.arange(P)[None, :]
    mid = BLK * (m // BLK) + BLK // 2 - 1
    sums = [((j > m) & (j <= mid)) * 1.0 - ((j > mid) & (j <= m)) * 1.0]
    sums += [(j > m) & (j < BLK * i) for i in (1, 2, 3)]
    sums += [j > m, (j <= m) & (j >= BLK * (m // BLK)), j <= m, j >= 0 * m]
    return np.stack([np.broadcast_to(s, (P, P)).astype(np.float32) for s in sums], 1)


def consts_p2():
    j, m = np.arange(P)[:, None], np.arange(P)[None, :]
    same = j // BLK == m // BLK
    tri = (j <= m).astype(np.float32)
    one = np.ones((P, P), np.float32)
    return {
        "sums": decay_sums(),
        "moves": np.stack([tri, one, (j == m + 1).astype(np.float32),
                           ((j == 0) & (m == P - 1)).astype(np.float32)], 1),
        "masks": np.stack([(same & (m > j)), (m // BLK > j // BLK)], 1).astype(np.float32),
    }


def layout_p2(x):
    w = np.asarray(x["L1_attn_W_in"])
    z, xr, rest, th = w[:, :256], w[:, 256:768], w[:, 768:1024], w[:, 1024:]
    rep = lambda a: np.broadcast_to(np.asarray(a), (P, NT, M_HEADS))
    b, c = np.asarray(x["L1_attn_B_norm_bias"])[0], np.asarray(x["L1_attn_C_norm_bias"])[0]
    return {
        "w_in": np.concatenate([xr, z, rest, th], 1),
        "w_out": np.asarray(x["L1_attn_W_out"]).reshape(2, P, D).transpose(1, 0, 2),
        "a_log": rep(x["L1_attn_A_log"]), "dt_bias": rep(x["L1_attn_dt_bias"]),
        "bc_bias": np.broadcast_to(np.stack([b, b, c]), (P, 3, N_STATE)),
        "ew": np.asarray(x["L1_ffn_expert_w"]).transpose(2, 0, 1),
        "eb": np.asarray(x["L1_ffn_expert_b"]).T,
    }


def load_layer1(nc, ctx, ins):
    sb = lambda name, shape: ctx.enter_context(nc.sbuf_tensor(name, shape, F32))
    w = {"w_in": sb("w_in", [P, 1056]), "w_out": sb("w_out", [P, 2, D]), "a_log": sb("a_log", [P, NT, M_HEADS]),
         "dt_bias": sb("dt_bias", [P, NT, M_HEADS]), "bc_bias": sb("bc_bias", [P, 3, N_STATE]),
         "ew": sb("ew", [P, EXPERTS, D]), "eb": sb("eb", [P, EXPERTS]), "sums": sb("sums", [P, 8, P]),
         "moves": sb("moves", [P, 4, P]), "masks": sb("masks", [P, 2, P]),
         "ident": sb("ident1", [P, P]), "gwT": sb("gwT1", [P, EXPERTS]),
         "gate_b": sb("gate_b1", [P, NT, EXPERTS]), "iota": sb("iota1", [P, NT, EXPERTS])}
    names = list(w)
    w["a"] = sb("a", [P, NT, M_HEADS])
    w["minus_half"] = sb("minus_half1", [P, NT * 3])
    with ExitStack() as tmp:
        loaded, vd, ex = (tmp.enter_context(nc.semaphore("k_" + n)) for n in ("loaded", "dve", "exp"))
        with nc.Block(no_gpsimd_drain=True) as block:
            @block.sync
            def _(sp):
                for n in names:
                    sp.dma_start(w[n][:], ins[n]).then_inc(loaded, 16)

            @block.scalar
            def _(act):
                act.wait_ge(loaded, 16 * len(names))
                nc.scalar.activation(w["a"][:], w["a_log"][:], ACT.Exp).then_inc(ex, 1)

            @block.vector
            def _(dve):
                nc.vector.memset(w["minus_half"][:, :], -0.5)
                dve.wait_ge(ex, 1)
                nc.vector.tensor_scalar(w["a"][:], w["a"][:], -1.0, None, ALU.mult)
                nc.vector.tensor_scalar(w["bc_bias"][:, 2, :], w["bc_bias"][:, 2, :], STATE_SCALE, None, ALU.mult)
        nums = (loaded.num, vd.num, ex.num)
        nc.gpsimd.sem_clear(range(min(nums), max(nums) + 1))
        nc.all_engine_barrier(sem_only=True)
    return w


def expert_weights(nc, tag, w, cnt_acc, ew):
    with ExitStack() as tmp:
        share = tmp.enter_context(nc.sbuf_tensor(tag + "share", [P, EXPERTS], F32))
        pc = tmp.enter_context(nc.psum_tensor(tag + "pc", [P, NT * TOPK * EXPERTS], F32))
        counted, vd = (tmp.enter_context(nc.semaphore(tag + n)) for n in ("counted", "dve"))
        with nc.Block(no_gpsimd_drain=True) as block:
            @block.tensor
            def _(pe):
                nc.tensor.matmul(pc[:, :], w["moves"][:, 1, :], cnt_acc[:, :], start=True, stop=True).then_inc(counted, 1)

            @block.vector
            def _(dve):
                v, n = nc.vector, [0]

                def wait(i):
                    n[0] += 1
                    i.then_inc(vd, 1)
                    dve.wait_ge(vd, n[0])
                dve.wait_ge(counted, 1)
                wait(v.tensor_reduce(share[:, :], pc[:, :].rearrange("p (a e) -> p e a", e=EXPERTS), AX, ALU.add))
                wait(v.tensor_scalar(share[:, :], share[:, :], 0.5 / (BATCH * SEQ * TOPK), None, ALU.mult))
                v.tensor_tensor(ew["w"][:, :, :], w["ew"][:, :, :],
                                share[:, :].rearrange("p (e o) -> p e o", o=1).to_broadcast([P, EXPERTS, D]), ALU.mult)
                wait(v.tensor_tensor(ew["posb"][:, :], w["eb"][:, :], share[:, :], ALU.mult))
                v.tensor_reduce(ew["sumb_all"][:, :], ew["posb"][:, :], AX, ALU.add)
                v.tensor_reduce(ew["sumb"][:, :], ew["posb"][:, 0:EXPERTS:2], AX, ALU.add)
                wait(v.tensor_scalar(ew["negb"][:, :], ew["posb"][:, :], -1.0, None, ALU.mult))
                v.memset(cnt_acc[:, :], 0.0)
        nc.gpsimd.sem_clear(range(min(counted.num, vd.num), max(counted.num, vd.num) + 1))
        nc.all_engine_barrier(sem_only=True)


MIXER_AT = {
    "turn_yz": (0, 2), "wo": 2, "out": 3, "stats_gate": 4, "xn_gate": 4, "turn_gate": 5, "gate": 6, "top": 6,
    "variants": (0, 2, 5, 14), "variants_p": (0, 1, 4, 16), "chunks": (4, 9, 12, 27), "outputs": (4, 9, 18, 28),
    "output_sums": (4, 9, 19, 31),
    "stats": 0, "xn": 3, "turn": 4, "experts": (7, 8, 10, 11, 13, 17, 20, 21), "sum": 21, "y": 23, "stats2": 26,
    "xn2": 30, "turn2": 33,
    "project": (0, 3, 4, 5), "shift": 6, "norm_bc": 16, "soft": 8, "keep": 15, "rates": 9, "steps": 10, "sums": 13,
    "angles": 17, "weights": 20, "rotate_p": 22, "rotate": 22, "bt": 29, "diagonal_p": 24, "diagonal": 25,
    "scores": 32,
}


def mixer_phase(nc, x_in, x_out, w, ew, cnt_acc):
    with ExitStack() as ctx:
        def sb(name, shape, dt=F32):
            return ctx.enter_context(nc.sbuf_tensor("m_" + name, shape, dt))

        x, y, y2 = (sb(n, [P, NT, D]) for n in ("x", "y", "y2"))
        ykeep = sb("ykeep", [P, 2, NT, D])
        stats, mv = sb("stats", [P, 2, NT, 6]), sb("mv", [P, 2, NT, 2])
        veps, rstd = sb("veps", [P, 2, NT]), sb("rstd", [P, 2, NT])
        nmean, shift = sb("nmean", [P, 2, NT]), sb("shift", [P, 2, NT])
        xn, xnT = sb("xn", [P, 2, NT, D]), sb("xnT", [P, 3, SEQ])
        acc, rl = sb("acc", [P, 2, SEQ]), sb("rl", [P, EXPERTS // 2, SEQ])
        xr, zs = sb("xr", [P, 2, NT, M_HEADS, R, HP]), sb("zs", [P, 2, NT, D_INNER])
        bcdl, th = sb("bcdl", [P, NT, 256]), sb("th", [P, NT, M_HEADS])
        bc = bcdl[:, :, 0:3 * N_STATE].rearrange("p t (c n) -> p t c n", c=3)
        dt_raw, lam_raw = bcdl[:, :, 3 * N_STATE:3 * N_STATE + M_HEADS], bcdl[:, :, 256 - M_HEADS:256]
        t_dt, dt = sb("t_dt", [P, NT, M_HEADS]), sb("dt", [P, NT, M_HEADS])
        lam, gam, bet = sb("lam", [P, NT, M_HEADS]), sb("gam", [P, NT, M_HEADS]), sb("bet", [P, NT, M_HEADS])
        wgt, lda, md = sb("wgt", [P, NT, M_HEADS]), sb("lda", [P, NT, M_HEADS]), sb("md", [P, NT])
        mid = sb("mid", [P, 2, NT, M_HEADS])
        dec = sb("dec", [P, 2, 9, NT, M_HEADS])
        coef = sb("coef", [P, 2, 6, NT, M_HEADS])
        ang, angk, sc = (sb(n, [P, 2, NT, M_HEADS]) for n in ("ang", "angk", "sc"))
        sqb, bcn = sb("sqb", [P, NT, 3, N_STATE]), sb("bcn", [P, NT, 3, N_STATE])
        rbc = sb("rbc", [P, NT * 3])
        rbc4 = rbc[:, :].rearrange("p (t c o) -> p t c o", t=NT, o=1).to_broadcast([P, NT, 3, N_STATE])
        br = sb("br", [P, 2, NT, 4, N_STATE])
        rp = sb("rp", [P, 4, NT, 3, N_STATE // 2])
        bt = sb("bt", [P, 2, NT, 2, P])
        gs, gt = (sb(n, [P, 2, NT, R, P]) for n in ("gs", "gt"))
        gdp, gd = sb("gdp", [P, NT, R, N_STATE]), sb("gd", [P, 2, NT, R])
        zero = sb("zero", [BLK, BLK])
        xv = sb("xv", [P, 2, 6, M_HEADS, R, HP])
        state = sb("state", [N_STATE, M_HEADS, HP])
        part = sb("part", [P, 2, 4, M_HEADS, HP])
        yz, yy = sb("yz", [P, 2, NT, D_INNER]), sb("yy", [P, D_INNER])
        ms, rms, yzT = sb("ms", [P, NT]), sb("rms", [P, 2, NT]), sb("yzT", [P, NT, 2, P])
        gl, g8 = sb("gl", [P, NT, EXPERTS]), sb("g8", [P, NT, 8])
        gix, gif = sb("gix", [P, NT, 8], U32), sb("gif", [P, NT, TOPK])
        onehot = sb("onehot", [P, NT, TOPK, EXPERTS])
        ps = ctx.enter_context(nc.psum_tensor("m_ps", [P, 8, 512], F32))

        names = ("x_in", "x_out", "dve", "pool", "act", "var", "rstd", "xn", "xT", "xnT", "ex", "relu", "ex_v",
                 "added", "sum", "y", "kept", "pr_x", "pr_z", "ev_x", "ev_z", "ev_th", "u", "soft", "dtl",
                 "beta", "prep_ps", "sq", "ms_bc", "bcn", "ang", "sin", "mid", "dec", "rp_p", "br", "gdp",
                 "bt_ps", "bt", "g_ps", "gs", "gt", "xv_v", "xv_p", "ymm", "y_read", "st_mm", "state", "yz",
                 "ms", "rms", "yzT_ps", "yzT", "th_ps", "wo", "y2", "var2", "rstd2", "xn2", "xT2", "xnT2", "gate",
                 "gate_read")
        S = {n: ctx.enter_context(nc.semaphore("m_" + n)) for n in names}
        nums = sorted(s.num for s in S.values())
        assert nums[-1] - nums[0] + 1 == len(nums)

        AT = MIXER_AT
        SLOTS = 1 + max(max(a) if isinstance(a, tuple) else a for a in AT.values())

        def iteration(i, par, ffn, prep, scan, tail, prefetch):
            pp = 1 - par

            with nc.Block(no_gpsimd_drain=True) as block:
                @block.sync
                def _(sp):
                    if prefetch:
                        sp.wait_ge(S["y"], 1)
                        sp.dma_start(x[:, :, :], x_in[bass.ds(i + 1, 1)].rearrange(
                            "b (t p) d -> p (b t) d", p=P)).then_inc(S["x_in"], 16)
                    if tail:
                        sp.wait_ge(S["y2"], NT)
                        sp.dma_start(x_out[bass.ds(i - 3, 1)].rearrange("b (t p) d -> p (b t) d", p=P),
                                     y2[:, :, :]).then_inc(S["x_out"], 16)
                        sp.wait_ge(S["x_out"], 16)
                    if prefetch:
                        sp.wait_ge(S["x_in"], 16)

                @block.vector
                def _(dve):
                    v, done = nc.vector, [0]

                    def mark(ins):
                        done[0] += 1
                        ins.then_inc(S["dve"], 1)
                        return done[0]

                    def wait(ins):
                        dve.wait_ge(S["dve"], mark(ins))

                    def statistics(src, k, var):
                        for t in range(NT):
                            n = mark(v.bn_stats(stats[:, k, t, :], src[:, t, :]))
                        dve.wait_ge(S["dve"], n)
                        for t in range(NT):
                            n = mark(v.bn_aggr(mv[:, k, t, :], stats[:, k, t, :]))
                        dve.wait_ge(S["dve"], n)
                        v.tensor_scalar(nmean[:, k, :], mv[:, k, :, 0], -1.0, None, ALU.mult)
                        v.tensor_scalar(veps[:, k, :], mv[:, k, :, 1], LN_EPS, None, ALU.add).then_inc(var, 1)

                    def expert(e):
                        n = e // 2
                        dve.wait_ge(S["ex"], e + 1)
                        if n == 0:
                            ins = v.tensor_scalar(acc[:, 0, :], ps[:, 0, :], ew["negb"][:, 0:1], ew["sumb"][:, 0:1],
                                                  ALU.max, ALU.add)
                        else:
                            dve.wait_ge(S["ex_v"], n)
                            ins = v.scalar_tensor_tensor(acc[:, n % 2, :], ps[:, 0, :], ew["negb"][:, e:e + 1],
                                                         acc[:, (n - 1) % 2, :], ALU.max, ALU.add)
                        ins.then_inc(S["ex_v"], 1)

                    def shift_dt():
                        dve.wait_ge(S["ev_z"], NT)
                        wait(v.tensor_tensor(t_dt[:, :, :], dt_raw, w["dt_bias"][:, :, :], ALU.add))
                        v.tensor_scalar(t_dt[:, :, :], t_dt[:, :, :], 0.0, None, ALU.min).then_inc(S["u"], 1)
                        dve.wait_ge(S["sq"], 1)
                        wait(v.tensor_reduce(rbc[:, :], sqb[:, :, :, :].rearrange("p t c n -> p (t c) n"), AX, ALU.add))
                        v.tensor_scalar(rbc[:, :], rbc[:, :], 1.0 / N_STATE, RMS_EPS, ALU.mult,
                                        ALU.add).then_inc(S["ms_bc"], 1)

                    def steps():
                        dve.wait_ge(S["soft"], 1)
                        wait(v.tensor_scalar(dt[:, :, :], dt[:, :, :], DT_MIN, DT_MAX, ALU.max, ALU.min))
                        v.tensor_tensor(lda[:, :, :], dt[:, :, :], w["a"][:, :, :], ALU.mult)
                        n = mark(v.tensor_reduce(md[:, :], dt[:, :, :], AX, ALU.add))
                        wait(v.tensor_scalar(lam[:, :, :], lam[:, :, :], 1.0, None, ALU.add))
                        wait(v.tensor_scalar(md[:, :], md[:, :], -1.0 / M_HEADS, None, ALU.mult))
                        dve.wait_ge(S["ev_th"], 1)
                        v.tensor_tensor(th[:, :, :], th[:, :, :], md[:, :].rearrange(
                            "p (t o) -> p t o", o=1).to_broadcast([P, NT, M_HEADS]), ALU.mult).then_inc(S["dtl"], 1)
                        wait(v.reciprocal(lam[:, :, :], lam[:, :, :]))
                        wait(v.tensor_tensor(gam[:, :, :], lam[:, :, :], dt[:, :, :], ALU.mult))
                        v.tensor_tensor(bet[:, :, :], dt[:, :, :], gam[:, :, :], ALU.subtract).then_inc(S["beta"], 1)

                    def angles():
                        dve.wait_ge(S["prep_ps"], 1)
                        pa = ps[:, 5, 128:256].rearrange("p (t h) -> p t h", t=NT)
                        v.tensor_scalar(mid[:, 0], ps[:, 3, 0:128].rearrange("p (t h) -> p t h", t=NT),
                                        CLAMP, None, ALU.min)
                        v.tensor_scalar(mid[:, 1], ps[:, 3, 0:128].rearrange("p (t h) -> p t h", t=NT),
                                        -CLAMP, None, ALU.max).then_inc(S["mid"], 1)
                        v.tensor_copy(ang[:, 0], pa)
                        wait(v.tensor_scalar(ang[:, 1], pa, float(np.pi) / 2, None, ALU.add))
                        reduce_angle(v, wait, ang[:, :], angk[:, :]).then_inc(S["ang"], 1)

                    def source_weights():
                        wait(v.tensor_tensor(wgt[:, :, :], gam[:, :, :], ps[:, 5, 256:384].rearrange(
                            "p (t h) -> p t h", t=NT), ALU.add))
                        dve.wait_ge(S["dec"], 1)
                        v.tensor_copy(coef[:, pp, 5], gam[:, :, :])
                        mark(v.tensor_tensor(
                            coef[:, pp, 0:5].rearrange("p c t h -> p c (t h)"),
                            dec[:, pp, 0:5].rearrange("p c t h -> p c (t h)"),
                            wgt[:, :, :].rearrange("p (o t) h -> p o (t h)", o=1).to_broadcast([P, 5, NT * M_HEADS]),
                            ALU.mult))

                    half = N_STATE // 2

                    def rotate():
                        dve.wait_ge(S["sin"], 1)
                        dve.wait_ge(S["bcn"], 1)
                        for c, (s0, k) in enumerate(((0, 1), (half, 0))):
                            n = mark(v.tensor_tensor(rp[:, c], bcn[:, :, :, s0:s0 + half],
                                                     sc[:, k].rearrange("p t (o n) -> p t o n", o=1).to_broadcast(
                                                         [P, NT, 3, half]), ALU.mult))
                        dve.wait_ge(S["dve"], n)
                        wait(v.tensor_tensor(br[:, pp, :, 0:3, 0:half], rp[:, 0], rp[:, 1], ALU.subtract))
                        dve.wait_ge(S["rp_p"], 1)
                        v.tensor_copy(br[:, pp, :, 3, :], br[:, pp, :, 2, :]).then_inc(S["br"], 1)

                    def diagonal():
                        dve.wait_ge(S["gdp"], 1)
                        mark(v.tensor_reduce(gd[:, pp], gdp[:, :, :, :], AX, ALU.add))

                    def mask_scores():
                        dve.wait_ge(S["g_ps"], 1)
                        dve.wait_ge(S["gt"], 2)
                        for r in range(R):
                            v.tensor_tensor(gs[:, pp, :, r, :], ps[:, 3 + r, :].rearrange("p (a m) -> p a m", a=4),
                                            w["masks"][:, 0:1, :].to_broadcast([P, 4, P]), ALU.mult).then_inc(S["gs"], 1)

                    def variants(t):
                        if t >= 2:
                            dve.wait_ge(S["ymm"], t - 1)
                        for c in (MID, REF1, REF1 + 1):
                            ins = v.tensor_tensor(xv[:, t % 2, c].rearrange("p h r q -> p h (r q)"),
                                                  xr[:, par, t].rearrange("p h r q -> p h (r q)"),
                                                  coef[:, par, c, t, :].rearrange("p (h o) -> p h o", o=1).to_broadcast(
                                                      [P, M_HEADS, R * HP]), ALU.mult)
                        ins.then_inc(S["xv_v"], 1)

                    def row(c, t, rows=P):
                        return dec[0:rows, par, c, t, :].rearrange("p (h o) -> p h o", o=1).to_broadcast(
                            [rows, M_HEADS, HP])

                    def halfbank(k, o, rows=P):
                        return ps[0:rows, k, o:o + 256].rearrange("p (h q) -> p h q", q=HP)

                    def read_outputs(t):
                        pt = part[:, t % 2]
                        dve.wait_ge(S["ymm"], t + 1)
                        v.tensor_tensor(pt[:, 0], halfbank(6, 0), row(8, t), ALU.mult)
                        ins = v.tensor_tensor(pt[:, 1], halfbank(6, 256), row(IN_BLOCK, t), ALU.mult)
                        if t < NT - 1:
                            dve.wait_ge(S["st_mm"], t + 1)
                        if t:
                            ins = v.tensor_tensor(pt[:, 2], halfbank(7, 0), row(FROM_START, t), ALU.mult)
                        ins.then_inc(S["y_read"], 1)
                        if t == 0:
                            v.tensor_copy(state[:, :, :], halfbank(7, 256, N_STATE)).then_inc(S["state"], 1)
                        elif t < NT - 1:
                            dve.wait_ge(S["state"], t)
                            wait(v.tensor_tensor(part[0:N_STATE, t % 2, 3], state[:, :, :],
                                                 row(WHOLE, t, N_STATE), ALU.mult))
                            v.tensor_tensor(state[:, :, :], part[0:N_STATE, t % 2, 3], halfbank(7, 256, N_STATE),
                                            ALU.add).then_inc(S["state"], 1)

                    def sum_outputs(t):
                        pt = part[:, t % 2]
                        dve.wait_ge(S["y_read"], t + 1)
                        wait(v.tensor_tensor(pt[:, 1], pt[:, 0], pt[:, 1], ALU.add))
                        if t:
                            wait(v.tensor_tensor(pt[:, 1], pt[:, 1], pt[:, 2], ALU.add))
                        dve.wait_ge(S["xv_p"], t + 1)
                        for r in range(R):
                            wait(v.scalar_tensor_tensor(pt[:, r], xv[:, t % 2, 5, :, r, :], gd[:, par, t, r:r + 1],
                                                        pt[:, 1 - r], ALU.mult, ALU.add))
                        v.tensor_tensor(yz[:, par, t, :], pt[:, 1].rearrange("p h q -> p (h q)"), zs[:, par, t, :],
                                        ALU.mult).then_inc(S["yz"], 1)
                        dve.wait_ge(S["yz"], t + 1)
                        n = mark(v.tensor_tensor_reduce(yy[:, :], yz[:, par, t, :], yz[:, par, t, :], 1.0, 0.0,
                                                        ALU.mult, ALU.add, ms[:, t:t + 1]))
                        if t == NT - 1:
                            dve.wait_ge(S["dve"], n)
                            v.tensor_scalar(ms[:, :], ms[:, :], 1.0 / D_INNER, RMS_EPS, ALU.mult,
                                            ALU.add).then_inc(S["ms"], 1)

                    for q in range(SLOTS):
                        if tail:
                            if q == AT["out"]:
                                dve.wait_ge(S["wo"], 1)
                                for t in range(NT):
                                    v.scalar_tensor_tensor(y2[:, t, :], ps[:, 5, P * t:P * t + P],
                                                           rms[:, pp, t:t + 1], ykeep[:, pp, t, :],
                                                           ALU.mult, ALU.add).then_inc(S["y2"], 1)
                            if q == AT["stats_gate"]:
                                dve.wait_ge(S["y2"], NT)
                                statistics(y2, 1, S["var2"])
                            if q == AT["gate"]:
                                dve.wait_ge(S["gate"], 1)
                                v.tensor_tensor(gl[:, :, :], ps[:, 5, 0:NT * EXPERTS].rearrange(
                                    "p (t e) -> p t e", t=NT), w["gate_b"][:, :, :], ALU.add).then_inc(S["gate_read"], 1)
                            if q == AT["top"]:
                                dve.wait_ge(S["gate_read"], 1)
                                top_two(v, dve, S["dve"], mark, gl, g8, gix, gif)
                                count_choices(v, dve, S["dve"], mark, gif, onehot, w, cnt_acc)
                        if scan:
                            if q in AT["variants"]:
                                variants(AT["variants"].index(q))
                            if q in AT["outputs"]:
                                read_outputs(AT["outputs"].index(q))
                            if q in AT["output_sums"]:
                                sum_outputs(AT["output_sums"].index(q))
                        if ffn:
                            if q == AT["stats"]:
                                statistics(x, 0, S["var"])
                            if q in AT["experts"] and AT["experts"].index(q) % 2 == 0:
                                expert(AT["experts"].index(q))
                            if q == AT["y"]:
                                dve.wait_ge(S["sum"], 1)
                                if prep:
                                    dve.wait_ge(S["kept"], 1)
                                v.tensor_tensor(y[:, :, :], x[:, :, :], ps[:, 2, :].rearrange(
                                    "p (t d) -> p t d", t=NT), ALU.add).then_inc(S["y"], 1)
                            if q == AT["stats2"]:
                                dve.wait_ge(S["y"], 1)
                                statistics(y, 0, S["var"])
                        if prep:
                            if q == AT["shift"]:
                                shift_dt()
                            if q == AT["steps"]:
                                steps()
                            if q == AT["angles"]:
                                angles()
                            if q == AT["weights"]:
                                source_weights()
                            if q == AT["rotate"]:
                                rotate()
                            if q == AT["diagonal"]:
                                diagonal()
                            if q == AT["scores"]:
                                mask_scores()

                @block.scalar
                def _(act):
                    a = nc.scalar

                    def evacuate(t):
                        act.wait_ge(S["pr_x"], t + 1)
                        a.activation(xr[:, pp, t].rearrange("p h r q -> p (h r q)"), ps[:, 3, :],
                                     ACT.Silu).then_inc(S["ev_x"], 1)
                        act.wait_ge(S["pr_z"], t + 1)
                        a.activation(zs[:, pp, t, :], ps[:, 4, 0:256], ACT.Silu)
                        a.copy(bcdl[:, t, :], ps[:, 4, 256:512]).then_inc(S["ev_z"], 1)

                    def normalise(src, k, xn_ready):
                        for t in range(NT):
                            ins = a.activation(xn[:, k, t, :], src[:, t, :], ACT.Identity, scale=rstd[:, k, t:t + 1],
                                               bias=shift[:, k, t:t + 1])
                        ins.then_inc(xn_ready, 1)

                    def turn(lap):
                        act.wait_ge(S["xT"], lap)
                        if lap == 2 and prep:
                            act.wait_ge(S["ev_z"], NT)
                        a.copy(xnT[:, lap - 1, :], ps[:, 2, :]).then_inc(S["xnT"], 1)

                    for q in range(SLOTS):
                        if tail:
                            if q in AT["turn_yz"]:
                                k = AT["turn_yz"].index(q)
                                act.wait_ge(S["yzT_ps"], k + 1)
                                a.copy(yzT[:, 2 * k:2 * k + 2], ps[:, 5, :].rearrange(
                                    "p (t c m) -> p t c m", t=2, c=2)).then_inc(S["yzT"], 1)
                            if q == AT["xn_gate"]:
                                act.wait_ge(S["rstd2"], 1)
                                normalise(y2, 1, S["xn2"])
                            if q == AT["turn_gate"]:
                                act.wait_ge(S["xT2"], 1)
                                a.copy(xnT[:, 2, :], ps[:, 5, :]).then_inc(S["xnT2"], 1)
                        if ffn:
                            if q == AT["xn"]:
                                act.wait_ge(S["rstd"], 1)
                                normalise(x, 0, S["xn"])
                            if q == AT["turn"]:
                                turn(1)
                            if q in AT["experts"] and AT["experts"].index(q) % 2:
                                e = AT["experts"].index(q)
                                act.wait_ge(S["ex"], e + 1)
                                a.activation(rl[:, e // 2, :], ps[:, 1, :], ACT.Relu,
                                             bias=ew["posb"][:, e:e + 1]).then_inc(S["relu"], 1)
                            if q == AT["xn2"]:
                                act.wait_ge(S["rstd"], 2)
                                normalise(y, 0, S["xn"])
                            if q == AT["turn2"]:
                                turn(2)
                        if prep:
                            if q in AT["project"]:
                                evacuate(AT["project"].index(q))
                            if q == AT["shift"]:
                                act.wait_ge(S["ev_z"], NT)
                                a.activation(sqb[:, :, :, :], bc, ACT.Square).then_inc(S["sq"], 1)
                            if q == AT["soft"]:
                                a.activation(lam[:, :, :], lam_raw, ACT.Exp, scale=-1.0)
                                act.wait_ge(S["u"], 1)
                                a.activation(dt[:, :, :], t_dt[:, :, :], ACT.Exp).then_inc(S["act"], 1)
                                act.wait_ge(S["act"], 1)
                                a.activation(dt[:, :, :], dt[:, :, :], ACT.Ln, bias=1.0).then_inc(S["soft"], 1)
                            if q == AT["rates"]:
                                act.wait_ge(S["th_ps"], 1)
                                a.copy(th[:, :, :], ps[:, 5, 0:NT * M_HEADS].rearrange(
                                    "p (t h) -> p t h", t=NT)).then_inc(S["ev_th"], 1)
                            if q == AT["angles"]:
                                act.wait_ge(S["prep_ps"], 1)
                                act.wait_ge(S["mid"], 1)
                                a.activation(dec[:, pp, 0], mid[:, 0], ACT.Exp)
                                a.activation(dec[:, pp, 8], mid[:, 1], ACT.Exp, scale=-1.0)
                                a.activation(dec[:, pp, 1:4].rearrange("p c t h -> p (c t h)"), ps[:, 3, 128:512], ACT.Exp)
                                a.activation(dec[:, pp, 4:8].rearrange("p c t h -> p (c t h)"), ps[:, 4, :],
                                             ACT.Exp).then_inc(S["dec"], 1)
                                act.wait_ge(S["ang"], 1)
                                a.activation(sc[:, :].rearrange("p c t h -> p (c t h)"),
                                             ang[:, :].rearrange("p c t h -> p (c t h)"), ACT.Sin).then_inc(S["sin"], 1)
                            if q == AT["bt"]:
                                act.wait_ge(S["bt_ps"], 1)
                                for k in range(2):
                                    ins = a.copy(bt[:, pp, 2 * k:2 * k + 2], ps[:, 3 + k, :].rearrange(
                                        "p (t c m) -> p t c m", t=2, c=2))
                                ins.then_inc(S["bt"], 1)
                            if q == AT["scores"]:
                                act.wait_ge(S["g_ps"], 1)
                                for r in range(R):
                                    a.copy(gt[:, pp, :, r, :], ps[:, 3 + r, :].rearrange(
                                        "p (a m) -> p a m", a=4)).then_inc(S["gt"], 1)

                @block.gpsimd
                def _(pool):
                    g, done = nc.gpsimd, [0]

                    def wait(ins):
                        done[0] += 1
                        ins.then_inc(S["pool"], 1)
                        pool.wait_ge(S["pool"], done[0])

                    def rsqrt(dst, src, n, ready):
                        g.tensor_tensor(dst, src, w["minus_half"][:, 0:n], ALU.pow).then_inc(ready, 1)

                    def deviations(k, var, lap, ready):
                        pool.wait_ge(var, lap)
                        wait(g.tensor_tensor(rstd[:, k, :], veps[:, k, :], w["minus_half"][:, 0:NT], ALU.pow))
                        g.tensor_tensor(shift[:, k, :], nmean[:, k, :], rstd[:, k, :], ALU.mult).then_inc(ready, 1)

                    half = N_STATE // 2
                    for q in range(SLOTS):
                        if tail:
                            if q == AT["stats_gate"]:
                                deviations(1, S["var2"], 1, S["rstd2"])
                        if scan:
                            if q in AT["variants_p"]:
                                t = AT["variants_p"].index(q)
                                if t >= 2:
                                    pool.wait_ge(S["ymm"], t - 1)
                                    pool.wait_ge(S["st_mm"], t - 1)
                                    pool.wait_ge(S["yz"], t - 1)
                                for c in (REF1 + 2, REF_END, 5):
                                    if c == REF_END and t == NT - 1:
                                        continue
                                    ins = g.tensor_tensor(
                                        xv[:, t % 2, c].rearrange("p h r q -> p h (r q)"),
                                        xr[:, par, t].rearrange("p h r q -> p h (r q)"),
                                        coef[:, par, c, t, :].rearrange("p (h o) -> p h o", o=1).to_broadcast(
                                            [P, M_HEADS, R * HP]), ALU.mult)
                                ins.then_inc(S["xv_p"], 1)
                            if q == AT["output_sums"][-1]:
                                pool.wait_ge(S["ms"], 1)
                                rsqrt(rms[:, par, :], ms[:, :], NT, S["rms"])
                                pool.wait_ge(S["rms"], 1)
                        if ffn:
                            if q == AT["stats"]:
                                deviations(0, S["var"], 1, S["rstd"])
                            if q in AT["experts"] and AT["experts"].index(q) % 4 == 3:
                                n = AT["experts"].index(q) // 2
                                pool.wait_ge(S["relu"], n + 1)
                                g.tensor_tensor(rl[:, n - 1, :], rl[:, n - 1, :], rl[:, n, :], ALU.add).then_inc(S["added"], 1)
                                if n == 3:
                                    pool.wait_ge(S["added"], 2)
                                    g.tensor_tensor(rl[:, 0, :], rl[:, 0, :], rl[:, 2, :], ALU.add).then_inc(S["added"], 1)
                            if q == AT["stats2"]:
                                deviations(0, S["var"], 2, S["rstd"])
                        if prep:
                            if q == AT["keep"]:
                                if tail:
                                    pool.wait_ge(S["y2"], NT)
                                g.tensor_copy(ykeep[:, pp], y[:, :, :]).then_inc(S["kept"], 1)
                            if q == AT["norm_bc"]:
                                pool.wait_ge(S["ms_bc"], 1)
                                wait(g.tensor_tensor(rbc[:, :], rbc[:, :], w["minus_half"][:, 0:NT * 3], ALU.pow))
                                wait(g.tensor_tensor(bcn[:, :, :, :],
                                                     bc, rbc4, ALU.mult))
                                g.tensor_tensor(bcn[:, :, :, :].rearrange("p t c n -> p t (c n)"),
                                                bcn[:, :, :, :].rearrange("p t c n -> p t (c n)"),
                                                w["bc_bias"][:, :, :].rearrange("p (o c) n -> p o (c n)", o=1).to_broadcast(
                                                    [P, NT, 3 * N_STATE]), ALU.mult).then_inc(S["bcn"], 1)
                            if q == AT["diagonal_p"]:
                                pool.wait_ge(S["br"], 1)
                                g.tensor_tensor(gdp[:, :, :, :], br[:, pp, :, 0:2, :], br[:, pp, :, 2:3, :].to_broadcast(
                                    [P, NT, 2, N_STATE]), ALU.mult).then_inc(S["gdp"], 1)
                            if q == AT["rotate_p"]:
                                pool.wait_ge(S["bcn"], 1)
                                pool.wait_ge(S["sin"], 1)
                                for c, (s0, k) in enumerate(((0, 0), (half, 1))):
                                    wait(g.tensor_tensor(rp[:, 2 + c], bcn[:, :, :, s0:s0 + half],
                                                         sc[:, k].rearrange("p t (o n) -> p t o n", o=1).to_broadcast(
                                                             [P, NT, 3, half]), ALU.mult))
                                g.tensor_tensor(br[:, pp, :, 0:3, half:], rp[:, 2], rp[:, 3], ALU.add).then_inc(S["rp_p"], 1)

                @block.tensor
                def _(pe):
                    mm = nc.tensor.matmul

                    def transposes(src, bank, ready):
                        for t in range(NT):
                            ins = nc.tensor.transpose(ps[:, bank, P * t:P * t + P], src[:, t, :], w["ident"][:, :])
                        ins.then_inc(ready, 1)

                    def project(t):
                        xs = xnT[:, 1, P * t:P * t + P]
                        if t:
                            pe.wait_ge(S["ev_x"], t)
                        mm(ps[:, 3, :], xs, w["w_in"][:, 0:512], start=True, stop=True).then_inc(S["pr_x"], 1)
                        if t:
                            pe.wait_ge(S["ev_z"], t)
                        mm(ps[:, 4, :], xs, w["w_in"][:, 512:1024], start=True, stop=True).then_inc(S["pr_z"], 1)

                    def rates():
                        if tail:
                            pe.wait_ge(S["gate_read"], 1)
                        for t in range(NT):
                            ins = mm(ps[:, 5, M_HEADS * t:M_HEADS * t + M_HEADS], xnT[:, 1, P * t:P * t + P],
                                     w["w_in"][:, 1024:1056], start=True, stop=True)
                        ins.then_inc(S["th_ps"], 1)

                    def sums():
                        pe.wait_ge(S["dtl"], 1)
                        pe.wait_ge(S["ev_z"], NT)
                        mm(ps[:, 5, 128:256], w["moves"][:, 0, :], th[:, :, :], start=True, stop=False, skip_group_check=True)
                        for s in range(1, NT):
                            mm(ps[:, 5, 128 + 32 * s:256], w["moves"][:, 1, :], th[:, 0:NT - s, :], start=False,
                               stop=s == NT - 1, skip_group_check=True)
                        for c in range(8):
                            mm(ps[:, 3 + c // 4, P * (c % 4):P * (c % 4) + P], w["sums"][:, c, :], lda[:, :, :],
                               start=True, stop=True)
                        pe.wait_ge(S["beta"], 1)
                        mm(ps[:, 5, 256:384], w["moves"][:, 2, :], bet[:, :, :], start=True, stop=False, skip_group_check=True)
                        mm(ps[:, 5, 256:352], w["moves"][:, 3, :], bet[:, 1:NT, :], start=False, stop=True,
                           skip_group_check=True).then_inc(S["prep_ps"], 1)

                    def turn_bc():
                        pe.wait_ge(S["br"], 1)
                        pe.wait_ge(S["dec"], 1)
                        for t in range(NT):
                            for c in range(2):
                                o = 256 * (t % 2) + P * c
                                ins = nc.tensor.transpose(ps[:, 3 + t // 2, o:o + P],
                                                          br[:, pp, t, 2 * c:2 * c + 2, :].rearrange("p c n -> p (c n)"),
                                                          w["ident"][:, :])
                        ins.then_inc(S["bt_ps"], 1)

                    def bc_scores():
                        pe.wait_ge(S["bt"], 1)
                        for t in range(NT):
                            for r in range(R):
                                n = slice(N_STATE * r, N_STATE * r + N_STATE)
                                ins = mm(ps[:, 3 + r, P * t:P * t + P], bt[n, pp, t, 0, :], bt[n, pp, t, 1, :],
                                         start=True, stop=True)
                        ins.then_inc(S["g_ps"], 1)

                    def chunk(t):
                        pe.wait_ge(S["xv_v"], t + 1)
                        if t:
                            pe.wait_ge(S["y_read"], t)
                            pe.wait_ge(S["state"], t)
                        for r in range(R):
                            mm(ps[:, 6, 0:256], gs[:, par, t, r, :], xv[:, t % 2, MID, :, r, :],
                               start=r == 0, stop=r == R - 1, skip_group_check=True)
                        pe.wait_ge(S["xv_p"], t + 1)
                        for r in range(R):
                            if r == 0:
                                ins = mm(ps[0:BLK, 6, 256:512], zero[:, :], xv[0:BLK, t % 2, 5, :, 0, :],
                                         start=True, stop=True, skip_group_check=True)
                            for blk in range(1, P // BLK):
                                rows, src = slice(BLK * blk, BLK * blk + BLK), slice(0, BLK * blk)
                                ins = mm(ps[rows, 6, 256:512], gt[src, par, t, r, rows], xv[src, t % 2, blk, :, r, :],
                                         start=r == 0, stop=r == R - 1, skip_group_check=True)
                        if t:
                            ins = mm(ps[:, 7, 0:256], bt[0:N_STATE, par, t, 1, :], state[:, :, :],
                                     start=True, stop=True, skip_group_check=True)
                        ins.then_inc(S["ymm"], 1)
                        if t < NT - 1:
                            for r in range(R):
                                ins = mm(ps[0:N_STATE, 7, 256:512], br[:, par, t, r, :], xv[:, t % 2, REF_END, :, r, :],
                                         start=r == 0, stop=r == R - 1, skip_group_check=True)
                            ins.then_inc(S["st_mm"], 1)

                    for q in range(SLOTS):
                        if tail:
                            if q in AT["turn_yz"]:
                                k = AT["turn_yz"].index(q)
                                if k:
                                    pe.wait_ge(S["yzT"], 1)
                                for t in range(2):
                                    for c in range(2):
                                        o = 256 * t + P * c
                                        ins = nc.tensor.transpose(ps[:, 5, o:o + P], yz[:, pp, 2 * k + t, P * c:P * c + P],
                                                                  w["ident"][:, :])
                                ins.then_inc(S["yzT_ps"], 1)
                            if q == AT["wo"]:
                                pe.wait_ge(S["yzT"], 2)
                                for t in range(NT):
                                    for c in range(2):
                                        ins = mm(ps[:, 5, P * t:P * t + P], yzT[:, t, c, :], w["w_out"][:, c, :],
                                                 start=c == 0, stop=c == 1)
                                ins.then_inc(S["wo"], 1)
                            if q == AT["turn_gate"]:
                                pe.wait_ge(S["xn2"], 1)
                                transposes(xn[:, 1], 5, S["xT2"])
                            if q == AT["gate"]:
                                pe.wait_ge(S["xnT2"], 1)
                                for t in range(NT):
                                    ins = mm(ps[:, 5, EXPERTS * t:EXPERTS * t + EXPERTS], xnT[:, 2, P * t:P * t + P],
                                             w["gwT"][:, :], start=True, stop=True)
                                ins.then_inc(S["gate"], 1)
                        if scan:
                            if q in AT["chunks"]:
                                chunk(AT["chunks"].index(q))
                        if ffn:
                            if q == AT["turn"]:
                                pe.wait_ge(S["xn"], 1)
                                transposes(xn[:, 0], 2, S["xT"])
                            if q in AT["experts"]:
                                e = AT["experts"].index(q)
                                if e == 0:
                                    pe.wait_ge(S["xnT"], 1)
                                if e >= 2:
                                    pe.wait_ge(S["relu" if e % 2 else "ex_v"], e // 2)
                                mm(ps[:, e % 2, :], ew["w"][:, e, :], xnT[:, 0, :], start=True, stop=True).then_inc(S["ex"], 1)
                            if q == AT["sum"]:
                                pe.wait_ge(S["ex_v"], EXPERTS // 2)
                                for t in range(NT):
                                    mm(ps[:, 2, P * t:P * t + P], acc[:, 1, P * t:P * t + P], w["ident"][:, :],
                                       start=t == 0, stop=False, skip_group_check=True)
                                pe.wait_ge(S["added"], 3)
                                for t in range(NT):
                                    ins = mm(ps[:, 2, P * t:P * t + P], rl[:, 0, P * t:P * t + P], w["ident"][:, :],
                                             start=False, stop=True, skip_group_check=True)
                                ins.then_inc(S["sum"], 1)
                            if q == AT["turn2"]:
                                pe.wait_ge(S["xn"], 2)
                                transposes(xn[:, 0], 2, S["xT"])
                        if prep:
                            if q in AT["project"]:
                                project(AT["project"].index(q))
                            if q == AT["rates"]:
                                rates()
                            if q == AT["sums"]:
                                sums()
                            if q == AT["bt"]:
                                turn_bc()
                            if q == AT["scores"]:
                                bc_scores()
            nc.gpsimd.sem_clear(range(nums[0], nums[-1] + 1))
            nc.all_engine_barrier(sem_only=True)

        with nc.Block(no_gpsimd_drain=True) as block:
            @block.vector
            def _(dve):
                nc.vector.memset(zero[:, :], 0.0)

            @block.sync
            def _(sp):
                sp.dma_start(x[:, :, :], x_in[0].rearrange("(t p) d -> p t d", p=P)).then_inc(S["x_in"], 16)
                sp.wait_ge(S["x_in"], 16)
        nc.gpsimd.sem_clear(range(nums[0], nums[-1] + 1))
        nc.all_engine_barrier(sem_only=True)

        def roles(i):
            return dict(ffn=i < BATCH, prep=1 <= i <= BATCH, scan=2 <= i <= BATCH + 1, tail=3 <= i, prefetch=i < BATCH - 1)

        for i in range(3):
            iteration(i, i % 2, **roles(i))
        with nc.Fori(0, (BATCH - 4) // 2, 1) as k:
            iteration(k * 2 + 3, 1, **roles(3))
            iteration(k * 2 + 4, 0, **roles(4))
        for i in range(BATCH - 1, BATCH + 3):
            iteration(i, i % 2, **roles(i))


def last_ffn_phase(nc, x_in, x_out, w, ew):
    GROUP = 4
    with ExitStack() as ctx:
        def sb(name, shape, dt=F32):
            return ctx.enter_context(nc.sbuf_tensor("f_" + name, shape, dt))

        x, y = sb("x", [P, GROUP, NT, D]), sb("y", [P, GROUP, NT, D])
        stats, mv = sb("stats", [P, 2, NT, 6]), sb("mv", [P, 2, NT, 2])
        veps, rstd = sb("veps", [P, 2, NT]), sb("rstd", [P, 2, NT])
        xn, xnT = sb("xn", [P, 2, NT, D]), sb("xnT", [P, 2, SEQ])
        acc = sb("acc", [P, 2, 2, SEQ])
        ps = ctx.enter_context(nc.psum_tensor("f_ps", [P, 8, 512], F32))
        names = ("x_first", "x_in", "x_out", "dve", "var", "rstd", "xn", "xT", "xnT", "ex", "ex_read", "sum", "y")
        S = {n: ctx.enter_context(nc.semaphore("f_" + n)) for n in names}
        nums = sorted(s.num for s in S.values())
        assert nums[-1] - nums[0] + 1 == len(nums)

        def group(i, first, prefetch):
            fronts = ([0] if first else []) + list(range(1, GROUP)) + ([GROUP] if prefetch else [])

            def nth(u):
                return fronts.index(u) + 1

            def before_last(u):
                return nth(u) - 2 if nth(u) > 2 else 0

            with nc.Block(no_gpsimd_drain=True) as block:
                @block.sync
                def _(sp):
                    for u in range(GROUP):
                        sp.wait_ge(S["y"], u + 1)
                        if prefetch:
                            sp.dma_start(x[:, u], x_in[bass.ds(i * GROUP + GROUP + u, 1)].rearrange(
                                "b (t p) d -> p (b t) d", p=P)).then_inc(S["x_in" if u else "x_first"], 16)
                        sp.dma_start(x_out[bass.ds(i * GROUP + u, 1)].rearrange("b (t p) d -> p (b t) d", p=P),
                                     y[:, u]).then_inc(S["x_out"], 16)
                    sp.wait_ge(S["x_out"], 16 * GROUP)
                    if prefetch:
                        sp.wait_ge(S["x_in"], 16 * (GROUP - 1))

                @block.vector
                def _(dve):
                    v, done = nc.vector, [0]

                    def mark(ins):
                        done[0] += 1
                        ins.then_inc(S["dve"], 1)
                        return done[0]

                    def statistics(u):
                        if before_last(u):
                            dve.wait_ge(S["xn"], before_last(u))
                        if u == GROUP:
                            dve.wait_ge(S["x_first"], 16)
                        for t in range(NT):
                            n = mark(v.bn_stats(stats[:, u % 2, t, :], x[:, u % GROUP, t, :]))
                        dve.wait_ge(S["dve"], n)
                        for t in range(NT):
                            n = mark(v.bn_aggr(mv[:, u % 2, t, :], stats[:, u % 2, t, :]))
                        dve.wait_ge(S["dve"], n)
                        v.tensor_scalar(veps[:, u % 2, :], mv[:, u % 2, :, 1], LN_EPS, None, ALU.add).then_inc(S["var"], 1)

                    def residual(u):
                        dve.wait_ge(S["sum"], u + 1)
                        v.tensor_tensor(y[:, u], x[:, u], ps[:, 6 + u % 2, :].rearrange("p (t d) -> p t d", t=NT),
                                        ALU.add).then_inc(S["y"], 1)

                    if 0 in fronts:
                        statistics(0)
                    statistics(1)
                    for u in range(GROUP):
                        for e in range(EXPERTS):
                            n = EXPERTS * u + e
                            dve.wait_ge(S["ex"], n + 1)
                            if n:
                                dve.wait_ge(S["ex_read"], n)
                            if e == 0:
                                ins = v.tensor_scalar(acc[:, u % 2, 0, :], ps[:, 0, :], ew["negb"][:, 0:1],
                                                      ew["sumb_all"][:, 0:1], ALU.max, ALU.add)
                            else:
                                ins = v.scalar_tensor_tensor(acc[:, u % 2, e % 2, :], ps[:, e % 4, :],
                                                             ew["negb"][:, e:e + 1], acc[:, u % 2, (e - 1) % 2, :],
                                                             ALU.max, ALU.add)
                            ins.then_inc(S["ex_read"], 1)
                            if e == 5 and u + 2 in fronts:
                                statistics(u + 2)
                            if e == 3 and u:
                                residual(u - 1)
                    residual(GROUP - 1)

                @block.gpsimd
                def _(pool):
                    g = nc.gpsimd
                    for u in fronts:
                        pool.wait_ge(S["var"], nth(u))
                        g.tensor_tensor(rstd[:, u % 2, :], veps[:, u % 2, :], w["minus_half"][:, 0:NT],
                                        ALU.pow).then_inc(S["rstd"], 1)
                        pool.wait_ge(S["rstd"], nth(u))
                        if before_last(u):
                            pool.wait_ge(S["xT"], before_last(u))
                        if u == GROUP:
                            pool.wait_ge(S["x_first"], 16)
                        for t in range(NT):
                            ins = g.tensor_scalar(xn[:, u % 2, t, :], x[:, u % GROUP, t, :], mv[:, u % 2, t, 0:1],
                                                  rstd[:, u % 2, t:t + 1], ALU.subtract, ALU.mult)
                        ins.then_inc(S["xn"], 1)

                @block.scalar
                def _(act):
                    for u in fronts:
                        act.wait_ge(S["xT"], nth(u))
                        if u >= 2:
                            act.wait_ge(S["ex"], EXPERTS * (u - 1))
                        nc.scalar.copy(xnT[:, u % 2, :], ps[:, 4 + u % 2, :]).then_inc(S["xnT"], 1)

                @block.tensor
                def _(pe):
                    def turn(u):
                        pe.wait_ge(S["xn"], nth(u))
                        if before_last(u):
                            pe.wait_ge(S["xnT"], before_last(u))
                        for t in range(NT):
                            ins = nc.tensor.transpose(ps[:, 4 + u % 2, P * t:P * t + P], xn[:, u % 2, t, :],
                                                      w["ident"][:, :])
                        ins.then_inc(S["xT"], 1)

                    def turn_sum(u):
                        pe.wait_ge(S["ex_read"], EXPERTS * (u + 1))
                        if u >= 2:
                            pe.wait_ge(S["y"], u - 1)
                        for t in range(NT):
                            ins = nc.tensor.transpose(ps[:, 6 + u % 2, P * t:P * t + P], acc[:, u % 2, 1, P * t:P * t + P],
                                                      w["ident"][:, :])
                        ins.then_inc(S["sum"], 1)

                    if 0 in fronts:
                        turn(0)
                    for u in range(GROUP):
                        if u in fronts:
                            pe.wait_ge(S["xnT"], nth(u))
                        for e in range(EXPERTS):
                            n = EXPERTS * u + e
                            if n >= 4:
                                pe.wait_ge(S["ex_read"], n - 3)
                            nc.tensor.matmul(ps[:, e % 4, :], ew["w"][:, e, :], xnT[:, u % 2, :],
                                             start=True, stop=True).then_inc(S["ex"], 1)
                            if e == 2 and u:
                                turn_sum(u - 1)
                            if e == 5 and u + 1 in fronts:
                                turn(u + 1)
                    turn_sum(GROUP - 1)
            nc.gpsimd.sem_clear(range(nums[0], nums[-1] + 1))
            nc.all_engine_barrier(sem_only=True)

        with nc.Block(no_gpsimd_drain=True) as block:
            @block.sync
            def _(sp):
                for u in range(GROUP):
                    sp.dma_start(x[:, u], x_in[u].rearrange("(t p) d -> p t d", p=P)).then_inc(S["x_in"], 16)
                sp.wait_ge(S["x_in"], 16 * GROUP)
        nc.gpsimd.sem_clear(range(nums[0], nums[-1] + 1))
        nc.all_engine_barrier(sem_only=True)
        group(0, True, True)
        with nc.Fori(1, BATCH // GROUP - 1, 1) as k:
            group(k, False, True)
        group(BATCH // GROUP - 1, False, False)


INS = ["q", "wq", "wk", "wv", "wo", "angles", "gwT", "gate_b", "rope", "ident", "iota",
       "w_in", "w_out", "a_log", "dt_bias", "bc_bias", "ew", "eb", "sums", "moves", "masks"]


def build(nc, ins, out):
    x3 = nc.dram_tensor("x3", (BATCH, SEQ, D), F32, kind="Internal").ap()
    x5 = nc.dram_tensor("x5", (BATCH, SEQ, D), F32, kind="Internal").ap()
    with ExitStack() as ctx:
        sb = lambda name, shape: ctx.enter_context(nc.sbuf_tensor(name, shape, F32))
        cnt_acc = sb("cnt_acc", [P, NT * TOPK * EXPERTS])
        with ExitStack() as layer0:
            w = load_layer0(nc, layer0, ins, cnt_acc)
            attention_phase(nc, ins["q"], ins["rope"], x3, w, cnt_acc)
        w = load_layer1(nc, ctx, ins)
        ew = {"w": sb("ew_s", [P, EXPERTS, D]), "posb": sb("posb", [P, EXPERTS]), "negb": sb("negb", [P, EXPERTS]),
              "sumb": sb("sumb", [P, 1]), "sumb_all": sb("sumb_all", [P, 1])}
        expert_weights(nc, "e1_", w, cnt_acc, ew)
        mixer_phase(nc, x3, x5, w, ew, cnt_acc)
        expert_weights(nc, "e2_", w, cnt_acc, ew)
        last_ffn_phase(nc, x5, out, w, ew)


def kernel(**inputs):
    import numpy as _np
    import concourse.bacc as _bacc
    from concourse import mybir as _mybir
    from concourse.bass_utils import run_bass_kernel_spmd as _run

    nc = _bacc.Bacc("TRN2", target_bir_lowering=False, num_devices=1)
    given = {**layout_p1(inputs), **layout_p2(inputs), **consts_p1(), **consts_p2()}
    arrays, aps = {}, {}
    for name in INS:
        a = _np.ascontiguousarray(given[name])
        arrays[f"in_{name}"] = a
        aps[name] = nc.dram_tensor(f"in_{name}", a.shape, _mybir.dt.from_np(a.dtype), kind="ExternalInput").ap()
    out = nc.dram_tensor("out_0", (BATCH, SEQ, D), F32, kind="ExternalOutput").ap()
    build(nc, aps, out)
    r = _run(nc, [arrays], core_ids=[0])
    return r.results[0]["out_0"]
```
